# Optimizing a Trainium2 kernel written in Bass

```python
import numpy as np
import jax
import jax.numpy as jnp

def _softmax(x, axis=-1):
    return jax.nn.softmax(x, axis=axis)

def _gelu(x):
    return jax.nn.gelu(x, approximate=True)

def _silu(x):
    return jax.nn.silu(x)

def _sigmoid(x):
    return jax.nn.sigmoid(x)

def _layernorm(x, axis=-1, eps=1e-05):
    m = jnp.mean(x, axis=axis, keepdims=True)
    v = jnp.var(x, axis=axis, keepdims=True)
    return (x - m) / jnp.sqrt(v + eps)

def _scatter_add(tgt, idx, src, axis=0):
    return tgt.at[idx].add(src)

def _segment_sum(src, seg, n):
    return jax.ops.segment_sum(src, seg, n)
kernel_name = 'mk_perceiver_d2_seqx_r4_574a49'

def setup_inputs(seed: int=0):
    np.random.seed(seed)
    _w = jnp.asarray

    def _rec_inputs():
        import jax
        import jax.numpy as jnp
        _rk = jax.random.key(seed)
        x = -0.0002928 + 1 * jax.random.normal(jax.random.fold_in(_rk, 1), (32, 64, 256), jnp.float32)
        _lenS = 64 - jax.random.randint(jax.random.fold_in(_rk, 7), (32,), 0, max(1, 64 // 4) + 1, jnp.int32)
        _lenS2 = 1601 - jax.random.randint(jax.random.fold_in(_rk, 8), (32,), 0, max(1, 1601 // 4) + 1, jnp.int32)
        _ctx_512P = jax.random.normal(jax.random.fold_in(_rk, 11), (32, 16, 128), jnp.float32)
        _ctx_512c = jax.random.dirichlet(jax.random.fold_in(_rk, 511), 0.3 * jnp.ones((16,), jnp.float32), (32, 1601))
        _ctx_512t = jnp.einsum('bsk,bkd->bsd', _ctx_512c, _ctx_512P)
        _ctx_512t = _ctx_512t * jax.lax.rsqrt(jnp.mean(jnp.square(_ctx_512t)) + 1e-12) * 0.953939
        ctx_512 = -0.000514642 + 1.00011 * (_ctx_512t + 0.3 * jax.random.normal(jax.random.fold_in(_rk, 611), (32, 1601, 128), jnp.float32))
        return (x, ctx_512)
    x, ctx_512 = _rec_inputs()

    def _L0_xattn_setup():
        import jax, jax.numpy as jnp
        import numpy as np
        DIM = 256
        LATENT_DIM = 128
        NUM_HEADS = 16
        HEAD_DIM = DIM // NUM_HEADS
        SCALE = HEAD_DIM ** (-0.5)
        key = jax.random.key(seed)
        k1, k2, k3, k4, k5 = jax.random.split(key, 5)
        B, xN, zN = (2, 512, 512)
        x = jax.random.normal(k1, (B, xN, DIM), dtype=jnp.float32)
        z = jax.random.normal(k2, (B, zN, LATENT_DIM), dtype=jnp.float32)
        Wq = jax.random.normal(k3, (DIM, DIM), dtype=jnp.float32) * DIM ** (-0.5)
        Wkv = jax.random.normal(k4, (2 * DIM, LATENT_DIM), dtype=jnp.float32) * LATENT_DIM ** (-0.5)
        Wo = jax.random.normal(k5, (DIM, DIM), dtype=jnp.float32) * DIM ** (-0.5)
        return {'x': x, 'z': z, 'Wq': Wq, 'Wkv': Wkv, 'Wo': Wo}
    _L0_xattn_all = _L0_xattn_setup()
    _L0_xattn_in = {k: v for k, v in _L0_xattn_all.items() if k in ('Wq', 'Wkv', 'Wo')}
    del _L0_xattn_all

    def _L0_attn_setup():
        import jax, jax.numpy as jnp
        import numpy as np
        import math
        B, S, D = (4, 2048, 256)
        CHUNK = 64

        def _forward(x, Wk, bk, Wv, bv, Wq, bq, Wkp, bkp, Wqp, bqp, phase_scale, ln_g, ln_b, Wo, bo):
            b, s, d = x.shape
            key = x @ Wk + bk
            value = x @ Wv + bv
            query = x @ Wq + bq
            key_phase = jnp.tanh(key @ Wkp + bkp) * phase_scale
            query_phase = jnp.tanh(query @ Wqp + bqp) * phase_scale
            bound_real = value * jnp.cos(key_phase)
            bound_imag = value * jnpp_sin((bound := None)) if False else value * jnp.sin(key_phase)
            pad = -s % CHUNK
            if pad:
                bound_real = jnp.pad(bound_real, ((0, 0), (0, pad), (0, 0)))
                bound_imag = jnp.pad(bound_imag, ((0, 0), (0, pad), (0, 0)))
                query_phase = jnp.pad(query_phase, ((0, 0), (0, pad), (0, 0)))
            nc = (s + pad) // CHUNK
            br = bound_real.reshape(b, nc, CHUNK, d)
            bi = bound_imag.reshape(b, nc, CHUNK, d)
            qp = query_phase.reshape(b, nc, CHUNK, d)
            mem_real = jnp.cumsum(br, axis=2)
            mem_imag = jnp.cumsum(bi, axis=2)
            retrieved = mem_real * jnp.cos(qp) + mem_imag * jnp.sin(qp)
            retrieved = retrieved.reshape(b, s + pad, d)[:, :s]
            retrieved = retrieved / math.sqrt(d)
            mu = jnp.mean(retrieved, axis=-1, keepdims=True)
            var = jnp.mean(jnp.square(retrieved - mu), axis=-1, keepdims=True)
            normed = (retrieved - mu) * jax.lax.rsqrt(var + 1e-05) * ln_g + ln_b
            out = normed @ Wo + bo
            return x + out
        key = jax.random.key(seed)
        ks = jax.random.split(key, 8)
        w = 0.02
        inp = {'x': jax.random.normal(ks[0], (B, S, D), jnp.float32), 'Wk': jax.random.normal(ks[1], (D, D), jnp.float32) * w, 'bk': jnp.zeros((D,), jnp.float32), 'Wv': jax.random.normal(ks[2], (D, D), jnp.float32) * w, 'bv': jnp.zeros((D,), jnp.float32), 'Wq': jax.random.normal(ks[3], (D, D), jnp.float32) * w, 'bq': jnp.zeros((D,), jnp.float32), 'Wkp': jax.random.normal(ks[4], (D, D), jnp.float32) * w, 'bkp': jnp.zeros((D,), jnp.float32), 'Wqp': jax.random.normal(ks[5], (D, D), jnp.float32) * w, 'bqp': jnp.zeros((D,), jnp.float32), 'phase_scale': jnp.ones((D,), jnp.float32) * math.pi, 'ln_g': jnp.ones((D,), jnp.float32), 'ln_b': jnp.zeros((D,), jnp.float32), 'Wo': jax.random.normal(ks[6], (D, D), jnp.float32) * w, 'bo': jnp.zeros((D,), jnp.float32)}
        return inp
    _L0_attn_all = _L0_attn_setup()
    _L0_attn_in = {k: v for k, v in _L0_attn_all.items() if k in ('Wk', 'bk', 'Wv', 'bv', 'Wq', 'bq', 'Wkp', 'bkp', 'Wqp', 'bqp', 'phase_scale', 'ln_g', 'ln_b', 'Wo', 'bo')}
    del _L0_attn_all

    def _L0_ffn_setup():
        import jax, jax.numpy as jnp
        import numpy as np
        B, S, H, E, K = (2, 256, 256, 8, 2)
        D = 2 * H
        key = jax.random.key(seed)
        ks = jax.random.split(key, 7)
        x = jax.random.normal(ks[0], (B, S, H), dtype=jnp.float32)
        Wr = jax.random.normal(ks[1], (H, E), dtype=jnp.float32) / np.sqrt(H)
        br = jnp.zeros((E,), dtype=jnp.float32)
        W1 = jax.random.normal(ks[2], (E, H, D), dtype=jnp.float32) / np.sqrt(H)
        b1 = jnp.zeros((E, D), dtype=jnp.float32)
        W2 = jax.random.normal(ks[3], (E, D, H), dtype=jnp.float32) / np.sqrt(D)
        b2 = jnp.zeros((E, H), dtype=jnp.float32)
        return {'x': x, 'Wr': Wr, 'br': br, 'W1': W1, 'b1': b1, 'W2': W2, 'b2': b2}
    _L0_ffn_all = _L0_ffn_setup()
    _L0_ffn_in = {k: v for k, v in _L0_ffn_all.items() if k in ('Wr', 'br', 'W1', 'b1', 'W2', 'b2')}
    del _L0_ffn_all

    def _L1_xattn_setup():
        import jax, jax.numpy as jnp
        import numpy as np
        B, LQ, LK = (8, 512, 512)
        QD, KD, VD = (256, 128, 128)
        key = jax.random.key(seed)
        ks = jax.random.split(key, 9)
        s = 0.02
        return {'query': jax.random.normal(ks[0], (B, LQ, QD), jnp.float32), 'key': jax.random.normal(ks[1], (B, LK, KD), jnp.float32), 'value': jax.random.normal(ks[2], (B, LK, VD), jnp.float32), 'Wq': jax.random.normal(ks[3], (QD, QD), jnp.float32) * s, 'bq': jnp.zeros((QD,), jnp.float32), 'Wk': jax.random.normal(ks[4], (KD, QD), jnp.float32) * s, 'bk': jnp.zeros((QD,), jnp.float32), 'Wv': jax.random.normal(ks[5], (VD, QD), jnp.float32) * s, 'bv': jnp.zeros((QD,), jnp.float32)}
    _L1_xattn_all = _L1_xattn_setup()
    _L1_xattn_in = {k: v for k, v in _L1_xattn_all.items() if k in ('Wq', 'bq', 'Wk', 'bk', 'Wv', 'bv')}
    del _L1_xattn_all

    def _L1_attn_setup():
        import jax, jax.numpy as jnp
        import numpy as np
        import math
        N_HEADS = 4
        N_KV_GROUPS = 1
        HEAD_DIM = 64
        SLIDING_WINDOW = 128
        ROPE_BASE = 1000000.0
        EPS = 1e-06

        def _rmsnorm(x, gamma):
            ms = jnp.mean(jnp.square(x), axis=-1, keepdims=True)
            return x * jax.lax.rsqrt(ms + EPS) * gamma

        def _rope_tables(T, head_dim, dtype):
            inv_freq = 1.0 / ROPE_BASE ** (jnp.arange(0, head_dim, 2, dtype=jnp.float32) / head_dim)
            t = jnp.arange(T, dtype=jnp.float32)
            freqs = jnp.outer(t, inv_freq)
            return (jnp.cos(freqs).astype(dtype), jnp.sin(freqs).astype(dtype))

        def _apply_rope(x, cos, sin):
            x0 = x[..., 0::2]
            x1 = x[..., 1::2]
            c = cos[None, :, None, :]
            s = sin[None, :, None, :]
            even = x0 * c - x1 * s
            odd = x0 * s + x1 * c
            return jnp.stack((even, odd), axis=-1).reshape(x.shape)
        key = jax.random.key(seed)
        ks = jax.random.split(key, 5)
        B, T, C = (2, 1024, 256)
        scale = 0.02
        return {'x': jax.random.normal(ks[0], (B, T, C), dtype=jnp.float32), 'Wq': jax.random.normal(ks[1], (C, C), dtype=jnp.float32) * scale, 'Wk': jax.random.normal(ks[2], (N_KV_GROUPS * HEAD_DIM, C), dtype=jnp.float32) * scale, 'Wv': jax.random.normal(ks[3], (N_KV_GROUPS * HEAD_DIM, C), dtype=jnp.float32) * scale, 'Wo': jax.random.normal(ks[4], (C, C), dtype=jnp.float32) * scale, 'q_gamma': jnp.ones((HEAD_DIM,), dtype=jnp.float32), 'k_gamma': jnp.ones((HEAD_DIM,), dtype=jnp.float32)}
    _L1_attn_all = _L1_attn_setup()
    _L1_attn_in = {k: v for k, v in _L1_attn_all.items() if k in ('Wq', 'Wk', 'Wv', 'Wo', 'q_gamma', 'k_gamma')}
    del _L1_attn_all

    def _L1_ffn_setup():
        import jax, jax.numpy as jnp
        import numpy as np
        QMAX = 127.0

        def _ste_round(v):
            return v + jax.lax.stop_gradient(jnp.round(v) - v)

        def _act_fake_quant(x, clip_factor):
            scale = jax.nn.sigmoid(clip_factor) * jnp.max(jnp.abs(x)) / QMAX
            return jnp.clip(_ste_round(x / scale), -QMAX - 1.0, QMAX) * scale

        def _weight_fake_quant(w):
            scale = jnp.max(jnp.abs(w), axis=1, keepdims=True) / QMAX
            return jnp.clip(_ste_round(w / scale), -QMAX - 1.0, QMAX) * scale
        key = jax.random.key(seed)
        k1, k2, k3, k4 = jax.random.split(key, 4)
        B, S, H, I = (8, 2048, 256, 704)
        return {'x': jax.random.normal(k1, (B, S, H), dtype=jnp.float32), 'clip_x': jnp.full((1,), 4.0, dtype=jnp.float32), 'clip_down': jnp.full((1,), 4.0, dtype=jnp.float32), 'w_gate': jax.random.normal(k2, (I, H), dtype=jnp.float32) * 0.02, 'w_up': jax.random.normal(k3, (I, H), dtype=jnp.float32) * 0.02, 'w_down': jax.random.normal(k4, (H, I), dtype=jnp.float32) * 0.02}
    _L1_ffn_all = _L1_ffn_setup()
    _L1_ffn_in = {k: v for k, v in _L1_ffn_all.items() if k in ('clip_x', 'clip_down', 'w_gate', 'w_up', 'w_down')}
    del _L1_ffn_all
    return {'x': x, 'ctx_512': ctx_512, 'L0_xattn_Wq': _L0_xattn_in['Wq'], 'L0_xattn_Wkv': _L0_xattn_in['Wkv'], 'L0_xattn_Wo': _L0_xattn_in['Wo'], 'L0_attn_Wk': _L0_attn_in['Wk'], 'L0_attn_bk': _L0_attn_in['bk'], 'L0_attn_Wv': _L0_attn_in['Wv'], 'L0_attn_bv': _L0_attn_in['bv'], 'L0_attn_Wq': _L0_attn_in['Wq'], 'L0_attn_bq': _L0_attn_in['bq'], 'L0_attn_Wkp': _L0_attn_in['Wkp'], 'L0_attn_bkp': _L0_attn_in['bkp'], 'L0_attn_Wqp': _L0_attn_in['Wqp'], 'L0_attn_bqp': _L0_attn_in['bqp'], 'L0_attn_phase_scale': _L0_attn_in['phase_scale'], 'L0_attn_ln_g': _L0_attn_in['ln_g'], 'L0_attn_ln_b': _L0_attn_in['ln_b'], 'L0_attn_Wo': _L0_attn_in['Wo'], 'L0_attn_bo': _L0_attn_in['bo'], 'L0_ffn_Wr': _L0_ffn_in['Wr'], 'L0_ffn_br': _L0_ffn_in['br'], 'L0_ffn_W1': _L0_ffn_in['W1'], 'L0_ffn_b1': _L0_ffn_in['b1'], 'L0_ffn_W2': _L0_ffn_in['W2'], 'L0_ffn_b2': _L0_ffn_in['b2'], 'L1_xattn_Wq': _L1_xattn_in['Wq'], 'L1_xattn_bq': _L1_xattn_in['bq'], 'L1_xattn_Wk': _L1_xattn_in['Wk'], 'L1_xattn_bk': _L1_xattn_in['bk'], 'L1_xattn_Wv': _L1_xattn_in['Wv'], 'L1_xattn_bv': _L1_xattn_in['bv'], 'L1_attn_Wq': _L1_attn_in['Wq'], 'L1_attn_Wk': _L1_attn_in['Wk'], 'L1_attn_Wv': _L1_attn_in['Wv'], 'L1_attn_Wo': _L1_attn_in['Wo'], 'L1_attn_q_gamma': _L1_attn_in['q_gamma'], 'L1_attn_k_gamma': _L1_attn_in['k_gamma'], 'L1_ffn_clip_x': _L1_ffn_in['clip_x'], 'L1_ffn_clip_down': _L1_ffn_in['clip_down'], 'L1_ffn_w_gate': _L1_ffn_in['w_gate'], 'L1_ffn_w_up': _L1_ffn_in['w_up'], 'L1_ffn_w_down': _L1_ffn_in['w_down']}

def reference(x, ctx_512, L0_xattn_Wq, L0_xattn_Wkv, L0_xattn_Wo, L0_attn_Wk, L0_attn_bk, L0_attn_Wv, L0_attn_bv, L0_attn_Wq, L0_attn_bq, L0_attn_Wkp, L0_attn_bkp, L0_attn_Wqp, L0_attn_bqp, L0_attn_phase_scale, L0_attn_ln_g, L0_attn_ln_b, L0_attn_Wo, L0_attn_bo, L0_ffn_Wr, L0_ffn_br, L0_ffn_W1, L0_ffn_b1, L0_ffn_W2, L0_ffn_b2, L1_xattn_Wq, L1_xattn_bq, L1_xattn_Wk, L1_xattn_bk, L1_xattn_Wv, L1_xattn_bv, L1_attn_Wq, L1_attn_Wk, L1_attn_Wv, L1_attn_Wo, L1_attn_q_gamma, L1_attn_k_gamma, L1_ffn_clip_x, L1_ffn_clip_down, L1_ffn_w_gate, L1_ffn_w_up, L1_ffn_w_down):
    import jax
    import jax.numpy as jnp

    def _L0_xattn_ref(x, z, Wq, Wkv, Wo):
        import jax, jax.numpy as jnp
        import numpy as np
        DIM = 256
        LATENT_DIM = 128
        NUM_HEADS = 16
        HEAD_DIM = DIM // NUM_HEADS
        SCALE = HEAD_DIM ** (-0.5)
        B, xN, _ = x.shape
        _, zN, _ = z.shape
        Q = (x @ Wq.T).reshape(B, xN, NUM_HEADS, HEAD_DIM)
        KV = (z @ Wkv.T).reshape(B, zN, 2, NUM_HEADS, HEAD_DIM)
        K = KV[:, :, 0]
        V = KV[:, :, 1]
        attn = jnp.einsum('bqhd,bkhd->bhqk', Q, K) * SCALE
        attn = jax.nn.softmax(attn, axis=-1)
        O = jnp.einsum('bhqk,bkhd->bqhd', attn, V).reshape(B, xN, DIM)
        return O @ Wo.T

    def _L0_attn_ref(x, Wk, bk, Wv, bv, Wq, bq, Wkp, bkp, Wqp, bqp, phase_scale, ln_g, ln_b, Wo, bo):
        import jax, jax.numpy as jnp
        import numpy as np
        import math
        B, S, D = (4, 2048, 256)
        CHUNK = 64

        def _forward(x, Wk, bk, Wv, bv, Wq, bq, Wkp, bkp, Wqp, bqp, phase_scale, ln_g, ln_b, Wo, bo):
            b, s, d = x.shape
            key = x @ Wk + bk
            value = x @ Wv + bv
            query = x @ Wq + bq
            key_phase = jnp.tanh(key @ Wkp + bkp) * phase_scale
            query_phase = jnp.tanh(query @ Wqp + bqp) * phase_scale
            bound_real = value * jnp.cos(key_phase)
            bound_imag = value * jnpp_sin((bound := None)) if False else value * jnp.sin(key_phase)
            pad = -s % CHUNK
            if pad:
                bound_real = jnp.pad(bound_real, ((0, 0), (0, pad), (0, 0)))
                bound_imag = jnp.pad(bound_imag, ((0, 0), (0, pad), (0, 0)))
                query_phase = jnp.pad(query_phase, ((0, 0), (0, pad), (0, 0)))
            nc = (s + pad) // CHUNK
            br = bound_real.reshape(b, nc, CHUNK, d)
            bi = bound_imag.reshape(b, nc, CHUNK, d)
            qp = query_phase.reshape(b, nc, CHUNK, d)
            mem_real = jnp.cumsum(br, axis=2)
            mem_imag = jnp.cumsum(bi, axis=2)
            retrieved = mem_real * jnp.cos(qp) + mem_imag * jnp.sin(qp)
            retrieved = retrieved.reshape(b, s + pad, d)[:, :s]
            retrieved = retrieved / math.sqrt(d)
            mu = jnp.mean(retrieved, axis=-1, keepdims=True)
            var = jnp.mean(jnp.square(retrieved - mu), axis=-1, keepdims=True)
            normed = (retrieved - mu) * jax.lax.rsqrt(var + 1e-05) * ln_g + ln_b
            out = normed @ Wo + bo
            return x + out
        return _forward(x, Wk, bk, Wv, bv, Wq, bq, Wkp, bkp, Wqp, bqp, phase_scale, ln_g, ln_b, Wo, bo)

    def _L0_ffn_ref(x, Wr, br, W1, b1, W2, b2):
        import jax, jax.numpy as jnp
        import numpy as np
        B, S, H, E, K = (2, 256, 256, 8, 2)
        D = 2 * H
        logits = jnp.einsum('bsh,he->bse', x, Wr) + br
        probs = jax.nn.softmax(logits, axis=-1)
        top_p, top_i = jax.lax.top_k(probs, K)
        cw = jnp.sum(jax.nn.one_hot(top_i, E, dtype=x.dtype) * top_p[..., None], axis=-2)
        h = jax.nn.relu(jnp.einsum('bsh,ehd->bsed', x, W1) + b1)
        y = jnp.einsum('bsed,edh->bseh', h, W2) + b2
        out = jnp.einsum('bseh,bse->bsh', y, cw)
        return out

    def _L1_xattn_ref(query, key, value, Wq, bq, Wk, bk, Wv, bv):
        import jax, jax.numpy as jnp
        import numpy as np
        B, LQ, LK = (8, 512, 512)
        QD, KD, VD = (256, 128, 128)
        q = jnp.einsum('bld,de->ble', query, Wq) + bq
        k = jnp.einsum('bld,de->ble', key, Wk) + bk
        v = jnp.einsum('bld,de->ble', value, Wv) + bv
        scores = jnp.einsum('bqe,bke->bqk', q, k)
        attn = jax.nn.softmax(scores, axis=-1)
        out = jnp.einsum('bqk,bke->bqe', attn, v)
        return out

    def _L1_attn_ref(x, Wq, Wk, Wv, Wo, q_gamma, k_gamma):
        import jax, jax.numpy as jnp
        import numpy as np
        import math
        N_HEADS = 4
        N_KV_GROUPS = 1
        HEAD_DIM = 64
        SLIDING_WINDOW = 128
        ROPE_BASE = 1000000.0
        EPS = 1e-06

        def _rmsnorm(x, gamma):
            ms = jnp.mean(jnp.square(x), axis=-1, keepdims=True)
            return x * jax.lax.rsqrt(ms + EPS) * gamma

        def _rope_tables(T, head_dim, dtype):
            inv_freq = 1.0 / ROPE_BASE ** (jnp.arange(0, head_dim, 2, dtype=jnp.float32) / head_dim)
            t = jnp.arange(T, dtype=jnp.float32)
            freqs = jnp.outer(t, inv_freq)
            return (jnp.cos(freqs).astype(dtype), jnp.sin(freqs).astype(dtype))

        def _apply_rope(x, cos, sin):
            x0 = x[..., 0::2]
            x1 = x[..., 1::2]
            c = cos[None, :, None, :]
            s = sin[None, :, None, :]
            even = x0 * c - x1 * s
            odd = x0 * s + x1 * c
            return jnp.stack((even, odd), axis=-1).reshape(x.shape)
        B, T, C = x.shape
        H, G, hd = (N_HEADS, N_KV_GROUPS, HEAD_DIM)
        rep = H // G
        q = (x @ Wq.T).reshape(B, T, H, hd)
        k = (x @ Wk.T).reshape(B, T, G, hd)
        v = (x @ Wv.T).reshape(B, T, G, hd)
        q = _rmsnorm(q, q_gamma)
        k = _rmsnorm(k, k_gamma)
        cos, sin = _rope_tables(T, hd, q.dtype)
        q = _apply_rope(q, cos, sin)
        k = _apply_rope(k, cos, sin)
        q = q.transpose(0, 2, 1, 3)
        k = k.transpose(0, 2, 1, 3)
        v = v.transpose(0, 2, 1, 3)
        k = jnp.repeat(k, rep, axis=1)
        v = jnp.repeat(v, rep, axis=1)
        scores = jnp.einsum('bhqd,bhkd->bhqk', q, k) / math.sqrt(hd)
        i = jnp.arange(T)[:, None]
        j = jnp.arange(T)[None, :]
        allowed = (j <= i) & (j >= i - SLIDING_WINDOW)
        scores = jnp.where(allowed, scores, -jnp.inf)
        attn = jax.nn.softmax(scores, axis=-1)
        out = jnp.einsum('bhqk,bhkd->bhqd', attn, v)
        out = out.transpose(0, 2, 1, 3).reshape(B, T, C)
        return out @ Wo.T

    def _L1_ffn_ref(x, clip_x, clip_down, w_gate, w_up, w_down):
        import jax, jax.numpy as jnp
        import numpy as np
        QMAX = 127.0

        def _ste_round(v):
            return v + jax.lax.stop_gradient(jnp.round(v) - v)

        def _act_fake_quant(x, clip_factor):
            scale = jax.nn.sigmoid(clip_factor) * jnp.max(jnp.abs(x)) / QMAX
            return jnp.clip(_ste_round(x / scale), -QMAX - 1.0, QMAX) * scale

        def _weight_fake_quant(w):
            scale = jnp.max(jnp.abs(w), axis=1, keepdims=True) / QMAX
            return jnp.clip(_ste_round(w / scale), -QMAX - 1.0, QMAX) * scale
        xq = _act_fake_quant(x, clip_x[0])
        gate = jnp.einsum('bsh,ih->bsi', xq, _weight_fake_quant(w_gate))
        up = jnp.einsum('bsh,ih->bsi', xq, _weight_fake_quant(w_up))
        h = _act_fake_quant(jax.nn.silu(gate) * up, clip_down[0])
        return jnp.einsum('bsi,hi->bsh', h, _weight_fake_quant(w_down))
    x = x + _L0_xattn_ref(_layernorm(x, axis=-1), ctx_512, L0_xattn_Wq, L0_xattn_Wkv, L0_xattn_Wo)
    x = x + _L0_attn_ref(_layernorm(x, axis=-1), L0_attn_Wk, L0_attn_bk, L0_attn_Wv, L0_attn_bv, L0_attn_Wq, L0_attn_bq, L0_attn_Wkp, L0_attn_bkp, L0_attn_Wqp, L0_attn_bqp, L0_attn_phase_scale, L0_attn_ln_g, L0_attn_ln_b, L0_attn_Wo, L0_attn_bo)
    x = x + _L0_ffn_ref(_layernorm(x, axis=-1), L0_ffn_Wr, L0_ffn_br, L0_ffn_W1, L0_ffn_b1, L0_ffn_W2, L0_ffn_b2)
    x = x + _L1_xattn_ref(_layernorm(x, axis=-1), ctx_512, ctx_512, L1_xattn_Wq, L1_xattn_bq, L1_xattn_Wk, L1_xattn_bk, L1_xattn_Wv, L1_xattn_bv)
    x = x + _L1_attn_ref(_layernorm(x, axis=-1), L1_attn_Wq, L1_attn_Wk, L1_attn_Wv, L1_attn_Wo, L1_attn_q_gamma, L1_attn_k_gamma)
    x = x + _L1_ffn_ref(_layernorm(x, axis=-1), L1_ffn_clip_x, L1_ffn_clip_down, L1_ffn_w_gate, L1_ffn_w_up, L1_ffn_w_down)
    return x

_drawn_inputs = setup_inputs


def setup_inputs(seed=0):
    import zlib

    import numpy as np

    out = dict(_drawn_inputs(seed))
    spreads = {'L0_attn_bk': (0.0, 0.644),
     'L0_attn_bv': (0.0, 0.1),
     'L0_attn_bq': (0.0, 0.654),
     'L0_attn_bkp': (0.0, 0.1),
     'L0_attn_bqp': (0.0, 0.1),
     'L0_attn_phase_scale': (3.1415927410125732, 0.6),
     'L0_attn_ln_g': (1.0, 0.2),
     'L0_attn_ln_b': (0.0, 0.466),
     'L0_attn_bo': (0.0, 0.1),
     'L0_ffn_br': (0.0, 0.1),
     'L0_ffn_b1': (0.0, 0.566),
     'L0_ffn_b2': (0.0, 0.399),
     'L1_xattn_bq': (0.0, 0.8),
     'L1_xattn_bk': (0.0, 0.8),
     'L1_xattn_bv': (0.0, 0.1),
     'L1_attn_q_gamma': (1.0, 0.6),
     'L1_attn_k_gamma': (1.0, 0.6)}
    factors = {'L0_attn_Wk': 2.716,
     'L1_attn_Wq': 6.141,
     'L1_attn_Wk': 6.219,
     'L1_ffn_w_gate': 4.145,
     'L1_ffn_w_up': 3.903,
     'L1_ffn_w_down': 3.844}
    for name, (base, spread) in spreads.items():
        noise = np.random.default_rng([zlib.crc32(name.encode()), seed]).standard_normal(out[name].shape)
        drawn = base * np.exp(spread * noise) if base else spread * noise
        out[name] = jnp.asarray(drawn.astype(out[name].dtype))
    for name, factor in factors.items():
        out[name] = (out[name] * factor).astype(out[name].dtype)
    return out
```

```python
from contextlib import ExitStack

import concourse.bass as bass
from concourse import mybir

ALU = mybir.AluOpType
ACT = mybir.ActivationFunctionType
F32 = mybir.dt.float32
BF16 = mybir.dt.bfloat16
AX_X = mybir.AxisListType.X

P = 128
B, T, D = 32, 64, 256
LK, C = 1601, 128
PAIRS = B // 2
DC = D // P
ROWS = B * T
KT = [(t * P, min(P, LK - t * P)) for t in range((LK + P - 1) // P)]
KFULL = LK // P
KREST = LK - KFULL * P
KGROUPS = [list(range(g, min(g + 4, len(KT)))) for g in range(0, len(KT), 4)]
SCORE_CHUNKS = [(c, min(512, LK - c)) for c in range(0, LK, 512)]
EPS = 1e-5


def at_least(eng, sem, value):
    if isinstance(value, int) and value <= 0:
        return
    eng.wait_ge(sem, value)


class Chain:

    def __init__(self, eng, sem, base=0):
        self.eng, self.sem, self.count = eng, sem, base

    def wait(self):
        at_least(self.eng, self.sem, self.count)

    def step(self, instruction):
        instruction.then_inc(self.sem, 1)
        self.count = self.count + 1
        self.wait()


class Memory:
    semaphores = []

    def __init__(self, nc, stack):
        self.nc, self.stack = nc, stack

    def sb(self, name, shape, dt=F32):
        return self.stack.enter_context(self.nc.sbuf_tensor(name, shape, dt))

    def psum(self, name, shape, dt=F32):
        return self.stack.enter_context(self.nc.psum_tensor(name, shape, dt))

    def sem(self, name):
        sem = self.nc.alloc_semaphore(name)
        Memory.semaphores.append(sem)
        return sem


def recycle(nc):
    nc.clear_and_free_semaphores(Memory.semaphores)
    nc.all_engine_barrier()
    Memory.semaphores.clear()


class Kept:

    def __init__(self, m):
        self.X = m.sb("X", [P, PAIRS, D])
        self.Y = m.sb("Y", [P, PAIRS, D])
        self.YT = m.sb("YT", [P, DC, ROWS])
        self.ident = m.sb("ident", [P, P])
        self.experts_loaded = m.sem("experts_loaded")


def setup(nc, g, x):
    with ExitStack() as stack:
        m = Memory(nc, stack)
        x_loaded, zeroed, built = m.sem("x_loaded"), m.sem("ident_zeroed"), m.sem("ident_built")
        with nc.Block() as block:

            @block.sync
            def _(sp):
                sp.dma_start(g.X[:], x.rearrange("(p b) q d -> (b q) p d", b=2)).then_inc(x_loaded, 16)
                sp.wait_ge(x_loaded, 16)

            @block.gpsimd
            def _(pool):
                nc.gpsimd.memset(g.ident[:], 0.0).then_inc(zeroed, 1)
                pool.wait_ge(zeroed, 1)
                nc.gpsimd.affine_select(out=g.ident[:], in_=g.ident[:], compare_op=ALU.not_equal, fill=1.0,
                                        base=0, pattern=[[-1, P]], channel_multiplier=1).then_inc(built, 1)
                pool.wait_ge(built, 1)


def normalise(nc, g, name, src=None, into_x=False, gain=None, shift=None):
    src = g.X if src is None else src
    with ExitStack() as stack:
        m = Memory(nc, stack)
        stats = m.sb(f"{name}_stats", [P, PAIRS, 6])
        total, dif, square, mean, inner, var, std, rstd = (m.sb(f"{name}_{n}", [P, PAIRS]) for n in
                                                   ("total", "dif", "square", "mean", "inner", "var", "std", "rstd"))
        turned = m.psum(f"{name}_turned", [P, 4, DC, 512])
        stats_done, sums_done, squares_done, var_done, std_done, rstd_done, y_done, x_added, turned_done, stored = (
            m.sem(f"{name}_{n}") for n in ("stats_done", "sums_done", "squares_done", "var_done", "std_done",
                                           "rstd_done", "y_done", "x_added", "turned_done", "stored"))
        with nc.Block() as block:

            @block.vector
            def _(dve):
                with dve.Fori(0, PAIRS) as t:
                    nc.vector.bn_stats(stats[:, t, :], src[:, t, :]).then_inc(stats_done, 1)
                dve.wait_ge(stats_done, PAIRS)
                mean_e, mean_o, var_e, var_o = stats[:, :, 1], stats[:, :, 4], stats[:, :, 2], stats[:, :, 5]
                nc.vector.tensor_tensor(total[:], mean_e, mean_o, ALU.add).then_inc(sums_done, 1)
                nc.vector.tensor_tensor(dif[:], mean_e, mean_o, ALU.subtract).then_inc(sums_done, 1)
                nc.vector.tensor_tensor(inner[:], var_e, var_o, ALU.add).then_inc(sums_done, 1)
                dve.wait_ge(sums_done, 3)
                nc.vector.tensor_scalar(mean[:], total[:], 0.5, None, ALU.mult).then_inc(squares_done, 1)
                nc.vector.tensor_tensor(square[:], dif[:], dif[:], ALU.mult).then_inc(squares_done, 1)
                nc.vector.tensor_scalar(inner[:], inner[:], 1.0 / D, EPS, ALU.mult, ALU.add).then_inc(squares_done, 1)
                dve.wait_ge(squares_done, 3)
                nc.vector.scalar_tensor_tensor(var[:], square[:], 0.25, inner[:], ALU.mult, ALU.add).then_inc(var_done, 1)
                dve.wait_ge(std_done, 1)
                nc.vector.reciprocal(rstd[:], std[:]).then_inc(rstd_done, 1)
                dve.wait_ge(rstd_done, 1)
                with dve.Fori(0, PAIRS) as t:
                    nc.vector.tensor_scalar(g.Y[:, t, :], src[:, t, :], mean[:, bass.ds(t, 1)], rstd[:, bass.ds(t, 1)],
                                            ALU.subtract, ALU.mult).then_inc(y_done, 1)
                if into_x:
                    dve.wait_ge(y_done, PAIRS)
                    nc.vector.tensor_tensor(g.X[:], g.X[:], g.Y[:], ALU.add).then_inc(x_added, 1)

            @block.scalar
            def _(act):
                act.wait_ge(var_done, 1)
                nc.scalar.activation(std[:], var[:], ACT.Sqrt).then_inc(std_done, 1)
                for n in range(4):
                    for c in range(DC):
                        act.wait_ge(turned_done, DC * n + c + 1)
                        out = g.YT[:, c, 512 * n:512 * n + 512]
                        if gain is None:
                            nc.scalar.copy(out, turned[:, n, c, :]).then_inc(stored, 1)
                        else:
                            nc.scalar.activation(out, turned[:, n, c, :], ACT.Identity, bias=shift[:, c:c + 1],
                                                 scale=gain[:, c:c + 1]).then_inc(stored, 1)

            @block.tensor
            def _(pe):
                for n in range(4):
                    pe.wait_ge(y_done, 4 * n + 4)
                    for c in range(DC):
                        for j in range(4):
                            mm = nc.tensor.transpose(turned[:, n, c, P * j:P * j + P],
                                                     g.Y[:, 4 * n + j, P * c:P * c + P], g.ident[:])
                        mm.then_inc(turned_done, 1)


HEADS, HD = 16, D // 16
HEAD_TILES = HEADS // 2
TILES = 2 * HEAD_TILES
SCALE0 = HD ** -0.5


def heads_cross_attention(nc, g, a):
    with ExitStack() as stack:
        m = Memory(nc, stack)
        wq_t = m.sb("wq_t", [P, DC, D])
        wk_by_head = m.sb("wk_by_head", [P, HEADS, C])
        wv_t = m.sb("wv_t", [C, D])
        wo_t = m.sb("wo_t", [P, DC, D])
        ctx = m.sb("ctx", [P, 2, len(KT), C])
        ctx_t = m.sb("ctx_t", [C, 2, LK])
        q_t = m.sb("q_t", [P, DC, P])
        qk_next = m.sb("qk_next", [C, 2, HEADS, T])
        qk = m.sb("qk", [C, 2, HEADS, T])
        neg_max = m.sb("neg_max", [P, 2])
        row_sum = m.sb("row_sum", [P, 2])
        inv_sum = m.sb("inv_sum", [P, 2])
        probs = m.sb("probs", [P, 2, LK])
        probs_t = m.sb("probs_t", [P, len(KT) * P])
        mixed = m.sb("mixed", [P, C])
        mixed_t = m.sb("mixed_t", [C, HEADS, 2, T])
        heads_out = m.sb("heads_out", [P, D])
        heads_out_t = m.sb("heads_out_t", [P, DC, P])

        scores = m.psum("scores", [P, 2048])
        turned = m.psum("turned", [P, 2, 512])
        mix = m.psum("mix", [P, 512])
        small = m.psum("small", [P, 512])

        sem = m.sem
        zeroed, weights_loaded, wk_loaded = sem("wk_zeroed"), sem("weights_loaded"), sem("wk_loaded")
        ctx_loaded = [sem("ctx_loaded_0"), sem("ctx_loaded_1")]
        scores_ready, max_ready, probs_ready = sem("scores_ready"), sem("max_ready"), sem("probs_ready")
        turned_ready, copied_act, copied_dve = sem("turned_ready"), sem("copied_act"), sem("copied_dve")
        mix_ready, inv_ready, mixed_ready = sem("mix_ready"), sem("inv_ready"), sem("mixed_ready")
        small_ready, small_taken = sem("small_ready"), sem("small_taken")
        qk_moved = sem("qk_moved")

        AFTER = {0: ["attn"], 1: ["attn_t"], 2: ["wo"]}
        PREPARE = {4: ["q"], 5: ["qk0"], 6: ["qk1"], 7: ["qk2"], 8: ["qk3"]}
        FIRST = ["q", "qk0", "qk1", "qk2", "qk3"]

        def jobs(before, after):
            out = []
            for r in range(TILES):
                if r > 0 or before:
                    out.append((r, "mixed_t"))
                out += [(r, n) for n in (AFTER.get(r, []) if before else [])]
                out += [(r, n) for n in (PREPARE.get(r, []) if after else [])]
            return out

        FULL = len(jobs(True, True))

        def job_base(p):
            first = len(FIRST) + len(jobs(False, True))
            return len(FIRST) if isinstance(p, int) and p == 0 else (p - 1) * FULL + first

        def job_no(p, before, after, r, name):
            return job_base(p) + jobs(before, after).index((r, name))

        def pairs(eng, body):
            body(0, False, True)
            with eng.Fori(1, PAIRS - 1) as p:
                body(p, True, True)
            body(PAIRS - 1, True, False)

        LAST_JOB = job_base(PAIRS - 1) + len(jobs(True, False))

        with nc.Block() as block:

            @block.sync
            def _(sp):
                sp.dma_start(wq_t[:], a["wq_t"].rearrange("(c p) n -> p c n", p=P)).then_inc(weights_loaded, 16)
                sp.dma_start(wv_t[:], a["wv_t"]).then_inc(weights_loaded, 16)
                sp.dma_start(wo_t[:], a["wo_t"].rearrange("(c p) n -> p c n", p=P)).then_inc(weights_loaded, 16)
                sp.wait_ge(zeroed, 1)
                for h in range(HEADS):
                    r = HD * (h % 8)
                    sp.dma_start(wk_by_head[r:r + HD, h, :], a["wkv"][HD * h:HD * h + HD, :]).then_inc(wk_loaded, 16)

                def load(p, before, after):
                    for b in range(2):
                        if before:
                            sp.wait_ge(mix_ready, TILES * (p - 1) + HEAD_TILES * (b + 1))
                        sp.dma_start(ctx_t[:, b, :], a["ctx_t"][2 * p + b]).then_inc(ctx_loaded[b], 16)
                        sp.dma_start(ctx[:, b, 0:KFULL, :], a["ctx_main"][2 * p + b]).then_inc(ctx_loaded[b], 16)
                        sp.dma_start(ctx[0:KREST, b, KFULL, :], a["ctx_rest"][2 * p + b]).then_inc(ctx_loaded[b], 16)

                load(0, False, True)
                with sp.Fori(1, PAIRS) as p:
                    load(p, True, True)

            @block.gpsimd
            def _(pool):
                nc.gpsimd.memset(wk_by_head[:], 0.0).then_inc(zeroed, 1)

            @block.tensor
            def _(pe):
                def small_job(job, name, p_rows, emit):
                    at_least(pe, small_taken, job)
                    emit().then_inc(small_ready, 1)

                def q_product(p):
                    for oc in range(DC):
                        for c in range(DC):
                            mm = nc.tensor.matmul(small[:, P * oc:P * oc + P], wq_t[:, c, P * oc:P * oc + P],
                                                  g.YT[:, c, bass.ds(P * p, P)], start=(c == 0), stop=(c == DC - 1))
                    return mm

                def qk_product(n):
                    for h in range(4 * n, 4 * n + 4):
                        mm = nc.tensor.matmul(small[:, P * (h % 4):P * (h % 4) + P], wk_by_head[:, h, :],
                                              q_t[:, h // 8, :], start=True, stop=True)
                    return mm

                def turn_mixed():
                    return nc.tensor.transpose(small[:, 0:P], mixed[:], g.ident[:])

                def attn_product():
                    for h in range(HEADS):
                        mm = nc.tensor.matmul(small[:, HD * h:HD * h + HD], mixed_t[:, h],
                                              wv_t[:, HD * h:HD * h + HD], start=True, stop=True)
                    return mm

                def turn_attn():
                    for c in range(DC):
                        mm = nc.tensor.transpose(small[:, P * c:P * c + P], heads_out[:, P * c:P * c + P], g.ident[:])
                    return mm

                def wo_product():
                    for c in range(DC):
                        mm = nc.tensor.matmul(small[:, 0:D], heads_out_t[:, c, :], wo_t[:, c, :],
                                              start=(c == 0), stop=(c == DC - 1))
                    return mm

                def score_tile(b, j):
                    for lo, n in SCORE_CHUNKS:
                        mm = nc.tensor.matmul(scores[:, lo:lo + n], qk[:, b, 2 * j:2 * j + 2, :],
                                              ctx_t[:, b, lo:lo + n], start=True, stop=True)
                    mm.then_inc(scores_ready, 1)

                def body(p, before, after):
                    def product(r, name):
                        job = job_no(p, before, after, r, name)
                        small_job(job, name, p, {
                            "mixed_t": turn_mixed, "attn": attn_product, "attn_t": turn_attn, "wo": wo_product,
                            "q": lambda: q_product(p + 1), "qk0": lambda: qk_product(0), "qk1": lambda: qk_product(1),
                            "qk2": lambda: qk_product(2), "qk3": lambda: qk_product(3)}[name])

                    for r in range(TILES):
                        row = TILES * p + r
                        if r + 1 < TILES or after:
                            pe.wait_ge(probs_ready, row + 1)
                            if r + 1 == HEAD_TILES:
                                pe.wait_ge(ctx_loaded[1], 48 * (p + 1))
                                pe.wait_ge(qk_moved, 2 * p + 2)
                            if r + 1 == TILES:
                                pe.wait_ge(ctx_loaded[0], 48 * (p + 2))
                                pe.wait_ge(qk_moved, 2 * p + 3)
                            nxt = (r + 1) % TILES
                            score_tile(nxt // HEAD_TILES, nxt % HEAD_TILES)
                        else:
                            pe.wait_ge(probs_ready, row + 1)
                        if r > 0 or before:
                            pe.wait_ge(mixed_ready, row)
                            product(r, "mixed_t")
                        b = r // HEAD_TILES

                        def turn(k):
                            if k == 2:
                                pe.wait_ge(copied_act, 2 * row + 1)
                            if k == 3:
                                pe.wait_ge(copied_act, 2 * row + 2)
                            for t in KGROUPS[k]:
                                lo, n = KT[t]
                                mm = nc.tensor.transpose(turned[0:n, k % 2, P * (t % 4):P * (t % 4) + P],
                                                         probs[:, r % 2, lo:lo + n], g.ident[:])
                            mm.then_inc(turned_ready, 1)

                        def weigh(k):
                            if k < 2:
                                pe.wait_ge(copied_act, 2 * row + k + 1)
                            else:
                                pe.wait_ge(copied_dve, 2 * row + k - 1)
                            for t in KGROUPS[k]:
                                n = KT[t][1]
                                mm = nc.tensor.matmul(mix[:, 0:C], probs_t[0:n, P * t:P * t + P], ctx[0:n, b, t, :],
                                                      start=(t == 0), stop=(t == len(KT) - 1))
                            if k == 3:
                                mm.then_inc(mix_ready, 1)

                        turn(0)
                        turn(1)
                        weigh(0)
                        turn(2)
                        weigh(1)
                        turn(3)
                        weigh(2)
                        weigh(3)
                        for n in (AFTER.get(r, []) if before else []) + (PREPARE.get(r, []) if after else []):
                            product(r, n)

                pe.wait_ge(weights_loaded, 48)
                pe.wait_ge(wk_loaded, 16 * HEADS)
                small_job(0, "q", 0, lambda: q_product(0))
                for n in range(4):
                    small_job(n + 1, "qk", 0, lambda: qk_product(n))
                pe.wait_ge(ctx_loaded[0], 48)
                pe.wait_ge(qk_moved, 1)
                score_tile(0, 0)
                pairs(pe, body)
                pe.wait_ge(mixed_ready, TILES * PAIRS)
                small_job(LAST_JOB, "mixed_t", 0, turn_mixed)
                small_job(LAST_JOB + 1, "attn", 0, attn_product)
                small_job(LAST_JOB + 2, "attn_t", 0, turn_attn)
                small_job(LAST_JOB + 3, "wo", 0, wo_product)

            @block.scalar
            def _(act):
                def take(job, name, r=0):
                    act.wait_ge(small_ready, job + 1)
                    if name == "q":
                        out, src, scale = q_t[:], small[:, 0:D].rearrange("p (c n) -> p c n", c=DC), SCALE0
                    elif name.startswith("qk"):
                        h = 4 * int(name[2])
                        out = qk_next[:, :, h:h + 4, :]
                        src, scale = small[:, 0:512].rearrange("p (h b q) -> p b h q", h=4, b=2), 1.0
                    elif name == "mixed_t":
                        tile = (r - 1) % TILES
                        j = tile % HEAD_TILES
                        out = mixed_t[:, 2 * j:2 * j + 2, tile // HEAD_TILES, :]
                        src, scale = small[:, 0:P].rearrange("p (h q) -> p h q", h=2), 1.0
                    elif name == "attn":
                        out, src, scale = heads_out[:], small[:, 0:D], 1.0
                    elif name == "attn_t":
                        out, src, scale = heads_out_t[:], small[:, 0:D].rearrange("p (c n) -> p c n", c=DC), 1.0
                    nc.scalar.activation(out, src, ACT.Copy, scale=scale).then_inc(small_taken, 1)

                def exp(tile, row):
                    act.wait_ge(max_ready, row + 1)
                    nc.scalar.activation(probs[:, tile % 2, :], scores[:, 0:LK], ACT.Exp, bias=neg_max[:, tile % 2:tile % 2 + 1],
                                         scale=1.0, accum_out=row_sum[:, tile % 2:tile % 2 + 1]).then_inc(probs_ready, 1)

                def body(p, before, after):
                    for r in range(TILES):
                        row = TILES * p + r
                        if r > 0 or before:
                            take(job_no(p, before, after, r, "mixed_t"), "mixed_t", r)
                        for k in range(2):
                            act.wait_ge(turned_ready, 4 * row + k + 1)
                            nc.scalar.copy(probs_t[:, 512 * k:512 * k + 512], turned[:, k, :]).then_inc(copied_act, 1)
                        if r + 1 < TILES or after:
                            exp((r + 1) % TILES, row + 1)
                        for n in (AFTER.get(r, []) if before else []) + (PREPARE.get(r, []) if after else []):
                            if n == "wo":
                                continue
                            if n == "qk0":
                                act.wait_ge(qk_moved, 2 * p + 2)
                            take(job_no(p, before, after, r, n), n)

                act.preload_act_table(ACT.Exp)
                for k, n in enumerate(FIRST):
                    take(k, n)
                exp(0, 0)
                pairs(act, body)
                take(LAST_JOB, "mixed_t", 0)
                take(LAST_JOB + 1, "attn")
                take(LAST_JOB + 2, "attn_t")

            @block.vector
            def _(dve):
                def row_max(tile, row):
                    dve.wait_ge(scores_ready, row + 1)
                    nc.vector.tensor_reduce(neg_max[:, tile % 2:tile % 2 + 1], scores[:, 0:LK], AX_X, ALU.max,
                                            negate=True).then_inc(max_ready, 1)

                def add_to_x(job, p):
                    dve.wait_ge(small_ready, job + 1)
                    nc.vector.tensor_tensor(g.X[:, p, :], g.X[:, p, :], small[:, 0:D], ALU.add).then_inc(small_taken, 1)

                def body(p, before, after):
                    for r in range(TILES):
                        row = TILES * p + r
                        if r + 1 < TILES or after:
                            row_max((r + 1) % TILES, row + 1)
                        dve.wait_ge(probs_ready, row + 1)
                        nc.vector.reciprocal(inv_sum[:, r % 2:r % 2 + 1], row_sum[:, r % 2:r % 2 + 1]).then_inc(inv_ready, 1)
                        for k in (2, 3):
                            dve.wait_ge(turned_ready, 4 * row + k + 1)
                            n, w = KT[KGROUPS[k][-1]][1], P * len(KGROUPS[k])
                            nc.vector.tensor_copy(probs_t[0:n, 512 * k:512 * k + w], turned[0:n, k % 2, 0:w])\
                                .then_inc(copied_dve, 1)
                        dve.wait_ge(mix_ready, row + 1)
                        dve.wait_ge(inv_ready, row + 1)
                        nc.vector.tensor_scalar(mixed[:], mix[:, 0:C], inv_sum[:, r % 2:r % 2 + 1], None, ALU.mult)\
                            .then_inc(mixed_ready, 1)
                        if after and r == 9:
                            dve.wait_ge(small_taken, job_no(p, before, after, 8, "qk3") + 1)
                            move(0)
                        if after and r == TILES - 2:
                            move(1)
                        if before and r == 2:
                            add_to_x(job_no(p, before, after, r, "wo"), p - 1)

                def move(b):
                    nc.vector.tensor_copy(qk[:, b], qk_next[:, b]).then_inc(qk_moved, 1)

                dve.wait_ge(small_taken, len(FIRST))
                move(0)
                move(1)
                row_max(0, 0)
                pairs(dve, body)
                add_to_x(LAST_JOB + 3, PAIRS - 1)


GROUP = 512
GROUPS = ROWS // GROUP
ROUND = 12582912.0
TWO_PI = 6.2831845
TURN = 0.15915494309189535
BK, BV, BQ, BKP, BQP, PHASE, GAIN, SHIFT = range(8)


def token_mixer(nc, g, a):
    with ExitStack() as stack:
        m = Memory(nc, stack)
        columns = m.sb("mix_columns", [P, 8, DC])
        wo = m.sb("mix_wo", [P, DC, D])
        bo = m.sb("mix_bo", [P, D])
        retrieve(nc, g, a, columns, wo, bo)
        normalise(nc, g, "ln_r", src=g.Y, gain=columns[:, GAIN], shift=columns[:, SHIFT])
        with ExitStack() as inner:
            n = Memory(nc, inner)
            product = n.psum("mix_product", [P, 2, 512])
            product_done, product_added = n.sem("mix_product_done"), n.sem("mix_product_added")
            with nc.Block() as block:

                @block.tensor
                def _(pe):
                    for t in range(PAIRS):
                        at_least(pe, product_added, t - 1)
                        for c in range(DC):
                            mm = nc.tensor.matmul(product[:, t % 2, 0:D], g.YT[:, c, P * t:P * t + P], wo[:, c, :],
                                                  start=(c == 0), stop=(c == DC - 1))
                        mm.then_inc(product_done, 1)

                @block.vector
                def _(dve):
                    for t in range(PAIRS):
                        dve.wait_ge(product_done, t + 1)
                        nc.vector.tensor_tensor(g.X[:, t, :], g.X[:, t, :], product[:, t % 2, 0:D],
                                                ALU.add).then_inc(product_added, 1)


def retrieve(nc, g, a, columns, wo, bo):
    with ExitStack() as stack:
        m = Memory(nc, stack)
        w = {n: m.sb(f"mix_{n}", [P, DC, D]) for n in ("wk", "wv", "wq", "wkp", "wqp")}
        key, value, query, turn_k, turn_q = (m.sb(f"mix_{n}", [P, DC, GROUP]) for n in
                                             ("key", "value", "query", "turn_k", "turn_q"))
        wave = {n: m.sb(f"mix_{n}", [P, DC, GROUP]) for n in ("cos_k", "sin_k", "cos_q", "sin_q")}
        whole = m.sb("mix_whole", [P, DC, GROUP])
        bound = m.sb("mix_bound", [P, DC, GROUP])
        memory = [m.sb("mix_memory_re", [P, DC, GROUP]), m.sb("mix_memory_im", [P, DC, GROUP])]
        retrieved = m.sb("mix_retrieved", [P, DC, GROUP])
        keep = m.sb("mix_keep", [P, GROUP])
        per_turn = m.sb("mix_per_turn", [P, DC])
        ps_k, ps_v, ps_q = (m.psum(f"mix_ps_{n}", [P, DC, 512]) for n in "kvq")
        ps_r = m.psum("mix_ps_r", [P, 2, 512])
        sem = m.sem
        weights, bo_loaded, bo_added = sem("mix_weights"), sem("mix_bo_loaded"), sem("mix_bo_added")
        made_k, made_q, made_v = sem("mix_made_k"), sem("mix_made_q"), sem("mix_made_v")
        made_kp, made_qp = sem("mix_made_kp"), sem("mix_made_qp")
        took_k, took_q, took_v, tanh_done = sem("mix_took_k"), sem("mix_took_q"), sem("mix_took_v"), sem("mix_tanh_done")
        angle_done, wave_done, step, retrieved_done = sem("mix_angle_done"), sem("mix_wave_done"), sem("mix_step"), sem("mix_retrieved_done")
        rows_turned, rows_stored = sem("mix_rows_turned"), sem("mix_rows_stored")
        SETUP, STEPS = 3, 4 * (DC + 1) + 2 * (1 + DC) + 2

        def groups(eng, body):
            body(0, True)
            with eng.Fori(1, GROUPS) as n:
                body(n, False)

        with nc.Block() as block:

            @block.sync
            def _(sp):
                sp.dma_start(columns[:], a["mix_columns"]).then_inc(weights, 16)
                for n, src in (("wk", a["mix_wk"]), ("wv", a["mix_wv"]), ("wq", a["mix_wq"]), ("wkp", a["mix_wkp"]), ("wqp", a["mix_wqp"])):
                    sp.dma_start(w[n][:], src.rearrange("(c p) n -> p c n", p=P)).then_inc(weights, 16)
                sp.dma_start(wo[:], a["mix_wo"].rearrange("(c p) n -> p c n", p=P)).then_inc(weights, 16)
                sp.dma_start(bo[:], a["mix_bo"].partition_broadcast(P)).then_inc(bo_loaded, 16)
                load_experts(sp, g, a)

            @block.gpsimd
            def _(pool):
                pool.wait_ge(bo_loaded, 16)
                nc.gpsimd.tensor_tensor(g.X[:], g.X[:], bo[:].unsqueeze(1).to_broadcast([P, PAIRS, D]),
                                        ALU.add).then_inc(bo_added, 1)

            @block.tensor
            def _(pe):
                def project(out, weight, moving, done):
                    for oc in range(DC):
                        for c in range(DC):
                            mm = nc.tensor.matmul(out[:, oc, :], weight[:, c, P * oc:P * oc + P], moving(c),
                                                  start=(c == 0), stop=(c == DC - 1))
                    mm.then_inc(done, 1)

                def turn_rows(n):
                    pe.wait_ge(retrieved_done, n + 1)
                    for j in range(4):
                        for c in range(DC):
                            mm = nc.tensor.transpose(ps_r[:, j // 2, D * (j % 2) + P * c:D * (j % 2) + P * c + P],
                                                     retrieved[:, c, P * j:P * j + P], g.ident[:])
                        if j % 2:
                            mm.then_inc(rows_turned, 1)

                def body(n, first):
                    y = lambda c: g.YT[:, c, bass.ds(GROUP * n, GROUP)]
                    if not first:
                        pe.wait_ge(tanh_done, 2 * n)
                        pe.wait_ge(took_v, n)
                    project(ps_k, w["wk"], y, made_k)
                    project(ps_q, w["wq"], y, made_q)
                    project(ps_v, w["wv"], y, made_v)
                    pe.wait_ge(took_k, n + 1)
                    project(ps_k, w["wkp"], lambda c: key[:, c, :], made_kp)
                    pe.wait_ge(took_q, n + 1)
                    project(ps_q, w["wqp"], lambda c: query[:, c, :], made_qp)
                    if not first:
                        turn_rows(n - 1)

                pe.wait_ge(weights, 16 * 7)
                groups(pe, body)
                turn_rows(GROUPS - 1)

            @block.scalar
            def _(act):
                def take(made, n, src, dst, row, func, done):
                    act.wait_ge(made, n + 1)
                    for c in range(DC):
                        ins = nc.scalar.activation(dst[:, c, :], src[:, c, :], func, bias=columns[:, row, c:c + 1], scale=1.0)
                    ins.then_inc(done, 1)

                def body(n, first):
                    take(made_k, n, ps_k, key, BK, ACT.Identity, took_k)
                    take(made_q, n, ps_q, query, BQ, ACT.Identity, took_q)
                    if not first:
                        act.wait_ge(retrieved_done, n)
                    take(made_v, n, ps_v, value, BV, ACT.Identity, took_v)
                    take(made_kp, n, ps_k, turn_k, BKP, ACT.Tanh, tanh_done)
                    take(made_qp, n, ps_q, turn_q, BQP, ACT.Tanh, tanh_done)
                    for k, name in enumerate(wave):
                        act.wait_ge(angle_done, 4 * n + k + 1)
                        nc.scalar.activation(wave[name][:], wave[name][:], ACT.Sin, scale=TWO_PI).then_inc(wave_done, 1)

                act.preload_act_table(ACT.Silu)
                act.wait_ge(weights, 16 * 7)
                groups(act, body)

            @block.vector
            def _(dve):
                chain = Chain(dve, step)
                chain.step(nc.vector.memset(keep[:], 1.0))
                chain.step(nc.vector.memset(keep[:].rearrange("p (b q) -> p b q", q=T)[:, :, 0:1], 0.0))
                dve.wait_ge(weights, 16 * 7)
                chain.step(nc.vector.tensor_scalar(per_turn[:], columns[:, PHASE, :], TURN, None, ALU.mult))

                def store_rows(n):
                    for j in range(2):
                        dve.wait_ge(rows_turned, 2 * n + j + 1)
                        nc.vector.tensor_scalar(g.Y[:, bass.ds(4 * n + 2 * j, 2), :],
                                                ps_r[:, j, :].rearrange("p (t d) -> p t d", t=2), D ** -0.5, None,
                                                ALU.mult).then_inc(rows_stored, 1)

                def body(n, first):
                    chain = Chain(dve, step, SETUP + STEPS * n)
                    for k, (name, turn) in enumerate(zip(wave, (turn_k, turn_k, turn_q, turn_q))):
                        if k % 2 == 0:
                            dve.wait_ge(tanh_done, 2 * n + k // 2 + 1)
                        for c in range(DC):
                            chain.step(nc.vector.tensor_scalar(wave[name][:, c, :], turn[:, c, :], per_turn[:, c:c + 1],
                                                               0.25 if name.startswith("cos") else 0.0, ALU.mult, ALU.add))
                        chain.step(nc.vector.tensor_scalar(whole[:], wave[name][:], ROUND, ROUND, ALU.add, ALU.subtract))
                        nc.vector.tensor_tensor(wave[name][:], wave[name][:], whole[:], ALU.subtract).then_inc(angle_done, 1)
                        dve.wait_ge(angle_done, 4 * n + k + 1)
                    if not first:
                        store_rows(n - 1)
                    dve.wait_ge(took_v, n + 1)
                    for k, name in enumerate(("cos_k", "sin_k")):
                        dve.wait_ge(wave_done, 4 * n + k + 1)
                        chain.step(nc.vector.tensor_tensor(bound[:], value[:], wave[name][:], ALU.mult))
                        for c in range(DC):
                            chain.step(nc.vector.tensor_tensor_scan(memory[k][:, c, :], keep[:], bound[:, c, :], 0.0,
                                                                    ALU.mult, ALU.add))
                    for k, name in enumerate(("cos_q", "sin_q")):
                        dve.wait_ge(wave_done, 4 * n + k + 3)
                        chain.step(nc.vector.tensor_tensor(memory[k][:], memory[k][:], wave[name][:], ALU.mult))
                    nc.vector.tensor_tensor(retrieved[:], memory[0][:], memory[1][:], ALU.add).then_inc(retrieved_done, 1)
                    dve.wait_ge(retrieved_done, n + 1)

                groups(dve, body)
                store_rows(GROUPS - 1)


E, H = 8, 2 * D
HC = H // P


def reserve_experts(g, m):
    g.w1, g.w2 = m.sb("expert_w1", [P, E, DC, H]), m.sb("expert_w2", [P, E, HC, D])
    g.b1, g.b2 = m.sb("expert_b1", [P, E, HC]), m.sb("expert_b2", [E, D])
    g.wr, g.br = m.sb("router_w", [P, DC, E]), m.sb("router_b", [P, E])
    g.share, g.share_t = m.sb("share", [P, PAIRS, E]), m.sb("share_t", [E, ROWS])


def load_experts(sp, g, a):
    sp.dma_start(g.w1[:], a["expert_w1"].rearrange("e (c p) d -> p e c d", p=P)).then_inc(g.experts_loaded, 16)
    sp.dma_start(g.w2[:], a["expert_w2"].rearrange("e (c p) d -> p e c d", p=P)).then_inc(g.experts_loaded, 16)
    sp.dma_start(g.b1[:], a["expert_b1"]).then_inc(g.experts_loaded, 16)
    sp.dma_start(g.b2[:], a["expert_b2"]).then_inc(g.experts_loaded, 16)
    sp.dma_start(g.wr[:], a["router_w"].rearrange("(c p) e -> p c e", p=P)).then_inc(g.experts_loaded, 16)
    sp.dma_start(g.br[:], a["router_b"].partition_broadcast(P)).then_inc(g.experts_loaded, 16)


def route(nc, g):
    with ExitStack() as stack:
        m = Memory(nc, stack)
        logits, probs, top, order, rank, chosen, rest = (m.sb(f"route_{n}", [P, PAIRS, E]) for n in
                                                         ("logits", "probs", "top", "order", "rank", "chosen", "rest"))
        best, total = m.sb("route_best", [P, PAIRS]), m.sb("route_total", [P, PAIRS])
        ps = m.psum("route_ps", [P, PAIRS, E])
        ps_t = m.psum("route_ps_t", [P, 4, 512])
        made, step, shifted, exp_done, share_done, turned, stored, order_done = (
            m.sem(f"route_{n}") for n in ("made", "step", "shifted", "exp_done", "share_done", "turned", "stored", "order_done"))

        def by_row(column):
            return column[:].unsqueeze(2).to_broadcast([P, PAIRS, E])

        with nc.Block() as block:

            @block.gpsimd
            def _(pool):
                nc.gpsimd.iota(order[:], pattern=[[0, PAIRS], [-1, E]], base=E, channel_multiplier=0,
                               allow_small_or_imprecise_dtypes=True).then_inc(order_done, 1)

            @block.tensor
            def _(pe):
                pe.wait_ge(g.experts_loaded, 96)
                for t in range(PAIRS):
                    for c in range(DC):
                        mm = nc.tensor.matmul(ps[:, t, :], g.YT[:, c, P * t:P * t + P], g.wr[:, c, :],
                                              start=(c == 0), stop=(c == DC - 1))
                mm.then_inc(made, 1)
                pe.wait_ge(share_done, 1)
                for t in range(PAIRS):
                    mm = nc.tensor.transpose(ps_t[0:E, t // 4, P * (t % 4):P * (t % 4) + P], g.share[:, t, :], g.ident[:])
                mm.then_inc(turned, 1)

            @block.scalar
            def _(act):
                act.wait_ge(shifted, 1)
                nc.scalar.activation(probs[:], logits[:], ACT.Exp).then_inc(exp_done, 1)
                act.wait_ge(turned, 1)
                nc.scalar.copy(g.share_t[:].rearrange("p (n r) -> p n r", n=4), ps_t[0:E, :, :]).then_inc(stored, 1)

            @block.vector
            def _(dve):
                chain = Chain(dve, step)
                tt, link = nc.vector.tensor_tensor, chain.step
                dve.wait_ge(made, 1)
                link(tt(logits[:], ps[:], g.br[:].unsqueeze(1).to_broadcast([P, PAIRS, E]), ALU.add))
                link(nc.vector.tensor_reduce(best[:], logits[:], AX_X, ALU.max))
                tt(logits[:], logits[:], by_row(best), ALU.subtract).then_inc(shifted, 1)
                dve.wait_ge(exp_done, 1)
                link(nc.vector.tensor_reduce(total[:], probs[:], AX_X, ALU.add))
                link(nc.vector.reciprocal(total[:], total[:]))
                link(tt(probs[:], probs[:], by_row(total), ALU.mult))
                dve.wait_ge(order_done, 1)
                for n, left in enumerate((probs, rest)):
                    pick = chosen if n == 0 else top
                    link(nc.vector.tensor_reduce(best[:], left[:], AX_X, ALU.max))
                    link(tt(rank[:], left[:], by_row(best), ALU.is_equal))
                    link(tt(rank[:], rank[:], order[:], ALU.mult))
                    link(nc.vector.tensor_reduce(best[:], rank[:], AX_X, ALU.max))
                    link(tt(pick[:], rank[:], by_row(best), ALU.is_equal))
                    if n == 0:
                        link(nc.vector.scalar_tensor_tensor(rest[:], pick[:], -2.0, probs[:], ALU.mult, ALU.add))
                link(tt(chosen[:], chosen[:], top[:], ALU.add))
                tt(g.share[:], probs[:], chosen[:], ALU.mult).then_inc(share_done, 1)


def experts(nc, g, a):
    route(nc, g)
    with ExitStack() as stack:
        m = Memory(nc, stack)
        hidden = m.sb("hidden", [P, 2, HC, GROUP])
        ps_h = m.psum("expert_ps_h", [P, HC, 512])
        ps_y = m.psum("expert_ps_y", [P, 4, 512])
        made_h, took_h, made_y, added_y, biased = (m.sem(f"expert_{n}") for n in
                                                   ("made_h", "took_h", "made_y", "added_y", "biased"))

        def steps(eng, body):
            body(0, True)
            with eng.Fori(1, GROUPS) as n:
                body(n, False)

        with nc.Block() as block:

            @block.tensor
            def _(pe):
                def first_product(n, e):
                    s = E * n + e
                    for h in range(HC):
                        at_least(pe, took_h, HC * (s - 1) + h + 1)
                        for c in range(DC):
                            mm = nc.tensor.matmul(ps_h[:, h, :], g.w1[:, e, c, P * h:P * h + P],
                                                  g.YT[:, c, bass.ds(GROUP * n, GROUP)], start=(c == 0), stop=(c == DC - 1))
                        mm.then_inc(made_h, 1)

                def second_product(s, e):
                    pe.wait_ge(took_h, HC * (s + 1))
                    for j in range(4):
                        at_least(pe, added_y, 4 * (s - 1) + j + 1)
                        for h in range(HC):
                            mm = nc.tensor.matmul(ps_y[:, j, 0:D], hidden[:, e % 2, h, P * j:P * j + P], g.w2[:, e, h, :],
                                                  start=(h == 0), stop=(h == HC - 1))
                        mm.then_inc(made_y, 1)

                def body(n, first):
                    for e in range(E):
                        first_product(n, e)
                        if e > 0 or not first:
                            second_product(E * n + e - 1, (e - 1) % E)

                for t in range(PAIRS):
                    at_least(pe, biased, t - 3)
                    nc.tensor.matmul(ps_y[:, t % 4, 0:D], g.share_t[:, P * t:P * t + P], g.b2[:],
                                     start=True, stop=True).then_inc(made_y, 1)
                pe.wait_ge(biased, PAIRS)
                steps(pe, body)
                second_product(E * GROUPS - 1, E - 1)

            @block.scalar
            def _(act):
                def body(n, first):
                    for e in range(E):
                        for h in range(HC):
                            act.wait_ge(made_h, HC * (E * n + e) + h + 1)
                            nc.scalar.activation(hidden[:, e % 2, h, :], ps_h[:, h, :], ACT.Relu,
                                                 bias=g.b1[:, e, h:h + 1], scale=1.0).then_inc(took_h, 1)

                act.preload_act_table(ACT.Relu)
                steps(act, body)

            @block.vector
            def _(dve):
                def add(s, n, e):
                    for j in range(4):
                        t = 4 * n + j
                        dve.wait_ge(made_y, PAIRS + 4 * s + j + 1)
                        nc.vector.scalar_tensor_tensor(g.X[:, t, :], ps_y[:, j, 0:D], g.share[:, t, e:e + 1],
                                                       g.X[:, t, :], ALU.mult, ALU.add).then_inc(added_y, 1)

                for t in range(PAIRS):
                    dve.wait_ge(made_y, t + 1)
                    nc.vector.tensor_tensor(g.X[:, t, :], g.X[:, t, :], ps_y[:, t % 4, 0:D], ALU.add).then_inc(biased, 1)
                with dve.Fori(0, GROUPS) as n:
                    for e in range(E):
                        add(E * n + e, n, e)


def wide_queries(nc, g, a, wq, bq, wk_t, bk, qk_all, shift):
    with ExitStack() as stack:
        m = Memory(nc, stack)
        q_t = m.sb("wide_q_t", [P, DC, ROWS])
        bv = m.sb("wide_bv", [P, D])
        ps_q = m.psum("wide_ps_q", [P, 2, DC, 512])
        ps_qk = m.psum("wide_ps_qk", [P, 2, 512])
        ps_shift = m.psum("wide_ps_shift", [P, PAIRS])
        weights, bv_loaded, bv_added, made_q, took_q, made_qk, took_qk, made_shift, took_shift = (
            m.sem(f"wide_{n}") for n in ("weights", "bv_loaded", "bv_added", "made_q", "took_q", "made_qk", "took_qk",
                                         "made_shift", "took_shift"))
        with nc.Block() as block:

            @block.sync
            def _(sp):
                sp.dma_start(wq[:], a["wide_wq"].rearrange("(c p) n -> p c n", p=P)).then_inc(weights, 16)
                sp.dma_start(wk_t[:], a["wide_wk_t"].rearrange("(c p) n -> p c n", p=P)).then_inc(weights, 16)
                sp.dma_start(bq[:], a["wide_bq"]).then_inc(weights, 16)
                sp.dma_start(bk[:], a["wide_bk"]).then_inc(weights, 16)
                sp.dma_start(bv[:], a["wide_bv"].partition_broadcast(P)).then_inc(bv_loaded, 16)

            @block.gpsimd
            def _(pool):
                pool.wait_ge(bv_loaded, 16)
                nc.gpsimd.tensor_tensor(g.X[:], g.X[:], bv[:].unsqueeze(1).to_broadcast([P, PAIRS, D]),
                                        ALU.add).then_inc(bv_added, 1)

            @block.tensor
            def _(pe):
                def queries(n):
                    at_least(pe, took_q, n - 1)
                    for oc in range(DC):
                        for c in range(DC):
                            mm = nc.tensor.matmul(ps_q[:, n % 2, oc, :], wq[:, c, P * oc:P * oc + P],
                                                  g.YT[:, c, GROUP * n:GROUP * n + GROUP], start=(c == 0), stop=(c == DC - 1))
                    mm.then_inc(made_q, 1)

                pe.wait_ge(weights, 64)
                queries(0)
                for n in range(GROUPS):
                    if n + 1 < GROUPS:
                        queries(n + 1)
                    pe.wait_ge(took_q, n + 1)
                    at_least(pe, took_qk, n - 1)
                    for c in range(DC):
                        mm = nc.tensor.matmul(ps_qk[:, n % 2, :], wk_t[:, c, :], q_t[:, c, GROUP * n:GROUP * n + GROUP],
                                              start=(c == 0), stop=(c == DC - 1))
                    mm.then_inc(made_qk, 1)
                for t in range(PAIRS):
                    for c in range(DC):
                        mm = nc.tensor.matmul(ps_shift[:, t:t + 1], q_t[:, c, P * t:P * t + P], bk[:, c:c + 1],
                                              start=(c == 0), stop=(c == DC - 1))
                mm.then_inc(made_shift, 1)

            @block.scalar
            def _(act):
                for n in range(GROUPS):
                    act.wait_ge(made_q, n + 1)
                    for c in range(DC):
                        ins = nc.scalar.activation(q_t[:, c, GROUP * n:GROUP * n + GROUP], ps_q[:, n % 2, c, :],
                                                   ACT.Identity, bias=bq[:, c:c + 1], scale=1.0)
                    ins.then_inc(took_q, 1)

            @block.vector
            def _(dve):
                for n in range(GROUPS):
                    dve.wait_ge(made_qk, n + 1)
                    nc.vector.tensor_copy(qk_all[:, GROUP * n:GROUP * n + GROUP], ps_qk[:, n % 2, :]).then_inc(took_qk, 1)
                dve.wait_ge(made_shift, 1)
                nc.vector.tensor_copy(shift[:], ps_shift[:]).then_inc(took_shift, 1)


def wide_cross_attention(nc, g, a):
    with ExitStack() as stack:
        m = Memory(nc, stack)
        wq, wk_t, wv = m.sb("wide_wq", [P, DC, D]), m.sb("wide_wk_t", [P, DC, C]), m.sb("wide_wv", [C, D])
        bq, bk = m.sb("wide_bq", [P, DC]), m.sb("wide_bk", [P, DC])
        qk_all, shift = m.sb("wide_qk_all", [C, ROWS]), m.sb("wide_shift", [P, PAIRS])
        wide_queries(nc, g, a, wq, bq, wk_t, bk, qk_all, shift)

        ctx = m.sb("wide_ctx", [P, 2, 2, len(KT), C])
        ctx_t = m.sb("wide_ctx_t", [C, 2, LK])
        qk = m.sb("wide_qk", [C, 2, P])
        neg_max, lowered, bias, row_sum, inv_sum = (m.sb(f"wide_{n}", [P, 2]) for n in
                                                    ("neg_max", "lowered", "bias", "row_sum", "inv_sum"))
        probs = m.sb("wide_probs", [P, 2, LK])
        probs_t = m.sb("wide_probs_t", [P, len(KT) * P])
        mixed, mixed_t = m.sb("wide_mixed", [P, C]), m.sb("wide_mixed_t", [C, P])
        scores = m.psum("wide_scores", [P, 2048])
        turned = m.psum("wide_turned", [P, 2, 512])
        mix, small = m.psum("wide_mix", [P, 512]), m.psum("wide_small", [P, 512])
        sem = m.sem
        wv_loaded, ctx_t_loaded, qk_copied = sem("wide_wv_loaded"), sem("wide_ctx_t_loaded"), sem("wide_qk_copied")
        ctx_loaded = [sem("wide_ctx_loaded_0"), sem("wide_ctx_loaded_1")]
        scores_ready, max_ready, probs_ready = sem("wide_scores_ready"), sem("wide_max_ready"), sem("wide_probs_ready")
        lowered_ready, bias_ready = sem("wide_lowered_ready"), sem("wide_bias_ready")
        turned_ready, copied_act, copied_dve = sem("wide_turned_ready"), sem("wide_copied_act"), sem("wide_copied_dve")
        mix_ready, inv_ready, mixed_ready = sem("wide_mix_ready"), sem("wide_inv_ready"), sem("wide_mixed_ready")
        mixed_turned, mixed_t_ready, out_ready, out_added = (sem("wide_mixed_turned"), sem("wide_mixed_t_ready"),
                                                             sem("wide_out_ready"), sem("wide_out_added"))

        def pairs(eng, body):
            for u in range(2):
                body(u, u, u > 0, True)
            with eng.Fori(1, PAIRS // 2 - 1) as i:
                for u in range(2):
                    body(2 * i + u, u, True, True)
            for u in range(2):
                body(PAIRS - 2 + u, u, True, u == 0)

        with nc.Block() as block:

            @block.sync
            def _(sp):
                def load_t(p):
                    sp.dma_start(ctx_t[:], a["ctx_t"][bass.ds(2 * p, 2)].rearrange("b f k -> f b k")).then_inc(ctx_t_loaded, 16)

                def load(p, u):
                    for b in range(2):
                        sp.dma_start(ctx[:, u, b, 0:KFULL, :], a["ctx_main"][2 * p + b]).then_inc(ctx_loaded[u], 16)
                        sp.dma_start(ctx[0:KREST, u, b, KFULL, :], a["ctx_rest"][2 * p + b]).then_inc(ctx_loaded[u], 16)

                sp.dma_start(wv[:], a["wide_wv"]).then_inc(wv_loaded, 16)
                load_t(0)
                load(0, 0)
                sp.wait_ge(scores_ready, 1)
                load_t(1)
                load(1, 1)
                with sp.Fori(1, PAIRS // 2) as i:
                    for u in range(2):
                        p = 2 * i + u
                        sp.wait_ge(scores_ready, p)
                        load_t(p)
                        sp.wait_ge(mix_ready, p - 1)
                        load(p, u)

            @block.gpsimd
            def _(pool):
                for u in range(2):
                    nc.gpsimd.tensor_copy(qk[:, u, :], qk_all[:, P * u:P * u + P]).then_inc(qk_copied, 1)
                with pool.Fori(1, PAIRS // 2) as i:
                    for u in range(2):
                        pool.wait_ge(scores_ready, 2 * i + u - 1)
                        pool.wait_ge(qk_copied, 2)
                        nc.gpsimd.tensor_copy(qk[:, u, :], qk_all[:, bass.ds(P * (2 * i + u), P)]).then_inc(qk_copied, 1)

            @block.tensor
            def _(pe):
                def score(p, u):
                    pe.wait_ge(ctx_t_loaded, 16 * (p + 1))
                    pe.wait_ge(qk_copied, p + 1)
                    for lo, n in SCORE_CHUNKS:
                        for b in range(2):
                            mm = nc.tensor.matmul(scores[T * b:T * b + T, lo:lo + n], qk[:, u, T * b:T * b + T],
                                                  ctx_t[:, b, lo:lo + n], start=True, stop=True)
                    mm.then_inc(scores_ready, 1)

                def turn_mixed(p):
                    pe.wait_ge(mixed_ready, p + 1)
                    at_least(pe, out_added, p)
                    nc.tensor.transpose(small[:, 0:P], mixed[:], g.ident[:]).then_inc(mixed_turned, 1)

                def project(p):
                    pe.wait_ge(mixed_t_ready, p + 1)
                    nc.tensor.matmul(small[:, 0:D], mixed_t[:], wv[:], start=True, stop=True).then_inc(out_ready, 1)

                def body(p, u, before, after):
                    pe.wait_ge(probs_ready, p + 1)
                    if after:
                        score(p + 1, 1 - u)
                    if before:
                        turn_mixed(p - 1)

                    def turn(k):
                        if k >= 2:
                            pe.wait_ge(copied_act, 2 * p + k - 1)
                        for t in KGROUPS[k]:
                            lo, n = KT[t]
                            mm = nc.tensor.transpose(turned[0:n, k % 2, P * (t % 4):P * (t % 4) + P],
                                                     probs[:, u, lo:lo + n], g.ident[:])
                        mm.then_inc(turned_ready, 1)

                    def weigh(k):
                        if k < 2:
                            pe.wait_ge(copied_act, 2 * p + k + 1)
                        else:
                            pe.wait_ge(copied_dve, 2 * p + k - 1)
                        if k == 0:
                            pe.wait_ge(ctx_loaded[u], 32 * (p - u) + 64)
                        for t in KGROUPS[k]:
                            n = KT[t][1]
                            for b in range(2):
                                mm = nc.tensor.matmul(mix[T * b:T * b + T, 0:C], probs_t[0:n, P * t + T * b:P * t + T * b + T],
                                                      ctx[0:n, u, b, t, :], start=(t == 0), stop=(t == len(KT) - 1))
                        if k == 3:
                            mm.then_inc(mix_ready, 1)

                    turn(0)
                    turn(1)
                    weigh(0)
                    turn(2)
                    if before:
                        project(p - 1)
                    weigh(1)
                    turn(3)
                    weigh(2)
                    weigh(3)

                pe.wait_ge(wv_loaded, 16)
                score(0, 0)
                pairs(pe, body)
                turn_mixed(PAIRS - 1)
                project(PAIRS - 1)

            @block.scalar
            def _(act):
                def exp(p, u):
                    act.wait_ge(bias_ready, p + 1)
                    nc.scalar.activation(probs[:, u, :], scores[:, 0:LK], ACT.Exp, bias=bias[:, u:u + 1], scale=1.0,
                                         accum_out=row_sum[:, u:u + 1]).then_inc(probs_ready, 1)

                def take_mixed(p):
                    act.wait_ge(mixed_turned, p + 1)
                    nc.scalar.copy(mixed_t[:], small[:, 0:P]).then_inc(mixed_t_ready, 1)

                def body(p, u, before, after):
                    if before:
                        take_mixed(p - 1)
                    for k in range(2):
                        act.wait_ge(turned_ready, 4 * p + k + 1)
                        nc.scalar.copy(probs_t[:, 512 * k:512 * k + 512], turned[:, k, :]).then_inc(copied_act, 1)
                    if after:
                        exp(p + 1, 1 - u)

                act.preload_act_table(ACT.Exp)
                exp(0, 0)
                pairs(act, body)
                take_mixed(PAIRS - 1)

            @block.vector
            def _(dve):
                def row_max(p, u):
                    dve.wait_ge(scores_ready, p + 1)
                    nc.vector.tensor_reduce(neg_max[:, u:u + 1], scores[:, 0:LK], AX_X, ALU.max, negate=True)\
                        .then_inc(max_ready, 1)
                    dve.wait_ge(max_ready, p + 1)
                    nc.vector.tensor_tensor(lowered[:, u:u + 1], neg_max[:, u:u + 1], shift[:, bass.ds(p, 1)],
                                            ALU.subtract).then_inc(lowered_ready, 1)
                    dve.wait_ge(lowered_ready, p + 1)
                    nc.vector.tensor_tensor(bias[:, u:u + 1], lowered[:, u:u + 1], shift[:, bass.ds(p, 1)],
                                            ALU.add).then_inc(bias_ready, 1)

                def add_out(p):
                    dve.wait_ge(out_ready, p + 1)
                    nc.vector.tensor_tensor(g.X[:, p, :], g.X[:, p, :], small[:, 0:D], ALU.add).then_inc(out_added, 1)

                def body(p, u, before, after):
                    if after:
                        row_max(p + 1, 1 - u)
                    dve.wait_ge(probs_ready, p + 1)
                    nc.vector.reciprocal(inv_sum[:, u:u + 1], row_sum[:, u:u + 1]).then_inc(inv_ready, 1)
                    for k in (2, 3):
                        dve.wait_ge(turned_ready, 4 * p + k + 1)
                        n, w = KT[KGROUPS[k][-1]][1], P * len(KGROUPS[k])
                        nc.vector.tensor_copy(probs_t[0:n, 512 * k:512 * k + w], turned[0:n, k % 2, 0:w])\
                            .then_inc(copied_dve, 1)
                    if before:
                        add_out(p - 1)
                    dve.wait_ge(mix_ready, p + 1)
                    dve.wait_ge(inv_ready, p + 1)
                    nc.vector.tensor_scalar(mixed[:], mix[:, 0:C], inv_sum[:, u:u + 1], None, ALU.mult)\
                        .then_inc(mixed_ready, 1)

                row_max(0, 0)
                pairs(dve, body)
                add_out(PAIRS - 1)


NH, HE = 4, 64
QK = (NH + 1) * HE
QKV = QK + HE
HALF = HE // 2
RMS_EPS = 1e-6


def rotary_qkv(nc, g, a, qkv):
    with ExitStack() as stack:
        m = Memory(nc, stack)
        w = m.sb("self_wqkv", [P, DC, QKV])
        angles = m.sb("self_angles", [P, 2, HALF])
        gain_q, gain_k = m.sb("self_gain_q", [P, HE]), m.sb("self_gain_k", [P, HE])
        table = {n: m.sb(f"self_table_{n}", [P, NH + 1, HALF]) for n in "abcd"}
        square = m.sb("self_square", [P, PAIRS, QK])
        power, root = m.sb("self_power", [P, PAIRS * (NH + 1)]), m.sb("self_root", [P, PAIRS * (NH + 1)])
        part = {n: m.sb(f"self_part_{n}", [P, PAIRS, NH + 1, HALF]) for n in "abcd"}
        ps = m.psum("self_ps_qkv", [P, 4, 512])
        loaded, made, taken, power_done, root_done, step = (m.sem(f"self_{n}") for n in
                                                            ("loaded", "made", "taken", "power_done", "root_done", "step"))
        halves = qkv[:, :, 0:QK].rearrange("p t (h j two) -> p t h j two", h=NH + 1, two=2)
        even, odd = halves[:, :, :, :, 0], halves[:, :, :, :, 1]
        heads = qkv[:, :, 0:QK].rearrange("p t (h j) -> p t h j", h=NH + 1)

        with nc.Block() as block:

            @block.sync
            def _(sp):
                sp.dma_start(w[:], a["self_wqkv_t"].rearrange("(c p) n -> p c n", p=P)).then_inc(loaded, 16)
                sp.dma_start(angles[:], a["self_angles"]).then_inc(loaded, 16)
                sp.dma_start(gain_q[:], a["self_gain_q"].partition_broadcast(P)).then_inc(loaded, 16)
                sp.dma_start(gain_k[:], a["self_gain_k"].partition_broadcast(P)).then_inc(loaded, 16)

            @block.tensor
            def _(pe):
                pe.wait_ge(loaded, 64)
                for t in range(PAIRS):
                    at_least(pe, taken, t - 3)
                    for c in range(DC):
                        mm = nc.tensor.matmul(ps[:, t % 4, 0:QKV], g.YT[:, c, P * t:P * t + P], w[:, c, :],
                                              start=(c == 0), stop=(c == DC - 1))
                    mm.then_inc(made, 1)

            @block.scalar
            def _(act):
                for t in range(PAIRS):
                    act.wait_ge(made, t + 1)
                    nc.scalar.copy(qkv[:, t, :], ps[:, t % 4, 0:QKV]).then_inc(taken, 1)
                act.wait_ge(power_done, 1)
                nc.scalar.activation(root[:], power[:], ACT.Sqrt).then_inc(root_done, 1)

            @block.vector
            def _(dve):
                chain = Chain(dve, step)
                tt, link = nc.vector.tensor_tensor, chain.step
                dve.wait_ge(loaded, 64)
                for name, wave, side in (("a", 0, 0), ("b", 1, 1), ("c", 1, 0), ("d", 0, 1)):
                    for lo, hi, gain in ((0, NH, gain_q), (NH, NH + 1, gain_k)):
                        n = hi - lo
                        link(tt(table[name][:, lo:hi, :], angles[:, wave, :].unsqueeze(1).to_broadcast([P, n, HALF]),
                                gain[:].rearrange("p (j two) -> p two j", two=2)[:, side, :].unsqueeze(1).to_broadcast([P, n, HALF]),
                                ALU.mult))
                    link(nc.vector.tensor_scalar(table[name][:, 0:NH, :], table[name][:, 0:NH, :], HE ** -0.5, None, ALU.mult))
                for n in range(4):
                    dve.wait_ge(taken, 4 * n + 4)
                    t = slice(4 * n, 4 * n + 4)
                    link(tt(square[:, t, :], qkv[:, t, 0:QK], qkv[:, t, 0:QK], ALU.mult))
                    link(nc.vector.tensor_reduce(power[:, 4 * n * (NH + 1):4 * (n + 1) * (NH + 1)],
                                                 square[:, t, :].rearrange("p t (h j) -> p (t h) j", j=HE), AX_X, ALU.add))
                nc.vector.tensor_scalar(power[:], power[:], 1.0 / HE, RMS_EPS, ALU.mult, ALU.add).then_inc(power_done, 1)
                dve.wait_ge(root_done, 1)
                link(nc.vector.reciprocal(power[:], root[:]))
                flat = qkv[:, :, 0:QK].rearrange("p t (h j) -> p t h j", h=NH + 1)
                link(tt(flat, flat, power[:].rearrange("p (t h) -> p t h", t=PAIRS).unsqueeze(3)
                        .to_broadcast([P, PAIRS, NH + 1, HE]), ALU.mult))
                for name, side in (("a", even), ("b", odd), ("c", even), ("d", odd)):
                    link(tt(part[name][:], side, table[name][:].unsqueeze(1).to_broadcast([P, PAIRS, NH + 1, HALF]), ALU.mult))
                link(tt(even, part["a"][:], part["b"][:], ALU.subtract))
                link(tt(odd, part["c"][:], part["d"][:], ALU.add))


def self_attention(nc, g, a):
    with ExitStack() as stack:
        m = Memory(nc, stack)
        qkv = m.sb("self_qkv", [P, PAIRS, QKV])
        rotary_qkv(nc, g, a, qkv)
        wo = m.sb("self_wo", [P, DC, D])
        mask = m.sb("self_mask", [P, P])
        now = m.sb("self_now", [P, QK + HE])
        q_t = m.sb("self_q_t", [P, DC, P])
        k_blocks = m.sb("self_k_blocks", [P, 2, P])
        masked, probs, shares = (m.sb(f"self_{n}", [P, NH, P]) for n in ("masked", "probs", "shares"))
        neg_max, row_sum, inv_sum = (m.sb(f"self_{n}", [P, NH]) for n in ("neg_max", "row_sum", "inv_sum"))
        shares_t = m.sb("self_shares_t", [P, NH, P])
        heads_out, heads_out_t = m.sb("self_heads_out", [P, D]), m.sb("self_heads_out_t", [P, DC, P])
        bank = {n: m.psum(f"self_ps_{n}", [P, 512]) for n in ("turn_qk", "scores", "turn_p", "mix", "turn_o", "out")}
        sem = m.sem
        loaded, zeroed, now_ready = sem("self_att_loaded"), sem("self_zeroed"), sem("self_now_ready")
        qk_turned, qk_taken, scores_ready = sem("self_qk_turned"), sem("self_qk_taken"), sem("self_scores_ready")
        masked_ready, max_ready, probs_ready = sem("self_masked_ready"), sem("self_max_ready"), sem("self_probs_ready")
        inv_ready, shares_ready = sem("self_inv_ready"), sem("self_shares_ready")
        shares_turned, shares_taken = sem("self_shares_turned"), sem("self_shares_taken")
        mix_ready, mix_taken = sem("self_mix_ready"), sem("self_mix_taken")
        out_turned, out_taken, out_ready, out_added = (sem("self_out_turned"), sem("self_out_taken"),
                                                       sem("self_out_ready"), sem("self_out_added"))
        LAST = 5

        def turns(eng, body):
            for i in range(LAST + 1):
                body(i, lambda k: 0 <= i - k)
            with eng.Fori(LAST + 1, PAIRS) as i:
                body(i, lambda k: True)
            for i in range(PAIRS, PAIRS + LAST):
                body(i, lambda k: i - k < PAIRS)

        with nc.Block() as block:

            @block.sync
            def _(sp):
                sp.dma_start(wo[:], a["self_wo_t"].rearrange("(c p) n -> p c n", p=P)).then_inc(loaded, 16)
                sp.dma_start(mask[:], a["self_mask"]).then_inc(loaded, 16)

            @block.gpsimd
            def _(pool):
                nc.gpsimd.memset(k_blocks[:], 0.0).then_inc(zeroed, 1)

                def copy(i):
                    if not isinstance(i, int) or i > 0:
                        pool.wait_ge(qk_turned, i)
                        pool.wait_ge(zeroed, 1)
                    nc.gpsimd.tensor_copy(now[:, 0:QK], qkv[:, i, 0:QK]).then_inc(now_ready, 1)
                    nc.gpsimd.tensor_copy(now[:, QK:QK + HE], qkv[:, i, QK - HE:QK]).then_inc(now_ready, 1)

                copy(0)
                with pool.Fori(1, PAIRS) as i:
                    copy(i)

            @block.tensor
            def _(pe):
                def body(i, stage):
                    if stage(5):
                        pe.wait_ge(out_taken, i - 4)
                        at_least(pe, out_added, i - 5)
                        for c in range(DC):
                            mm = nc.tensor.matmul(bank["out"][:, 0:D], heads_out_t[:, c, :], wo[:, c, :],
                                                  start=(c == 0), stop=(c == DC - 1))
                        mm.then_inc(out_ready, 1)
                    if stage(4):
                        pe.wait_ge(mix_taken, i - 3)
                        for c in range(DC):
                            mm = nc.tensor.transpose(bank["turn_o"][:, P * c:P * c + P], heads_out[:, P * c:P * c + P], g.ident[:])
                        mm.then_inc(out_turned, 1)
                    if stage(3):
                        pe.wait_ge(shares_taken, i - 2)
                        for h in range(NH):
                            mm = nc.tensor.matmul(bank["mix"][:, HE * h:HE * h + HE], shares_t[:, h, :],
                                                  qkv[:, i - 3, QK:QKV], start=True, stop=True)
                        mm.then_inc(mix_ready, 1)
                    if stage(2):
                        pe.wait_ge(shares_ready, i - 1)
                        for h in range(NH):
                            mm = nc.tensor.transpose(bank["turn_p"][:, P * h:P * h + P], shares[:, h, :], g.ident[:])
                        mm.then_inc(shares_turned, 1)
                    if stage(1):
                        pe.wait_ge(qk_taken, 3 * i)
                        for c in range(DC):
                            mm = nc.tensor.matmul(bank["scores"][:, 2 * P * c:2 * P * c + 2 * P], q_t[:, c, :], k_blocks[:],
                                                  start=True, stop=True)
                        mm.then_inc(scores_ready, 1)
                    if stage(0):
                        pe.wait_ge(now_ready, 2 * i + 2)
                        for c in range(3):
                            mm = nc.tensor.transpose(bank["turn_qk"][:, P * c:P * c + P], now[:, P * c:P * c + P], g.ident[:])
                        mm.then_inc(qk_turned, 1)

                pe.wait_ge(loaded, 32)
                turns(pe, body)

            @block.scalar
            def _(act):
                def body(i, stage):
                    if stage(4):
                        act.wait_ge(out_turned, i - 3)
                        nc.scalar.copy(heads_out_t[:].rearrange("p c n -> p (c n)"), bank["turn_o"][:, 0:D]).then_inc(out_taken, 1)
                    if stage(3):
                        act.wait_ge(mix_ready, i - 2)
                        nc.scalar.copy(heads_out[:], bank["mix"][:, 0:D]).then_inc(mix_taken, 1)
                    if stage(1):
                        act.wait_ge(max_ready, i)
                        for h in range(NH):
                            nc.scalar.activation(probs[:, h, :], masked[:, h, :], ACT.Exp, bias=neg_max[:, h:h + 1], scale=1.0,
                                                 accum_out=row_sum[:, h:h + 1]).then_inc(probs_ready, 1)
                    if stage(0):
                        act.wait_ge(qk_turned, i + 1)
                        nc.scalar.copy(q_t[:].rearrange("p c n -> p (c n)"), bank["turn_qk"][:, 0:2 * P]).then_inc(qk_taken, 1)
                        for b in range(2):
                            nc.scalar.copy(k_blocks[HE * b:HE * b + HE, b, :], bank["turn_qk"][HE * b:HE * b + HE, 2 * P:3 * P])\
                                .then_inc(qk_taken, 1)

                act.preload_act_table(ACT.Exp)
                act.wait_ge(zeroed, 1)
                turns(act, body)

            @block.vector
            def _(dve):
                def body(i, stage):
                    if stage(5):
                        dve.wait_ge(out_ready, i - 4)
                        nc.vector.tensor_tensor(g.X[:, i - 5, :], g.X[:, i - 5, :], bank["out"][:, 0:D], ALU.add)\
                            .then_inc(out_added, 1)
                    if stage(2):
                        dve.wait_ge(shares_turned, i - 1)
                        nc.vector.tensor_copy(shares_t[:].rearrange("p h n -> p (h n)"), bank["turn_p"][:]).then_inc(shares_taken, 1)
                    if stage(1):
                        dve.wait_ge(scores_ready, i)
                        nc.vector.tensor_tensor(masked[:], bank["scores"][:].rearrange("p (h n) -> p h n", h=NH),
                                                mask[:].unsqueeze(1).to_broadcast([P, NH, P]), ALU.add).then_inc(masked_ready, 1)
                        dve.wait_ge(masked_ready, i)
                        nc.vector.tensor_reduce(neg_max[:], masked[:], AX_X, ALU.max, negate=True).then_inc(max_ready, 1)
                        dve.wait_ge(probs_ready, NH * i)
                        nc.vector.reciprocal(inv_sum[:], row_sum[:]).then_inc(inv_ready, 1)
                        dve.wait_ge(inv_ready, i)
                        nc.vector.tensor_tensor(shares[:], probs[:], inv_sum[:].unsqueeze(2).to_broadcast([P, NH, P]),
                                                ALU.mult).then_inc(shares_ready, 1)

                dve.wait_ge(loaded, 32)
                turns(dve, body)


I = 704
IT = [(i, min(P, I - i)) for i in range(0, I, P)]
IREST = I - P * (I // P)
QMAX = 127.0


class Quantised:

    def __init__(self, m):
        self.gate_t = m.sb("ffn_gate_t", [P, DC, I], BF16)
        self.up_t = m.sb("ffn_up_t", [P, DC, I], BF16)
        self.down_t = m.sb("ffn_down_t", [P, len(IT), D], BF16)
        self.down_scale = m.sb("ffn_down_scale", [P, D])
        self.scale = {n: m.sb(f"ffn_scale_{n}", [P, t]) for n, t in (("gate", len(IT)), ("up", len(IT)), ("down", DC))}


def quantise_weights(nc, g, a, q):
    with ExitStack() as stack:
        m = Memory(nc, stack)
        shapes = {"gate": (len(IT), D), "up": (len(IT), D), "down": (DC, I)}
        w = {n: m.sb(f"quant_{n}", [P, *s]) for n, s in shapes.items()}
        low = {n: m.sb(f"quant_{n}_int", [P, *s], BF16) for n, s in shapes.items()}
        inverse = {n: m.sb(f"quant_{n}_inverse", [P, s[0]]) for n, s in shapes.items()}
        small_ident, ones, diagonal = m.sb("quant_ident", [P, P], BF16), m.sb("quant_ones", [P, P]), m.sb("quant_diagonal", [P, DC, P])
        turned = m.psum("quant_turned", [P, 6, 1024], BF16)
        spread = m.psum("quant_spread", [P, DC, P])
        loaded, filled, step, low_ready, turned_ready, stored, spread_ready, diagonal_ready = (
            m.sem(f"quant_{n}") for n in ("loaded", "filled", "step", "low_ready", "turned_ready", "stored",
                                          "spread_ready", "diagonal_ready"))
        with nc.Block() as block:

            @block.sync
            def _(sp):
                whole = P * (I // P)
                sp.wait_ge(filled, 2)
                for n, src in (("gate", a["quant_gate"]), ("up", a["quant_up"])):
                    sp.dma_start(w[n][:, 0:I // P, :], src[0:whole].rearrange("(t p) h -> p t h", p=P)).then_inc(loaded, 16)
                    sp.dma_start(w[n][0:IREST, I // P, :], src[whole:I]).then_inc(loaded, 16)
                sp.dma_start(w["down"][:], a["quant_down"].rearrange("(t p) i -> p t i", p=P)).then_inc(loaded, 16)

            @block.gpsimd
            def _(pool):
                nc.gpsimd.memset(w["gate"][:, I // P, :], 1.0).then_inc(filled, 1)
                nc.gpsimd.memset(w["up"][:, I // P, :], 1.0).then_inc(filled, 1)
                nc.gpsimd.memset(ones[:], 1.0).then_inc(filled, 1)
                nc.gpsimd.tensor_copy(small_ident[:], g.ident[:]).then_inc(filled, 1)

            @block.vector
            def _(dve):
                chain = Chain(dve, step)
                link = chain.step
                dve.wait_ge(loaded, 80)
                for n, (tiles, width) in shapes.items():
                    link(nc.vector.tensor_reduce(q.scale[n][:], w[n][:], AX_X, ALU.max, apply_absolute_value=True))
                    link(nc.vector.tensor_scalar(q.scale[n][:], q.scale[n][:], 1.0 / QMAX, None, ALU.mult))
                    link(nc.vector.reciprocal(inverse[n][:], q.scale[n][:]))
                    link(nc.vector.tensor_tensor(w[n][:], w[n][:], inverse[n][:].unsqueeze(2).to_broadcast([P, tiles, width]), ALU.mult))
                    link(nc.vector.tensor_scalar(w[n][:], w[n][:], ROUND, ROUND, ALU.add, ALU.subtract))
                    nc.vector.tensor_scalar(low[n][:], w[n][:], QMAX, -QMAX - 1.0, ALU.min, ALU.max).then_inc(low_ready, 1)
                for c in range(DC):
                    nc.vector.tensor_scalar(diagonal[:, c, :], g.ident[:], q.scale["down"][:, c:c + 1], None, ALU.mult)\
                        .then_inc(diagonal_ready, 1)
                dve.wait_ge(spread_ready, 1)
                nc.vector.tensor_copy(q.down_scale[:], spread[:].rearrange("p c n -> p (c n)")).then_inc(stored, 1)

            @block.tensor
            def _(pe):
                pe.wait_ge(filled, 4)
                for k, n in enumerate(("gate", "up")):
                    pe.wait_ge(low_ready, k + 1)
                    for c in range(DC):
                        for t, (lo, size) in enumerate(IT):
                            mm = nc.tensor.transpose(turned[:, 2 * k + c, lo:lo + size], low[n][0:size, t, P * c:P * c + P],
                                                     small_ident[0:size, 0:size])
                        mm.then_inc(turned_ready, 1)
                pe.wait_ge(low_ready, 3)
                for t, (lo, size) in enumerate(IT):
                    for c in range(DC):
                        mm = nc.tensor.transpose(turned[0:size, 4 + t // 4, 256 * (t % 4) + P * c:256 * (t % 4) + P * c + P],
                                                 low["down"][:, c, lo:lo + size], small_ident[:])
                    if t in (3, 5):
                        mm.then_inc(turned_ready, 1)
                pe.wait_ge(diagonal_ready, DC)
                for c in range(DC):
                    mm = nc.tensor.matmul(spread[:, c, :], ones[:], diagonal[:, c, :], start=True, stop=True)
                mm.then_inc(spread_ready, 1)

            @block.scalar
            def _(act):
                for k, out in enumerate((q.gate_t, q.up_t)):
                    for c in range(DC):
                        act.wait_ge(turned_ready, 2 * k + c + 1)
                        nc.scalar.copy(out[:, c, :], turned[:, 2 * k + c, 0:I]).then_inc(stored, 1)
                act.wait_ge(turned_ready, 5)
                nc.scalar.copy(q.down_t[:, 0:4, :].rearrange("p t n -> p (t n)"), turned[:, 4, :]).then_inc(stored, 1)
                act.wait_ge(turned_ready, 6)
                nc.scalar.copy(q.down_t[:, 4, :], turned[:, 5, 0:D]).then_inc(stored, 1)
                nc.scalar.copy(q.down_t[0:IREST, 5, :], turned[0:IREST, 5, D:2 * D]).then_inc(stored, 1)


def largest(nc, m, name, clip, rows_of, scale, inverse):
    top, top_all = m.sb(f"{name}_top", [P, len(rows_of)]), m.sb(f"{name}_top_all", [P, 1])
    best, clip_col, decay = m.sb(f"{name}_best", [P, 1]), m.sb(f"{name}_clip", [P, 1]), m.sb(f"{name}_decay", [P, 1])
    loaded, zeroed, step, best_ready, all_ready, decay_ready = (m.sem(f"{name}_{n}") for n in
                                                        ("loaded", "zeroed", "step", "best_ready", "all_ready", "decay_ready"))
    with nc.Block() as block:

        @block.sync
        def _(sp):
            sp.dma_start(clip_col[:], clip.partition_broadcast(P)).then_inc(loaded, 16)

        @block.gpsimd
        def _(pool):
            pool.wait_ge(best_ready, 1)
            nc.gpsimd.partition_all_reduce(top_all[:], best[:], P, bass.bass_isa.ReduceOp.max).then_inc(all_ready, 1)

        @block.scalar
        def _(act):
            act.wait_ge(loaded, 16)
            nc.scalar.activation(decay[:], clip_col[:], ACT.Exp, scale=-1.0).then_inc(decay_ready, 1)

        @block.vector
        def _(dve):
            chain = Chain(dve, step)
            link = chain.step
            link(nc.vector.memset(top[:], 0.0))
            for k, (rows, part) in enumerate(rows_of):
                link(nc.vector.tensor_reduce(top[0:rows, k:k + 1], part, AX_X, ALU.max, apply_absolute_value=True))
            nc.vector.tensor_reduce(best[:], top[:], AX_X, ALU.max).then_inc(best_ready, 1)
            dve.wait_ge(decay_ready, 1)
            link(nc.vector.tensor_scalar(decay[:], decay[:], 1.0, None, ALU.add))
            link(nc.vector.reciprocal(decay[:], decay[:]))
            dve.wait_ge(all_ready, 1)
            link(nc.vector.tensor_scalar(scale[:], top_all[:], decay[:], 1.0 / QMAX, ALU.mult, ALU.mult))
            link(nc.vector.reciprocal(inverse[:], scale[:]))


def quantised_ffn(nc, g, a):
    with ExitStack() as stack:
        m = Memory(nc, stack)
        q = Quantised(m)
        quantise_weights(nc, g, a, q)
        x_scale, x_inverse, h_scale, h_inverse = (m.sb(f"ffn_{n}", [P, 1]) for n in
                                                  ("x_scale", "x_inverse", "h_scale", "h_inverse"))
        hidden = m.sb("ffn_hidden", [P, len(IT), ROWS])
        largest(nc, m, "ffn_x", a["quant_clip_x"], [(P, g.YT[:, c, :]) for c in range(DC)], x_scale, x_inverse)
        gate_and_up(nc, g, q, x_scale, x_inverse, hidden)
        parts = [(size, hidden[0:size, t, :]) for t, (lo, size) in enumerate(IT)]
        largest(nc, m, "ffn_h", a["quant_clip_down"], parts, h_scale, h_inverse)
        down(nc, g, q, h_scale, h_inverse, hidden)


def gate_and_up(nc, g, q, x_scale, x_inverse, hidden):
    with ExitStack() as stack:
        m = Memory(nc, stack)
        low = m.sb("gate_low", [P, DC, ROWS], BF16)
        gate_scale, up_scale = m.sb("gate_scale", [P, len(IT)]), m.sb("up_scale", [P, len(IT)])
        active = m.sb("gate_active", [P, 2, 512])
        round_col = m.sb("gate_round", [P, 1])
        ps_gate, ps_up = m.psum("gate_ps_gate", [P, 2, 512]), m.psum("gate_ps_up", [P, 2, 512])
        filled, scales_ready, rounded, clipped, low_ready = (m.sem(f"gate_{n}") for n in
                                                             ("filled", "scales_ready", "rounded", "clipped", "low_ready"))
        made, active_ready, hidden_ready = m.sem("gate_made"), m.sem("gate_active_ready"), m.sem("gate_hidden_ready")
        tiles = [(n, t, lo, size) for n in range(GROUPS) for t, (lo, size) in enumerate(IT)]
        with nc.Block() as block:

            @block.vector
            def _(dve):
                nc.vector.memset(round_col[:], ROUND).then_inc(filled, 1)
                nc.vector.tensor_scalar(gate_scale[:], q.scale["gate"][:], x_scale[:], None, ALU.mult).then_inc(scales_ready, 1)
                nc.vector.tensor_scalar(up_scale[:], q.scale["up"][:], x_scale[:], None, ALU.mult).then_inc(scales_ready, 1)
                for n in range(GROUPS):
                    r = slice(GROUP * n, GROUP * n + GROUP)
                    dve.wait_ge(rounded, n + 1)
                    nc.vector.tensor_scalar(g.YT[:, :, r], g.YT[:, :, r], ROUND + QMAX, ROUND - QMAX - 1.0, ALU.min,
                                            ALU.max).then_inc(clipped, 1)
                    dve.wait_ge(clipped, n + 1)
                    nc.vector.tensor_scalar(low[:, :, r], g.YT[:, :, r], ROUND, None, ALU.subtract).then_inc(low_ready, 1)
                dve.wait_ge(scales_ready, 2)
                for k, (n, t, lo, size) in enumerate(tiles):
                    dve.wait_ge(active_ready, k + 1)
                    nc.vector.scalar_tensor_tensor(hidden[0:size, t, GROUP * n:GROUP * n + GROUP], ps_up[0:size, k % 2, :],
                                                   up_scale[0:size, t:t + 1], active[0:size, k % 2, :], ALU.mult, ALU.mult)\
                        .then_inc(hidden_ready, 1)

            @block.scalar
            def _(act):
                act.wait_ge(filled, 1)
                for n in range(GROUPS):
                    r = slice(GROUP * n, GROUP * n + GROUP)
                    nc.scalar.activation(g.YT[:, :, r], g.YT[:, :, r], ACT.Identity, bias=round_col[:],
                                         scale=x_inverse[:]).then_inc(rounded, 1)
                act.wait_ge(scales_ready, 2)
                for k, (n, t, lo, size) in enumerate(tiles):
                    act.wait_ge(made, k + 1)
                    at_least(act, hidden_ready, k - 1)
                    nc.scalar.activation(active[0:size, k % 2, :], ps_gate[0:size, k % 2, :], ACT.Silu,
                                         scale=gate_scale[0:size, t:t + 1]).then_inc(active_ready, 1)

            @block.tensor
            def _(pe):
                for k, (n, t, lo, size) in enumerate(tiles):
                    pe.wait_ge(low_ready, n + 1)
                    at_least(pe, hidden_ready, k - 1)
                    for ps, w in ((ps_gate, q.gate_t), (ps_up, q.up_t)):
                        for c in range(DC):
                            mm = nc.tensor.matmul(ps[0:size, k % 2, :], w[:, c, lo:lo + size], low[:, c, GROUP * n:GROUP * n + GROUP],
                                                  start=(c == 0), stop=(c == DC - 1))
                    mm.then_inc(made, 1)


def down(nc, g, q, h_scale, h_inverse, hidden):
    with ExitStack() as stack:
        m = Memory(nc, stack)
        low = m.sb("down_low", [P, len(IT), ROWS], BF16)
        round_col, scale = m.sb("down_round", [P, 1]), m.sb("down_scale", [P, D])
        scaled = m.sb("down_scaled", [P, 2, D])
        ps = m.psum("down_ps", [P, 4, 512])
        filled, rounded, clipped, low_ready, scale_ready, made, scaled_ready, added = (
            m.sem(f"down_{n}") for n in ("filled", "rounded", "clipped", "low_ready", "scale_ready", "made",
                                         "scaled_ready", "added"))
        parts = [(n, t, size) for n in range(GROUPS) for t, (lo, size) in ((slice(0, 5), (0, P)), (slice(5, 6), (0, IREST)))]
        with nc.Block() as block:

            @block.scalar
            def _(act):
                act.wait_ge(filled, 1)
                for n, t, size in parts:
                    v = hidden[0:size, t, GROUP * n:GROUP * n + GROUP]
                    nc.scalar.activation(v, v, ACT.Identity, bias=round_col[0:size], scale=h_inverse[0:size]).then_inc(rounded, 1)

            @block.vector
            def _(dve):
                nc.vector.memset(round_col[:], ROUND).then_inc(filled, 1)
                nc.vector.tensor_scalar(scale[:], q.down_scale[:], h_scale[:], None, ALU.mult).then_inc(scale_ready, 1)
                dve.wait_ge(scale_ready, 1)

                def quantise(k):
                    n, t, size = parts[k]
                    v = hidden[0:size, t, GROUP * n:GROUP * n + GROUP]
                    dve.wait_ge(rounded, k + 1)
                    nc.vector.tensor_scalar(v, v, ROUND + QMAX, ROUND - QMAX - 1.0, ALU.min, ALU.max).then_inc(clipped, 1)
                    dve.wait_ge(clipped, k + 1)
                    nc.vector.tensor_scalar(low[0:size, t, GROUP * n:GROUP * n + GROUP], v, ROUND, None, ALU.subtract)\
                        .then_inc(low_ready, 1)

                for n in range(GROUPS + 1):
                    if n < GROUPS:
                        quantise(2 * n)
                        quantise(2 * n + 1)
                    if n == 0:
                        continue
                    for r in range(4 * (n - 1), 4 * n):
                        dve.wait_ge(made, r + 1)
                        at_least(dve, added, r - 1)
                        nc.vector.tensor_tensor(scaled[:, r % 2, :], ps[:, r % 4, 0:D], scale[:], ALU.mult).then_inc(scaled_ready, 1)
                        dve.wait_ge(scaled_ready, r + 1)
                        nc.vector.tensor_tensor(g.X[:, r, :], g.X[:, r, :], scaled[:, r % 2, :], ALU.add).then_inc(added, 1)

            @block.tensor
            def _(pe):
                for r in range(PAIRS):
                    pe.wait_ge(low_ready, 2 * (r // 4) + 2)
                    at_least(pe, scaled_ready, r - 3)
                    for t, (lo, size) in enumerate(IT):
                        mm = nc.tensor.matmul(ps[:, r % 4, 0:D], low[0:size, t, P * r:P * r + P], q.down_t[0:size, t, :],
                                              start=(t == 0), stop=(t == len(IT) - 1))
                    mm.then_inc(made, 1)


def store(nc, g, out):
    with ExitStack() as stack:
        out_stored = Memory(nc, stack).sem("out_stored")
        with nc.Block() as block:

            @block.sync
            def _(sp):
                sp.dma_start(out.rearrange("(p b) q d -> (b q) p d", b=2), g.X[:]).then_inc(out_stored, 16)
                sp.wait_ge(out_stored, 16)


def lay_out(inputs):
    import numpy as np
    f = {k: np.asarray(v) for k, v in inputs.items()}
    ctx = f["ctx_512"]
    wkv = f["L0_xattn_Wkv"]
    main = ctx[:, :KFULL * P].reshape(B, KFULL, P, C).transpose(0, 2, 1, 3)
    arrays = dict(
        x=f["x"], ctx_main=main, ctx_rest=ctx[:, KFULL * P:], ctx_t=ctx.transpose(0, 2, 1),
        wq_t=f["L0_xattn_Wq"].T, wkv=wkv, wv_t=wkv[D:].T, wo_t=f["L0_xattn_Wo"].T,
    )
    columns = [f[f"L0_attn_{n}"] for n in ("bk", "bv", "bq", "bkp", "bqp", "phase_scale", "ln_g", "ln_b")]
    arrays.update(
        mix_columns=np.stack(columns).reshape(8, DC, P).transpose(2, 0, 1),
        mix_wk=f["L0_attn_Wk"], mix_wv=f["L0_attn_Wv"], mix_wq=f["L0_attn_Wq"], mix_wkp=f["L0_attn_Wkp"],
        mix_wqp=f["L0_attn_Wqp"], mix_wo=f["L0_attn_Wo"], mix_bo=f["L0_attn_bo"],
        router_w=f["L0_ffn_Wr"], router_b=f["L0_ffn_br"], expert_w1=f["L0_ffn_W1"], expert_w2=f["L0_ffn_W2"],
        expert_b1=f["L0_ffn_b1"].reshape(E, HC, P).transpose(2, 0, 1), expert_b2=f["L0_ffn_b2"],
    )
    arrays.update(
        wide_wq=f["L1_xattn_Wq"], wide_wk_t=f["L1_xattn_Wk"].T, wide_wv=f["L1_xattn_Wv"],
        wide_bq=f["L1_xattn_bq"].reshape(DC, P).T, wide_bk=f["L1_xattn_bk"].reshape(DC, P).T, wide_bv=f["L1_xattn_bv"],
    )
    inverse = (1.0 / np.float32(1000000.0) ** (np.arange(0, HE, 2, dtype=np.float32) / np.float32(HE))).astype(np.float32)
    turns = np.outer(np.arange(T, dtype=np.float32), inverse)
    angles = np.tile(np.stack([np.cos(turns), np.sin(turns)], axis=1), (2, 1, 1)).astype(np.float32)
    row, key = np.arange(P)[:, None], np.arange(P)[None, :]
    allowed = (row // T == key // T) & (key <= row) & (key >= row - 128)
    arrays.update(
        self_wqkv_t=np.concatenate([f["L1_attn_Wq"], f["L1_attn_Wk"], f["L1_attn_Wv"]]).T, self_wo_t=f["L1_attn_Wo"].T,
        self_gain_q=f["L1_attn_q_gamma"], self_gain_k=f["L1_attn_k_gamma"], self_angles=angles,
        self_mask=np.where(allowed, 0.0, -1e30).astype(np.float32),
    )
    arrays.update(
        quant_gate=f["L1_ffn_w_gate"], quant_up=f["L1_ffn_w_up"], quant_down=f["L1_ffn_w_down"],
        quant_clip_x=f["L1_ffn_clip_x"], quant_clip_down=f["L1_ffn_clip_down"],
    )
    return {k: np.ascontiguousarray(v) for k, v in arrays.items()}


def program(nc, a, out):
    Memory.semaphores.clear()
    with ExitStack() as stack:
        m = Memory(nc, stack)
        g = Kept(m)
        setup(nc, g, a["x"])
        normalise(nc, g, "ln_a")
        heads_cross_attention(nc, g, a)
        normalise(nc, g, "ln_b", into_x=True)
        with ExitStack() as held:
            reserve_experts(g, Memory(nc, held))
            token_mixer(nc, g, a)
            normalise(nc, g, "ln_c")
            experts(nc, g, a)
        recycle(nc)
        normalise(nc, g, "ln_d")
        wide_cross_attention(nc, g, a)
        normalise(nc, g, "ln_e")
        self_attention(nc, g, a)
        normalise(nc, g, "ln_f")
        quantised_ffn(nc, g, a)
        store(nc, g, out)


def kernel(**inputs):
    import numpy as np
    import concourse.bacc as bacc
    from concourse import mybir as m
    from concourse.bass_utils import run_bass_kernel_spmd

    nc = bacc.Bacc("TRN2", target_bir_lowering=False, num_devices=1)
    arrays = lay_out(inputs)
    a = {n: nc.dram_tensor(f"in_{n}", v.shape, m.dt.from_np(v.dtype), kind="ExternalInput").ap()
                 for n, v in arrays.items()}
    out = nc.dram_tensor("out_x", (B, T, D), m.dt.float32, kind="ExternalOutput").ap()
    program(nc, a, out)
    r = run_bass_kernel_spmd(nc, [{f"in_{n}": v for n, v in arrays.items()}], core_ids=[0])
    return np.asarray(r.results[0]["out_x"])
```

```python
from contextlib import ExitStack

import concourse.bass as bass
from concourse import mybir

ALU = mybir.AluOpType
ACT = mybir.ActivationFunctionType
F32 = mybir.dt.float32
F32R = mybir.dt.float32r
BF16 = mybir.dt.bfloat16
AX_X = mybir.AxisListType.X

P = 128
B, T, D = 32, 64, 256
LK, C = 1601, 128
PAIRS = B // 2
DC = D // P
ROWS = B * T
KT = [(t * P, min(P, LK - t * P)) for t in range((LK + P - 1) // P)]
KFULL = LK // P
KREST = LK - KFULL * P
KGROUPS = [list(range(g, min(g + 4, len(KT)))) for g in range(0, len(KT), 4)]
SCORE_CHUNKS = [(c, min(512, LK - c)) for c in range(0, LK, 512)]
EPS = 1e-5


def at_least(eng, sem, value):
    if isinstance(value, int) and value <= 0:
        return
    eng.wait_ge(sem, value)


class Chain:

    def __init__(self, eng, sem, base=0):
        self.eng, self.sem, self.count = eng, sem, base

    def wait(self):
        at_least(self.eng, self.sem, self.count)

    def step(self, instruction):
        instruction.then_inc(self.sem, 1)
        self.count = self.count + 1
        self.wait()


class Memory:
    semaphores = []

    def __init__(self, nc, stack):
        self.nc, self.stack = nc, stack

    def sb(self, name, shape, dt=F32):
        return self.stack.enter_context(self.nc.sbuf_tensor(name, shape, dt))

    def psum(self, name, shape, dt=F32):
        return self.stack.enter_context(self.nc.psum_tensor(name, shape, dt))

    def sem(self, name):
        sem = self.nc.alloc_semaphore(name)
        Memory.semaphores.append(sem)
        return sem


def recycle(nc):
    nc.clear_and_free_semaphores(Memory.semaphores)
    nc.all_engine_barrier()
    Memory.semaphores.clear()


class Kept:

    def __init__(self, m):
        self.X = m.sb("X", [P, PAIRS, D])
        self.Y = m.sb("Y", [P, PAIRS, D])
        self.YT = m.sb("YT", [P, DC, ROWS])
        self.ident = m.sb("ident", [P, P])
        self.experts_loaded = m.sem("experts_loaded")


def setup(nc, g, x):
    with ExitStack() as stack:
        m = Memory(nc, stack)
        x_loaded, zeroed, built = m.sem("x_loaded"), m.sem("ident_zeroed"), m.sem("ident_built")
        with nc.Block() as block:

            @block.sync
            def _(sp):
                sp.dma_start(g.X[:], x.rearrange("(p b) q d -> (b q) p d", b=2)).then_inc(x_loaded, 16)
                sp.wait_ge(x_loaded, 16)

            @block.gpsimd
            def _(pool):
                nc.gpsimd.memset(g.ident[:], 0.0).then_inc(zeroed, 1)
                pool.wait_ge(zeroed, 1)
                nc.gpsimd.affine_select(out=g.ident[:], in_=g.ident[:], compare_op=ALU.not_equal, fill=1.0,
                                        base=0, pattern=[[-1, P]], channel_multiplier=1).then_inc(built, 1)
                pool.wait_ge(built, 1)


def normalise(nc, g, name, src=None, into_x=False, gain=None, shift=None):
    src = g.X if src is None else src
    with ExitStack() as stack:
        m = Memory(nc, stack)
        stats = m.sb(f"{name}_stats", [P, PAIRS, 6])
        total, dif, square, mean, inner, var, std, rstd = (m.sb(f"{name}_{n}", [P, PAIRS]) for n in
                                                   ("total", "dif", "square", "mean", "inner", "var", "std", "rstd"))
        turned = m.psum(f"{name}_turned", [P, 4, DC, 512])
        stats_done, sums_done, squares_done, var_done, std_done, rstd_done, y_done, x_added, turned_done, stored = (
            m.sem(f"{name}_{n}") for n in ("stats_done", "sums_done", "squares_done", "var_done", "std_done",
                                           "rstd_done", "y_done", "x_added", "turned_done", "stored"))
        with nc.Block() as block:

            @block.vector
            def _(dve):
                with dve.Fori(0, PAIRS) as t:
                    nc.vector.bn_stats(stats[:, t, :], src[:, t, :]).then_inc(stats_done, 1)
                dve.wait_ge(stats_done, PAIRS)
                mean_e, mean_o, var_e, var_o = stats[:, :, 1], stats[:, :, 4], stats[:, :, 2], stats[:, :, 5]
                nc.vector.tensor_tensor(total[:], mean_e, mean_o, ALU.add).then_inc(sums_done, 1)
                nc.vector.tensor_tensor(dif[:], mean_e, mean_o, ALU.subtract).then_inc(sums_done, 1)
                nc.vector.tensor_tensor(inner[:], var_e, var_o, ALU.add).then_inc(sums_done, 1)
                dve.wait_ge(sums_done, 3)
                nc.vector.tensor_scalar(mean[:], total[:], 0.5, None, ALU.mult).then_inc(squares_done, 1)
                nc.vector.tensor_tensor(square[:], dif[:], dif[:], ALU.mult).then_inc(squares_done, 1)
                nc.vector.tensor_scalar(inner[:], inner[:], 1.0 / D, EPS, ALU.mult, ALU.add).then_inc(squares_done, 1)
                dve.wait_ge(squares_done, 3)
                nc.vector.scalar_tensor_tensor(var[:], square[:], 0.25, inner[:], ALU.mult, ALU.add).then_inc(var_done, 1)
                dve.wait_ge(std_done, 1)
                nc.vector.reciprocal(rstd[:], std[:]).then_inc(rstd_done, 1)
                dve.wait_ge(rstd_done, 1)
                with dve.Fori(0, PAIRS) as t:
                    nc.vector.tensor_scalar(g.Y[:, t, :], src[:, t, :], mean[:, bass.ds(t, 1)], rstd[:, bass.ds(t, 1)],
                                            ALU.subtract, ALU.mult).then_inc(y_done, 1)
                if into_x:
                    dve.wait_ge(y_done, PAIRS)
                    nc.vector.tensor_tensor(g.X[:], g.X[:], g.Y[:], ALU.add).then_inc(x_added, 1)

            @block.scalar
            def _(act):
                act.wait_ge(var_done, 1)
                nc.scalar.activation(std[:], var[:], ACT.Sqrt).then_inc(std_done, 1)
                for n in range(4):
                    for c in range(DC):
                        act.wait_ge(turned_done, DC * n + c + 1)
                        out = g.YT[:, c, 512 * n:512 * n + 512]
                        if gain is None:
                            nc.scalar.copy(out, turned[:, n, c, :]).then_inc(stored, 1)
                        else:
                            nc.scalar.activation(out, turned[:, n, c, :], ACT.Identity, bias=shift[:, c:c + 1],
                                                 scale=gain[:, c:c + 1]).then_inc(stored, 1)

            @block.tensor
            def _(pe):
                for n in range(4):
                    pe.wait_ge(y_done, 4 * n + 4)
                    for c in range(DC):
                        for j in range(4):
                            mm = nc.tensor.transpose(turned[:, n, c, P * j:P * j + P],
                                                     g.Y[:, 4 * n + j, P * c:P * c + P], g.ident[:])
                        mm.then_inc(turned_done, 1)


HEADS, HD = 16, D // 16
HEAD_TILES = HEADS // 2
TILES = 2 * HEAD_TILES
QUAD = 4
SCALE0 = HD ** -0.5
LKE = LK + LK % 2
PARTS = [(0, 512), (512, 1024), (1024, LK)]
PART_CHUNKS = [[(c, min(512, (hi + hi % 2) - c)) for c in range(lo, hi, 512)] for lo, hi in PARTS]
NP = len(PARTS)
VALUE_JOBS = (len(KT) + 1) // 2
QK_JOBS = HEADS // 4


def slot_jobs(before, after):
    out = [(r, 2, "inverse") for r in range(QUAD - 1, TILES, QUAD)]
    out += [(r, 2, "gather") for r in range(0 if before else QUAD, TILES, QUAD)]
    if before:
        out.append((2, 2, "wo"))
    if after:
        out.append((1, 3, "q"))
        out += [(r, place, f"qk{k}") for k, (r, place) in enumerate(((5, 3), (6, 3), (8, 3), (10, 2)))]
    places = [((1, 2), (2, 3), (3, 3), (4, 3), (5, 2), (6, 2), (7, 3))]
    if after:
        places.append(((9, 2), (10, 3), (11, 3), (12, 3), (13, 2), (14, 2), (15, 3)))
    for batch in places:
        out += [(r, place, f"v{k}") for k, (r, place) in enumerate(batch)]
    return sorted(out)


def heads_cross_attention(nc, g, a):
    with ExitStack() as stack:
        m = Memory(nc, stack)
        wq_t = m.sb("wq_t", [P, DC, D])
        wk_by_head = m.sb("wk_by_head", [P, HEADS, C])
        wv_t = m.sb("wv_t", [C, D])
        wv_parts = m.sb("wv_parts", [C, 2, D], F32R)
        wo_t = m.sb("wo_t", [P, DC, D])
        ctx_t = m.sb("ctx_t", [C, 2, LKE])
        ctx_parts = m.sb("ctx_parts", [C, 2, 2, LKE], F32R)
        values = m.sb("values", [P, 2, len(KT), D])
        q_t = m.sb("q_t", [P, DC, P])
        qk_next = m.sb("qk_next", [C, 2, HEADS, T])
        qk_parts = m.sb("qk_parts", [C, 2, 2, HEADS, T], F32R)
        part_max = m.sb("part_max", [P, 2, NP])
        neg_max = m.sb("neg_max", [P, 2])
        part_sum = m.sb("part_sum", [P, 2, NP, QUAD])
        row_sum = m.sb("row_sum", [P, QUAD])
        inv_sum = m.sb("inv_sum", [P, QUAD])
        inv_spread = m.sb("inv_spread", [P, QUAD, 2 * HD])
        weight = m.sb("weight", [P, P])
        weighed = m.sb("weighed", [P, P])
        own_head = m.sb("own_head", [P, P])
        zero = m.sb("zero", [P, 1])
        stacked = m.sb("stacked", [P, 2 * HD])
        probs = m.sb("probs", [P, 2, LK])
        probs_t = m.sb("probs_t", [P, len(KT) * P])
        quarters = m.sb("quarters", [P, QUAD, P])
        heads_out_t = m.sb("heads_out_t", [P, DC, P])

        scores = m.psum("scores", [P, 2048])
        turned = m.psum("turned", [P, 2, 512])
        mix = m.psum("mix", [P, 512])
        small = m.psum("small", [P, 512])

        sem = m.sem
        zeroed, weights_loaded, wk_loaded = sem("wk_zeroed"), sem("weights_loaded"), sem("wk_loaded")
        built, wv_split = sem("built"), sem("wv_split")
        ctx_loaded, ctx_split = [sem("ctx_loaded_0"), sem("ctx_loaded_1")], sem("ctx_split")
        scores_ready, part_max_ready, max_ready = sem("scores_ready"), sem("part_max_ready"), sem("max_ready")
        probs_ready, sum_ready = sem("probs_ready"), sem("sum_ready")
        turned_ready, copied_act, copied_dve = sem("turned_ready"), sem("copied_act"), sem("copied_dve")
        mix_ready, quarters_ready = sem("mix_ready"), sem("quarters_ready")
        inv_ready, spread_ready, weighed_ready, heads_ready = sem("inv_ready"), sem("spread_ready"), sem("weighed_ready"), sem("heads_ready")
        small_ready, small_taken = sem("small_ready"), sem("small_taken")
        qk_moved = sem("qk_moved")

        FIRST = ["q"] + [f"qk{k}" for k in range(QK_JOBS)] + [f"v{k}" for k in range(VALUE_JOBS)]
        FULL, EARLY = len(slot_jobs(True, True)), len(slot_jobs(False, True))

        def job_no(p, before, after, job):
            base = len(FIRST) if isinstance(p, int) and p == 0 else (p - 1) * FULL + len(FIRST) + EARLY
            return base + slot_jobs(before, after).index(job)

        LAST_JOB = len(FIRST) + EARLY + (PAIRS - 2) * FULL + len(slot_jobs(True, False))

        def pairs(eng, body):
            body(0, False, True)
            with eng.Fori(1, PAIRS - 1) as p:
                body(p, True, True)
            body(PAIRS - 1, True, False)

        def jobs_at(r, place, before, after):
            return [j for j in slot_jobs(before, after) if j[:2] == (r, place)]

        with nc.Block() as block:

            @block.sync
            def _(sp):
                sp.dma_start(wq_t[:], a["wq_t"].rearrange("(c p) n -> p c n", p=P)).then_inc(weights_loaded, 16)
                sp.dma_start(wv_t[:], a["wv_t"]).then_inc(weights_loaded, 16)
                sp.dma_start(wo_t[:], a["wo_t"].rearrange("(c p) n -> p c n", p=P)).then_inc(weights_loaded, 16)
                sp.dma_start(own_head[:], a["own_head"]).then_inc(weights_loaded, 16)
                sp.wait_ge(zeroed, 2)

                def load(p, before):
                    for b in range(2):
                        if before:
                            sp.wait_ge(ctx_split, 4 * (p - 1) + 2 * b + 2)
                        sp.dma_start(ctx_t[:, b, 0:LK], a["ctx_t"][2 * p + b]).then_inc(ctx_loaded[b], 16)

                load(0, False)
                for h in range(HEADS):
                    r = HD * (h % 8)
                    sp.dma_start(wk_by_head[r:r + HD, h, :], a["wkv"][HD * h:HD * h + HD, :]).then_inc(wk_loaded, 16)
                with sp.Fori(1, PAIRS) as p:
                    load(p, True)

            @block.gpsimd
            def _(pool):
                nc.gpsimd.memset(wk_by_head[:], 0.0).then_inc(zeroed, 1)
                nc.gpsimd.memset(ctx_t[:, :, LK:LKE], 0.0).then_inc(zeroed, 1)
                nc.gpsimd.memset(zero[:], 0.0).then_inc(zeroed, 1)
                nc.gpsimd.tensor_tensor(stacked[:], g.ident[:, 0:32], g.ident[:, 32:64], ALU.add).then_inc(built, 1)
                for c in (2, 3):
                    pool.wait_ge(built, c - 1)
                    nc.gpsimd.tensor_tensor(stacked[:], stacked[:], g.ident[:, 32 * c:32 * c + 32], ALU.add).then_inc(built, 1)
                pool.wait_ge(zeroed, 3)

                def split(p, b, before):
                    pool.wait_ge(ctx_loaded[b], 16 * (p + 1))
                    if before:
                        pool.wait_ge(scores_ready, NP * TILES * (p - 1) + NP * HEAD_TILES * (b + 1))
                    nc.gpsimd.tensor_tensor(ctx_parts[:, b, 0, :], ctx_t[:, b, :], zero[:].to_broadcast([P, LKE]), ALU.add)\
                        .then_inc(ctx_split, 1)
                    pool.wait_ge(ctx_split, 4 * p + 2 * b + 1)
                    nc.gpsimd.tensor_tensor(ctx_parts[:, b, 1, :], ctx_t[:, b, :], ctx_parts[:, b, 0, :].bitcast(F32),
                                            ALU.subtract).then_inc(ctx_split, 1)

                def move(p, b):
                    nc.gpsimd.tensor_tensor(qk_parts[:, b, 0], qk_next[:, b],
                                            zero[:].unsqueeze(2).to_broadcast([P, HEADS, T]), ALU.add).then_inc(qk_moved, 1)
                    pool.wait_ge(qk_moved, 4 * p + 2 * b + 1)
                    nc.gpsimd.tensor_tensor(qk_parts[:, b, 1], qk_next[:, b], qk_parts[:, b, 0].bitcast(F32), ALU.subtract)\
                        .then_inc(qk_moved, 1)

                split(0, 0, False)
                split(0, 1, False)
                pool.wait_ge(small_taken, 1 + QK_JOBS)
                move(0, 0)
                move(0, 1)

                def body(p, before):
                    split(p + 1, 0, True)
                    pool.wait_ge(small_taken, job_no(p, before, True, (10, 2, "qk3")) + 1)
                    move(p + 1, 0)
                    split(p + 1, 1, True)
                    move(p + 1, 1)

                body(0, False)
                with pool.Fori(1, PAIRS - 1) as p:
                    body(p, True)

            @block.tensor
            def _(pe):
                def three_products(out, left, right):
                    for k, (x, y) in enumerate(((0, 0), (0, 1), (1, 0))):
                        mm = nc.tensor.matmul(out, left(x), right(y), start=(k == 0), stop=(k == 2))
                    return mm

                def q_product(p):
                    for oc in range(DC):
                        for c in range(DC):
                            mm = nc.tensor.matmul(small[:, P * oc:P * oc + P], wq_t[:, c, P * oc:P * oc + P],
                                                  g.YT[:, c, bass.ds(P * p, P)], start=(c == 0), stop=(c == DC - 1))
                    return mm

                def qk_product(n):
                    for h in range(4 * n, 4 * n + 4):
                        mm = nc.tensor.matmul(small[:, P * (h % 4):P * (h % 4) + P], wk_by_head[:, h, :],
                                              q_t[:, h // 8, :], start=True, stop=True)
                    return mm

                def v_product(b, k):
                    for t in range(2 * k, min(2 * k + 2, len(KT))):
                        lo, n = KT[t]
                        out = D * (t % 2)
                        mm = three_products(small[0:n, out:out + D], lambda x: ctx_parts[:, b, x, lo:lo + n],
                                            lambda y: wv_parts[:, y, :])
                    return mm

                def gather():
                    for j in range(QUAD):
                        q = 2 * HD * j
                        mm = nc.tensor.matmul(small[q:q + 2 * HD, 0:P], stacked[:], quarters[:, j, :], start=True, stop=True)
                    return mm

                def wo_product():
                    for c in range(DC):
                        mm = nc.tensor.matmul(small[:, 0:D], heads_out_t[:, c, :], wo_t[:, c, :],
                                              start=(c == 0), stop=(c == DC - 1))
                    return mm

                def score_part(b, j, part):
                    for lo, n in PART_CHUNKS[part]:
                        mm = three_products(scores[:, lo:lo + n], lambda x: qk_parts[:, b, x, 2 * j:2 * j + 2, :],
                                            lambda y: ctx_parts[:, b, y, lo:lo + n])
                    mm.then_inc(scores_ready, 1)

                def weigh(row, tile, k):
                    if k < 2:
                        pe.wait_ge(copied_act, 2 * row + k + 1)
                    else:
                        pe.wait_ge(copied_dve, 2 * row + k - 1)
                    b, heads = tile // HEAD_TILES, 2 * HD * (tile % HEAD_TILES)
                    for t in KGROUPS[k]:
                        n, q = KT[t][1], 2 * HD * (t % 4)
                        mm = nc.tensor.matmul(mix[q:q + 2 * HD, 0:P], values[0:n, b, t, heads:heads + 2 * HD],
                                              probs_t[0:n, P * t:P * t + P], start=(t < 4), stop=(t + 4 >= len(KT)))
                    if k == len(KGROUPS) - 1:
                        mm.then_inc(mix_ready, 1)

                def body(p, before, after):
                    def run(r, place):
                        for job in jobs_at(r, place, before, after):
                            name = job[2]
                            pe.wait_ge(small_taken, job_no(p, before, after, job))
                            if name == "gather":
                                pe.wait_ge(quarters_ready, TILES * p + r)
                                mm = gather()
                            elif name == "inverse":
                                pe.wait_ge(spread_ready, (TILES // QUAD) * p + r // QUAD + 1)
                                mm = nc.tensor.transpose(small[:, 0:P], inv_spread[:].rearrange("p j d -> p (j d)"), g.ident[:])
                            elif name == "wo":
                                pe.wait_ge(heads_ready, (TILES // QUAD) * p)
                                mm = wo_product()
                            elif name == "q":
                                mm = q_product(p + 1)
                            elif name[0] == "q":
                                mm = qk_product(int(name[2:]))
                            else:
                                k = int(name[1:])
                                if k == 0:
                                    pe.wait_ge(ctx_split, 4 * p + (4 if r < HEAD_TILES else 6))
                                mm = v_product(1 if r < HEAD_TILES else 0, k)
                            mm.then_inc(small_ready, 1)

                    for r in range(TILES):
                        row = TILES * p + r
                        b = r // HEAD_TILES

                        def next_scores(part):
                            pe.wait_ge(probs_ready, NP * row + part + 1)
                            if r + 1 < TILES or after:
                                nxt = (r + 1) % TILES
                                if part == 0 and nxt == HEAD_TILES:
                                    pe.wait_ge(qk_moved, 4 * p + 4)
                                if part == 0 and nxt == 0:
                                    pe.wait_ge(qk_moved, 4 * p + 6)
                                score_part(nxt // HEAD_TILES, nxt % HEAD_TILES, part)

                        def turn(k):
                            if k >= 2:
                                pe.wait_ge(copied_act, 2 * row + k - 1)
                            elif r > 0 or before:
                                pe.wait_ge(copied_dve, 2 * row + k - 1)
                            for t in KGROUPS[k]:
                                lo, n = KT[t]
                                mm = nc.tensor.transpose(turned[0:n, k % 2, P * (t % 4):P * (t % 4) + P],
                                                         probs[:, r % 2, lo:lo + n], g.ident[:])
                            mm.then_inc(turned_ready, 1)

                        for part in range(NP):
                            next_scores(part)
                        turn(0)
                        if r > 0 or before:
                            weigh(row - 1, (r - 1) % TILES, 2)
                            weigh(row - 1, (r - 1) % TILES, 3)
                        turn(1)
                        run(r, 2)
                        turn(2)
                        if r > 0 or before:
                            pe.wait_ge(quarters_ready, row)
                        weigh(row, r, 0)
                        weigh(row, r, 1)
                        turn(3)
                        run(r, 3)

                pe.wait_ge(weights_loaded, 64)
                pe.wait_ge(wk_loaded, 16 * HEADS)
                pe.wait_ge(built, 3)
                pe.wait_ge(wv_split, 2)
                for k, n in enumerate(FIRST):
                    at_least(pe, small_taken, k)
                    if n == "v0":
                        pe.wait_ge(ctx_split, 2)
                    (q_product(0) if n == "q" else qk_product(int(n[2:])) if n[0] == "q" else v_product(0, int(n[1:])))\
                        .then_inc(small_ready, 1)
                pe.wait_ge(qk_moved, 2)
                for part in range(NP):
                    score_part(0, 0, part)
                pairs(pe, body)
                weigh(TILES * PAIRS - 1, TILES - 1, 2)
                weigh(TILES * PAIRS - 1, TILES - 1, 3)
                pe.wait_ge(quarters_ready, TILES * PAIRS)
                pe.wait_ge(small_taken, LAST_JOB)
                gather().then_inc(small_ready, 1)
                pe.wait_ge(small_taken, LAST_JOB + 1)
                pe.wait_ge(heads_ready, (TILES // QUAD) * PAIRS)
                wo_product().then_inc(small_ready, 1)

            @block.scalar
            def _(act):
                def take(job, name, b):
                    act.wait_ge(small_ready, job + 1)
                    scale = 1.0
                    if name == "q":
                        out, src, scale = q_t[:], small[:, 0:D].rearrange("p (c n) -> p c n", c=DC), SCALE0
                    elif name[0] == "q":
                        h = 4 * int(name[2:])
                        out = qk_next[:, :, h:h + 4, :]
                        src = small[:].rearrange("p (h b q) -> p b h q", h=4, b=2)
                    else:
                        t = 2 * int(name[1:])
                        tiles = min(2, len(KT) - t)
                        n = KT[t][1]
                        out, src = values[0:n, b, t:t + tiles, :], small[0:n, 0:D * tiles].rearrange("p (t d) -> p t d", t=tiles)
                    nc.scalar.activation(out, src, ACT.Copy, scale=scale).then_inc(small_taken, 1)

                def exp(tile, row, part):
                    act.wait_ge(max_ready, row + 1)
                    k, (lo, hi) = tile % (2 * QUAD), PARTS[part]
                    nc.scalar.activation(probs[:, tile % 2, lo:hi], scores[:, lo:hi], ACT.Exp,
                                         bias=neg_max[:, tile % 2:tile % 2 + 1], scale=1.0,
                                         accum_out=part_sum[:, k // QUAD, part, k % QUAD:k % QUAD + 1]).then_inc(probs_ready, 1)

                def body(p, before, after):
                    def run(r, place):
                        for job in jobs_at(r, place, before, after):
                            if job[2] in ("gather", "inverse", "wo"):
                                continue
                            if job[2] == "qk0":
                                act.wait_ge(qk_moved, 4 * p + 4)
                            take(job_no(p, before, after, job), job[2], 1 if r < HEAD_TILES else 0)

                    for r in range(TILES):
                        row = TILES * p + r
                        for k in range(2):
                            act.wait_ge(turned_ready, 4 * row + k + 1)
                            nc.scalar.copy(probs_t[:, 512 * k:512 * k + 512], turned[:, k, :]).then_inc(copied_act, 1)
                        if r + 1 < TILES or after:
                            exp((r + 1) % TILES, row + 1, 0)
                        run(r, 2)
                        if r + 1 < TILES or after:
                            exp((r + 1) % TILES, row + 1, 1)
                            exp((r + 1) % TILES, row + 1, 2)
                        run(r, 3)

                act.preload_act_table(ACT.Exp)
                for k, n in enumerate(FIRST):
                    take(k, n, 0)
                for part in range(NP):
                    exp(0, 0, part)
                pairs(act, body)

            @block.vector
            def _(dve):
                def part_row_max(tile, row, part):
                    lo, hi = PARTS[part]
                    dve.wait_ge(scores_ready, NP * row + part + 1)
                    nc.vector.tensor_reduce(part_max[:, tile % 2, part:part + 1], scores[:, lo:hi], AX_X, ALU.max)\
                        .then_inc(part_max_ready, 1)

                def row_max(tile, row):
                    dve.wait_ge(part_max_ready, NP * (row + 1))
                    nc.vector.tensor_reduce(neg_max[:, tile % 2:tile % 2 + 1], part_max[:, tile % 2, :], AX_X, ALU.max,
                                            negate=True).then_inc(max_ready, 1)

                def finish_quad(job, tile):
                    dve.wait_ge(small_ready, job + 1)
                    nc.vector.tensor_tensor(weighed[:], small[:, 0:P], weight[:], ALU.mult).then_inc(small_taken, 1)
                    dve.wait_ge(small_taken, job + 1)
                    b, c = tile // HEAD_TILES, (tile // QUAD) % 2
                    nc.vector.tensor_tensor(heads_out_t[:, c, T * b:T * b + T], weighed[:, 0:T], weighed[:, T:2 * T], ALU.add)\
                        .then_inc(heads_ready, 1)

                def take_quarters(rows, tile):
                    dve.wait_ge(mix_ready, rows)
                    nc.vector.tensor_copy(quarters[:, tile % QUAD, :], mix[:, 0:P]).then_inc(quarters_ready, 1)

                def take_turned(row, k):
                    dve.wait_ge(turned_ready, 4 * row + k + 1)
                    n, w = KT[KGROUPS[k][-1]][1], P * len(KGROUPS[k])
                    nc.vector.tensor_copy(probs_t[0:n, 512 * k:512 * k + w], turned[0:n, k % 2, 0:w]).then_inc(copied_dve, 1)

                def add_to_x(job, p):
                    dve.wait_ge(small_ready, job + 1)
                    nc.vector.tensor_tensor(g.X[:, p, :], g.X[:, p, :], small[:, 0:D], ALU.add).then_inc(small_taken, 1)

                def body(p, before, after):
                    for r in range(TILES):
                        row = TILES * p + r
                        quad = (TILES // QUAD) * p + r // QUAD
                        if r % QUAD == QUAD - 1:
                            dve.wait_ge(probs_ready, NP * (row + 1))
                            k = (r // QUAD) % 2
                            nc.vector.tensor_reduce(row_sum[:], part_sum[:, k].rearrange("p n q -> p q n"), AX_X, ALU.add)\
                                .then_inc(sum_ready, 1)
                            dve.wait_ge(sum_ready, quad + 1)
                            nc.vector.reciprocal(inv_sum[:], row_sum[:]).then_inc(inv_ready, 1)
                            dve.wait_ge(inv_ready, quad + 1)
                            nc.vector.tensor_copy(inv_spread[:], inv_sum[:].unsqueeze(2).to_broadcast([P, QUAD, 2 * HD]))\
                                .then_inc(spread_ready, 1)
                        if r + 1 < TILES or after:
                            for part in range(NP):
                                part_row_max((r + 1) % TILES, row + 1, part)
                        if r > 0 or before:
                            take_quarters(row, (r - 1) % TILES)
                        if r + 1 < TILES or after:
                            row_max((r + 1) % TILES, row + 1)
                        if r % QUAD == 0 and (r > 0 or before):
                            finish_quad(job_no(p, before, after, (r, 2, "gather")), (r - 1) % TILES)
                        if before and r == 2:
                            add_to_x(job_no(p, before, after, (2, 2, "wo")), p - 1)
                        take_turned(row, 2)
                        if r % QUAD == QUAD - 1:
                            inverse = job_no(p, before, after, (r, 2, "inverse"))
                            dve.wait_ge(small_ready, inverse + 1)
                            nc.vector.tensor_tensor(weight[:], small[:, 0:P], own_head[:], ALU.mult).then_inc(small_taken, 1)
                            dve.wait_ge(small_taken, inverse + 1)
                        take_turned(row, 3)

                dve.wait_ge(weights_loaded, 64)
                nc.vector.tensor_copy(wv_parts[:, 0, :], wv_t[:]).then_inc(wv_split, 1)
                dve.wait_ge(wv_split, 1)
                nc.vector.tensor_tensor(wv_parts[:, 1, :], wv_t[:], wv_parts[:, 0, :].bitcast(F32), ALU.subtract).then_inc(wv_split, 1)
                for part in range(NP):
                    part_row_max(0, 0, part)
                row_max(0, 0)
                pairs(dve, body)
                take_quarters(TILES * PAIRS, TILES - 1)
                finish_quad(LAST_JOB, TILES - 1)
                add_to_x(LAST_JOB + 1, PAIRS - 1)


GROUP = 512
GROUPS = ROWS // GROUP
ROUND = 12582912.0
TWO_PI = 6.2831845
TURN = 0.15915494309189535
BK, BV, BQ, BKP, BQP, PHASE, GAIN, SHIFT = range(8)


def token_mixer(nc, g, a):
    with ExitStack() as stack:
        m = Memory(nc, stack)
        columns = m.sb("mix_columns", [P, 8, DC])
        wo = m.sb("mix_wo", [P, DC, D])
        bo = m.sb("mix_bo", [P, D])
        retrieve(nc, g, a, columns, wo, bo)
        normalise(nc, g, "ln_r", src=g.Y, gain=columns[:, GAIN], shift=columns[:, SHIFT])
        with ExitStack() as inner:
            n = Memory(nc, inner)
            product = n.psum("mix_product", [P, 2, 512])
            product_done, product_added = n.sem("mix_product_done"), n.sem("mix_product_added")
            with nc.Block() as block:

                @block.tensor
                def _(pe):
                    for t in range(PAIRS):
                        at_least(pe, product_added, t - 1)
                        for c in range(DC):
                            mm = nc.tensor.matmul(product[:, t % 2, 0:D], g.YT[:, c, P * t:P * t + P], wo[:, c, :],
                                                  start=(c == 0), stop=(c == DC - 1))
                        mm.then_inc(product_done, 1)

                @block.vector
                def _(dve):
                    for t in range(PAIRS):
                        dve.wait_ge(product_done, t + 1)
                        nc.vector.tensor_tensor(g.X[:, t, :], g.X[:, t, :], product[:, t % 2, 0:D],
                                                ALU.add).then_inc(product_added, 1)


def retrieve(nc, g, a, columns, wo, bo):
    with ExitStack() as stack:
        m = Memory(nc, stack)
        w = {n: m.sb(f"mix_{n}", [P, DC, D]) for n in ("wk", "wv", "wq", "wkp", "wqp")}
        key, value, query, turn_k, turn_q = (m.sb(f"mix_{n}", [P, DC, GROUP]) for n in
                                             ("key", "value", "query", "turn_k", "turn_q"))
        wave = {n: m.sb(f"mix_{n}", [P, DC, GROUP]) for n in ("cos_k", "sin_k", "cos_q", "sin_q")}
        whole = m.sb("mix_whole", [P, DC, GROUP])
        bound = m.sb("mix_bound", [P, DC, GROUP])
        memory = [m.sb("mix_memory_re", [P, DC, GROUP]), m.sb("mix_memory_im", [P, DC, GROUP])]
        retrieved = m.sb("mix_retrieved", [P, DC, GROUP])
        keep = m.sb("mix_keep", [P, GROUP])
        per_turn = m.sb("mix_per_turn", [P, DC])
        ps_k, ps_v, ps_q = (m.psum(f"mix_ps_{n}", [P, DC, 512]) for n in "kvq")
        ps_r = m.psum("mix_ps_r", [P, 2, 512])
        sem = m.sem
        weights, bo_loaded, bo_added = sem("mix_weights"), sem("mix_bo_loaded"), sem("mix_bo_added")
        made_k, made_q, made_v = sem("mix_made_k"), sem("mix_made_q"), sem("mix_made_v")
        made_kp, made_qp = sem("mix_made_kp"), sem("mix_made_qp")
        took_k, took_q, took_v, tanh_done = sem("mix_took_k"), sem("mix_took_q"), sem("mix_took_v"), sem("mix_tanh_done")
        angle_done, wave_done, step, retrieved_done = sem("mix_angle_done"), sem("mix_wave_done"), sem("mix_step"), sem("mix_retrieved_done")
        rows_turned, rows_stored = sem("mix_rows_turned"), sem("mix_rows_stored")
        SETUP, STEPS = 3, 4 * (DC + 1) + 2 * (1 + DC) + 2

        def groups(eng, body):
            body(0, True)
            with eng.Fori(1, GROUPS) as n:
                body(n, False)

        with nc.Block() as block:

            @block.sync
            def _(sp):
                sp.dma_start(columns[:], a["mix_columns"]).then_inc(weights, 16)
                for n, src in (("wk", a["mix_wk"]), ("wv", a["mix_wv"]), ("wq", a["mix_wq"]), ("wkp", a["mix_wkp"]), ("wqp", a["mix_wqp"])):
                    sp.dma_start(w[n][:], src.rearrange("(c p) n -> p c n", p=P)).then_inc(weights, 16)
                sp.dma_start(wo[:], a["mix_wo"].rearrange("(c p) n -> p c n", p=P)).then_inc(weights, 16)
                sp.dma_start(bo[:], a["mix_bo"].partition_broadcast(P)).then_inc(bo_loaded, 16)
                load_experts(sp, g, a)

            @block.gpsimd
            def _(pool):
                pool.wait_ge(bo_loaded, 16)
                nc.gpsimd.tensor_tensor(g.X[:], g.X[:], bo[:].unsqueeze(1).to_broadcast([P, PAIRS, D]),
                                        ALU.add).then_inc(bo_added, 1)

            @block.tensor
            def _(pe):
                def project(out, weight, moving, done):
                    for oc in range(DC):
                        for c in range(DC):
                            mm = nc.tensor.matmul(out[:, oc, :], weight[:, c, P * oc:P * oc + P], moving(c),
                                                  start=(c == 0), stop=(c == DC - 1))
                    mm.then_inc(done, 1)

                def turn_rows(n):
                    pe.wait_ge(retrieved_done, n + 1)
                    for j in range(4):
                        for c in range(DC):
                            mm = nc.tensor.transpose(ps_r[:, j // 2, D * (j % 2) + P * c:D * (j % 2) + P * c + P],
                                                     retrieved[:, c, P * j:P * j + P], g.ident[:])
                        if j % 2:
                            mm.then_inc(rows_turned, 1)

                def body(n, first):
                    y = lambda c: g.YT[:, c, bass.ds(GROUP * n, GROUP)]
                    if not first:
                        pe.wait_ge(tanh_done, 2 * n)
                        pe.wait_ge(took_v, n)
                    project(ps_k, w["wk"], y, made_k)
                    project(ps_q, w["wq"], y, made_q)
                    project(ps_v, w["wv"], y, made_v)
                    pe.wait_ge(took_k, n + 1)
                    project(ps_k, w["wkp"], lambda c: key[:, c, :], made_kp)
                    pe.wait_ge(took_q, n + 1)
                    project(ps_q, w["wqp"], lambda c: query[:, c, :], made_qp)
                    if not first:
                        turn_rows(n - 1)

                pe.wait_ge(weights, 16 * 7)
                groups(pe, body)
                turn_rows(GROUPS - 1)

            @block.scalar
            def _(act):
                def take(made, n, src, dst, row, func, done):
                    act.wait_ge(made, n + 1)
                    for c in range(DC):
                        ins = nc.scalar.activation(dst[:, c, :], src[:, c, :], func, bias=columns[:, row, c:c + 1], scale=1.0)
                    ins.then_inc(done, 1)

                def body(n, first):
                    take(made_k, n, ps_k, key, BK, ACT.Identity, took_k)
                    take(made_q, n, ps_q, query, BQ, ACT.Identity, took_q)
                    if not first:
                        act.wait_ge(retrieved_done, n)
                    take(made_v, n, ps_v, value, BV, ACT.Identity, took_v)
                    take(made_kp, n, ps_k, turn_k, BKP, ACT.Tanh, tanh_done)
                    take(made_qp, n, ps_q, turn_q, BQP, ACT.Tanh, tanh_done)
                    for k, name in enumerate(wave):
                        act.wait_ge(angle_done, 4 * n + k + 1)
                        nc.scalar.activation(wave[name][:], wave[name][:], ACT.Sin, scale=TWO_PI).then_inc(wave_done, 1)

                act.preload_act_table(ACT.Silu)
                act.wait_ge(weights, 16 * 7)
                groups(act, body)

            @block.vector
            def _(dve):
                chain = Chain(dve, step)
                chain.step(nc.vector.memset(keep[:], 1.0))
                chain.step(nc.vector.memset(keep[:].rearrange("p (b q) -> p b q", q=T)[:, :, 0:1], 0.0))
                dve.wait_ge(weights, 16 * 7)
                chain.step(nc.vector.tensor_scalar(per_turn[:], columns[:, PHASE, :], TURN, None, ALU.mult))

                def store_rows(n):
                    for j in range(2):
                        dve.wait_ge(rows_turned, 2 * n + j + 1)
                        nc.vector.tensor_scalar(g.Y[:, bass.ds(4 * n + 2 * j, 2), :],
                                                ps_r[:, j, :].rearrange("p (t d) -> p t d", t=2), D ** -0.5, None,
                                                ALU.mult).then_inc(rows_stored, 1)

                def body(n, first):
                    chain = Chain(dve, step, SETUP + STEPS * n)
                    for k, (name, turn) in enumerate(zip(wave, (turn_k, turn_k, turn_q, turn_q))):
                        if k % 2 == 0:
                            dve.wait_ge(tanh_done, 2 * n + k // 2 + 1)
                        for c in range(DC):
                            chain.step(nc.vector.tensor_scalar(wave[name][:, c, :], turn[:, c, :], per_turn[:, c:c + 1],
                                                               0.25 if name.startswith("cos") else 0.0, ALU.mult, ALU.add))
                        chain.step(nc.vector.tensor_scalar(whole[:], wave[name][:], ROUND, ROUND, ALU.add, ALU.subtract))
                        nc.vector.tensor_tensor(wave[name][:], wave[name][:], whole[:], ALU.subtract).then_inc(angle_done, 1)
                        dve.wait_ge(angle_done, 4 * n + k + 1)
                    if not first:
                        store_rows(n - 1)
                    dve.wait_ge(took_v, n + 1)
                    for k, name in enumerate(("cos_k", "sin_k")):
                        dve.wait_ge(wave_done, 4 * n + k + 1)
                        chain.step(nc.vector.tensor_tensor(bound[:], value[:], wave[name][:], ALU.mult))
                        for c in range(DC):
                            chain.step(nc.vector.tensor_tensor_scan(memory[k][:, c, :], keep[:], bound[:, c, :], 0.0,
                                                                    ALU.mult, ALU.add))
                    for k, name in enumerate(("cos_q", "sin_q")):
                        dve.wait_ge(wave_done, 4 * n + k + 3)
                        chain.step(nc.vector.tensor_tensor(memory[k][:], memory[k][:], wave[name][:], ALU.mult))
                    nc.vector.tensor_tensor(retrieved[:], memory[0][:], memory[1][:], ALU.add).then_inc(retrieved_done, 1)
                    dve.wait_ge(retrieved_done, n + 1)

                groups(dve, body)
                store_rows(GROUPS - 1)


E, H = 8, 2 * D
HC = H // P


def reserve_experts(g, m):
    g.w1, g.w2 = m.sb("expert_w1", [P, E, DC, H]), m.sb("expert_w2", [P, E, HC, D])
    g.b1, g.b2 = m.sb("expert_b1", [P, E, HC]), m.sb("expert_b2", [E, D])
    g.wr, g.br = m.sb("router_w", [P, DC, E]), m.sb("router_b", [P, E])
    g.share, g.share_t = m.sb("share", [P, PAIRS, E]), m.sb("share_t", [E, ROWS])


def load_experts(sp, g, a):
    sp.dma_start(g.w1[:], a["expert_w1"].rearrange("e (c p) d -> p e c d", p=P)).then_inc(g.experts_loaded, 16)
    sp.dma_start(g.w2[:], a["expert_w2"].rearrange("e (c p) d -> p e c d", p=P)).then_inc(g.experts_loaded, 16)
    sp.dma_start(g.b1[:], a["expert_b1"]).then_inc(g.experts_loaded, 16)
    sp.dma_start(g.b2[:], a["expert_b2"]).then_inc(g.experts_loaded, 16)
    sp.dma_start(g.wr[:], a["router_w"].rearrange("(c p) e -> p c e", p=P)).then_inc(g.experts_loaded, 16)
    sp.dma_start(g.br[:], a["router_b"].partition_broadcast(P)).then_inc(g.experts_loaded, 16)


def route(nc, g):
    with ExitStack() as stack:
        m = Memory(nc, stack)
        logits, probs, top, order, rank, chosen, rest = (m.sb(f"route_{n}", [P, PAIRS, E]) for n in
                                                         ("logits", "probs", "top", "order", "rank", "chosen", "rest"))
        best, total = m.sb("route_best", [P, PAIRS]), m.sb("route_total", [P, PAIRS])
        ps = m.psum("route_ps", [P, PAIRS, E])
        ps_t = m.psum("route_ps_t", [P, 4, 512])
        made, step, shifted, exp_done, share_done, turned, stored, order_done = (
            m.sem(f"route_{n}") for n in ("made", "step", "shifted", "exp_done", "share_done", "turned", "stored", "order_done"))

        def by_row(column):
            return column[:].unsqueeze(2).to_broadcast([P, PAIRS, E])

        with nc.Block() as block:

            @block.gpsimd
            def _(pool):
                nc.gpsimd.iota(order[:], pattern=[[0, PAIRS], [-1, E]], base=E, channel_multiplier=0,
                               allow_small_or_imprecise_dtypes=True).then_inc(order_done, 1)

            @block.tensor
            def _(pe):
                pe.wait_ge(g.experts_loaded, 96)
                for t in range(PAIRS):
                    for c in range(DC):
                        mm = nc.tensor.matmul(ps[:, t, :], g.YT[:, c, P * t:P * t + P], g.wr[:, c, :],
                                              start=(c == 0), stop=(c == DC - 1))
                mm.then_inc(made, 1)
                pe.wait_ge(share_done, 1)
                for t in range(PAIRS):
                    mm = nc.tensor.transpose(ps_t[0:E, t // 4, P * (t % 4):P * (t % 4) + P], g.share[:, t, :], g.ident[:])
                mm.then_inc(turned, 1)

            @block.scalar
            def _(act):
                act.wait_ge(shifted, 1)
                nc.scalar.activation(probs[:], logits[:], ACT.Exp).then_inc(exp_done, 1)
                act.wait_ge(turned, 1)
                nc.scalar.copy(g.share_t[:].rearrange("p (n r) -> p n r", n=4), ps_t[0:E, :, :]).then_inc(stored, 1)

            @block.vector
            def _(dve):
                chain = Chain(dve, step)
                tt, link = nc.vector.tensor_tensor, chain.step
                dve.wait_ge(made, 1)
                link(tt(logits[:], ps[:], g.br[:].unsqueeze(1).to_broadcast([P, PAIRS, E]), ALU.add))
                link(nc.vector.tensor_reduce(best[:], logits[:], AX_X, ALU.max))
                tt(logits[:], logits[:], by_row(best), ALU.subtract).then_inc(shifted, 1)
                dve.wait_ge(exp_done, 1)
                link(nc.vector.tensor_reduce(total[:], probs[:], AX_X, ALU.add))
                link(nc.vector.reciprocal(total[:], total[:]))
                link(tt(probs[:], probs[:], by_row(total), ALU.mult))
                dve.wait_ge(order_done, 1)
                for n, left in enumerate((probs, rest)):
                    pick = chosen if n == 0 else top
                    link(nc.vector.tensor_reduce(best[:], left[:], AX_X, ALU.max))
                    link(tt(rank[:], left[:], by_row(best), ALU.is_equal))
                    link(tt(rank[:], rank[:], order[:], ALU.mult))
                    link(nc.vector.tensor_reduce(best[:], rank[:], AX_X, ALU.max))
                    link(tt(pick[:], rank[:], by_row(best), ALU.is_equal))
                    if n == 0:
                        link(nc.vector.scalar_tensor_tensor(rest[:], pick[:], -2.0, probs[:], ALU.mult, ALU.add))
                link(tt(chosen[:], chosen[:], top[:], ALU.add))
                tt(g.share[:], probs[:], chosen[:], ALU.mult).then_inc(share_done, 1)


def experts(nc, g, a):
    route(nc, g)
    with ExitStack() as stack:
        m = Memory(nc, stack)
        hidden = m.sb("hidden", [P, 2, HC, GROUP])
        ps_h = m.psum("expert_ps_h", [P, HC, 512])
        ps_y = m.psum("expert_ps_y", [P, 4, 512])
        made_h, took_h, made_y, added_y, biased = (m.sem(f"expert_{n}") for n in
                                                   ("made_h", "took_h", "made_y", "added_y", "biased"))

        def steps(eng, body):
            body(0, True)
            with eng.Fori(1, GROUPS) as n:
                body(n, False)

        with nc.Block() as block:

            @block.tensor
            def _(pe):
                def first_product(n, e):
                    s = E * n + e
                    for h in range(HC):
                        at_least(pe, took_h, HC * (s - 1) + h + 1)
                        for c in range(DC):
                            mm = nc.tensor.matmul(ps_h[:, h, :], g.w1[:, e, c, P * h:P * h + P],
                                                  g.YT[:, c, bass.ds(GROUP * n, GROUP)], start=(c == 0), stop=(c == DC - 1))
                        mm.then_inc(made_h, 1)

                def second_product(s, e):
                    pe.wait_ge(took_h, HC * (s + 1))
                    for j in range(4):
                        at_least(pe, added_y, 4 * (s - 1) + j + 1)
                        for h in range(HC):
                            mm = nc.tensor.matmul(ps_y[:, j, 0:D], hidden[:, e % 2, h, P * j:P * j + P], g.w2[:, e, h, :],
                                                  start=(h == 0), stop=(h == HC - 1))
                        mm.then_inc(made_y, 1)

                def body(n, first):
                    for e in range(E):
                        first_product(n, e)
                        if e > 0 or not first:
                            second_product(E * n + e - 1, (e - 1) % E)

                for t in range(PAIRS):
                    at_least(pe, biased, t - 3)
                    nc.tensor.matmul(ps_y[:, t % 4, 0:D], g.share_t[:, P * t:P * t + P], g.b2[:],
                                     start=True, stop=True).then_inc(made_y, 1)
                pe.wait_ge(biased, PAIRS)
                steps(pe, body)
                second_product(E * GROUPS - 1, E - 1)

            @block.scalar
            def _(act):
                def body(n, first):
                    for e in range(E):
                        for h in range(HC):
                            act.wait_ge(made_h, HC * (E * n + e) + h + 1)
                            nc.scalar.activation(hidden[:, e % 2, h, :], ps_h[:, h, :], ACT.Relu,
                                                 bias=g.b1[:, e, h:h + 1], scale=1.0).then_inc(took_h, 1)

                act.preload_act_table(ACT.Relu)
                steps(act, body)

            @block.vector
            def _(dve):
                def add(s, n, e):
                    for j in range(4):
                        t = 4 * n + j
                        dve.wait_ge(made_y, PAIRS + 4 * s + j + 1)
                        nc.vector.scalar_tensor_tensor(g.X[:, t, :], ps_y[:, j, 0:D], g.share[:, t, e:e + 1],
                                                       g.X[:, t, :], ALU.mult, ALU.add).then_inc(added_y, 1)

                for t in range(PAIRS):
                    dve.wait_ge(made_y, t + 1)
                    nc.vector.tensor_tensor(g.X[:, t, :], g.X[:, t, :], ps_y[:, t % 4, 0:D], ALU.add).then_inc(biased, 1)
                with dve.Fori(0, GROUPS) as n:
                    for e in range(E):
                        add(E * n + e, n, e)


def wide_queries(nc, g, a, wq, bq, wk_t, bk, qk_all, shift):
    with ExitStack() as stack:
        m = Memory(nc, stack)
        q_t = m.sb("wide_q_t", [P, DC, ROWS])
        bv = m.sb("wide_bv", [P, D])
        ps_q = m.psum("wide_ps_q", [P, 2, DC, 512])
        ps_qk = m.psum("wide_ps_qk", [P, 2, 512])
        ps_shift = m.psum("wide_ps_shift", [P, PAIRS])
        weights, bv_loaded, bv_added, made_q, took_q, made_qk, took_qk, made_shift, took_shift = (
            m.sem(f"wide_{n}") for n in ("weights", "bv_loaded", "bv_added", "made_q", "took_q", "made_qk", "took_qk",
                                         "made_shift", "took_shift"))
        with nc.Block() as block:

            @block.sync
            def _(sp):
                sp.dma_start(wq[:], a["wide_wq"].rearrange("(c p) n -> p c n", p=P)).then_inc(weights, 16)
                sp.dma_start(wk_t[:], a["wide_wk_t"].rearrange("(c p) n -> p c n", p=P)).then_inc(weights, 16)
                sp.dma_start(bq[:], a["wide_bq"]).then_inc(weights, 16)
                sp.dma_start(bk[:], a["wide_bk"]).then_inc(weights, 16)
                sp.dma_start(bv[:], a["wide_bv"].partition_broadcast(P)).then_inc(bv_loaded, 16)

            @block.gpsimd
            def _(pool):
                pool.wait_ge(bv_loaded, 16)
                nc.gpsimd.tensor_tensor(g.X[:], g.X[:], bv[:].unsqueeze(1).to_broadcast([P, PAIRS, D]),
                                        ALU.add).then_inc(bv_added, 1)

            @block.tensor
            def _(pe):
                def queries(n):
                    at_least(pe, took_q, n - 1)
                    for oc in range(DC):
                        for c in range(DC):
                            mm = nc.tensor.matmul(ps_q[:, n % 2, oc, :], wq[:, c, P * oc:P * oc + P],
                                                  g.YT[:, c, GROUP * n:GROUP * n + GROUP], start=(c == 0), stop=(c == DC - 1))
                    mm.then_inc(made_q, 1)

                pe.wait_ge(weights, 64)
                queries(0)
                for n in range(GROUPS):
                    if n + 1 < GROUPS:
                        queries(n + 1)
                    pe.wait_ge(took_q, n + 1)
                    at_least(pe, took_qk, n - 1)
                    for c in range(DC):
                        mm = nc.tensor.matmul(ps_qk[:, n % 2, :], wk_t[:, c, :], q_t[:, c, GROUP * n:GROUP * n + GROUP],
                                              start=(c == 0), stop=(c == DC - 1))
                    mm.then_inc(made_qk, 1)
                for t in range(PAIRS):
                    for c in range(DC):
                        mm = nc.tensor.matmul(ps_shift[:, t:t + 1], q_t[:, c, P * t:P * t + P], bk[:, c:c + 1],
                                              start=(c == 0), stop=(c == DC - 1))
                mm.then_inc(made_shift, 1)

            @block.scalar
            def _(act):
                for n in range(GROUPS):
                    act.wait_ge(made_q, n + 1)
                    for c in range(DC):
                        ins = nc.scalar.activation(q_t[:, c, GROUP * n:GROUP * n + GROUP], ps_q[:, n % 2, c, :],
                                                   ACT.Identity, bias=bq[:, c:c + 1], scale=1.0)
                    ins.then_inc(took_q, 1)

            @block.vector
            def _(dve):
                for n in range(GROUPS):
                    dve.wait_ge(made_qk, n + 1)
                    nc.vector.tensor_copy(qk_all[:, GROUP * n:GROUP * n + GROUP], ps_qk[:, n % 2, :]).then_inc(took_qk, 1)
                dve.wait_ge(made_shift, 1)
                nc.vector.tensor_copy(shift[:], ps_shift[:]).then_inc(took_shift, 1)


def wide_cross_attention(nc, g, a):
    with ExitStack() as stack:
        m = Memory(nc, stack)
        wq, wk_t, wv = m.sb("wide_wq", [P, DC, D]), m.sb("wide_wk_t", [P, DC, C]), m.sb("wide_wv", [C, D])
        bq, bk = m.sb("wide_bq", [P, DC]), m.sb("wide_bk", [P, DC])
        qk_all, shift = m.sb("wide_qk_all", [C, ROWS]), m.sb("wide_shift", [P, PAIRS])
        wide_queries(nc, g, a, wq, bq, wk_t, bk, qk_all, shift)

        ctx = m.sb("wide_ctx", [P, 2, 2, len(KT), C])
        ctx_t = m.sb("wide_ctx_t", [C, 2, LK])
        qk = m.sb("wide_qk", [C, 2, P])
        neg_max, lowered, bias, row_sum, inv_sum = (m.sb(f"wide_{n}", [P, 2]) for n in
                                                    ("neg_max", "lowered", "bias", "row_sum", "inv_sum"))
        probs = m.sb("wide_probs", [P, 2, LK])
        probs_t = m.sb("wide_probs_t", [P, len(KT) * P])
        mixed, mixed_t = m.sb("wide_mixed", [P, C]), m.sb("wide_mixed_t", [C, P])
        scores = m.psum("wide_scores", [P, 2048])
        turned = m.psum("wide_turned", [P, 2, 512])
        mix, small = m.psum("wide_mix", [P, 512]), m.psum("wide_small", [P, 512])
        sem = m.sem
        wv_loaded, ctx_t_loaded, qk_copied = sem("wide_wv_loaded"), sem("wide_ctx_t_loaded"), sem("wide_qk_copied")
        ctx_loaded = [sem("wide_ctx_loaded_0"), sem("wide_ctx_loaded_1")]
        scores_ready, max_ready, probs_ready = sem("wide_scores_ready"), sem("wide_max_ready"), sem("wide_probs_ready")
        lowered_ready, bias_ready = sem("wide_lowered_ready"), sem("wide_bias_ready")
        turned_ready, copied_act, copied_dve = sem("wide_turned_ready"), sem("wide_copied_act"), sem("wide_copied_dve")
        mix_ready, inv_ready, mixed_ready = sem("wide_mix_ready"), sem("wide_inv_ready"), sem("wide_mixed_ready")
        mixed_turned, mixed_t_ready, out_ready, out_added = (sem("wide_mixed_turned"), sem("wide_mixed_t_ready"),
                                                             sem("wide_out_ready"), sem("wide_out_added"))

        def pairs(eng, body):
            for u in range(2):
                body(u, u, u > 0, True)
            with eng.Fori(1, PAIRS // 2 - 1) as i:
                for u in range(2):
                    body(2 * i + u, u, True, True)
            for u in range(2):
                body(PAIRS - 2 + u, u, True, u == 0)

        with nc.Block() as block:

            @block.sync
            def _(sp):
                def load_t(p):
                    sp.dma_start(ctx_t[:], a["ctx_t"][bass.ds(2 * p, 2)].rearrange("b f k -> f b k")).then_inc(ctx_t_loaded, 16)

                def load(p, u):
                    for b in range(2):
                        sp.dma_start(ctx[:, u, b, 0:KFULL, :], a["ctx_main"][2 * p + b]).then_inc(ctx_loaded[u], 16)
                        sp.dma_start(ctx[0:KREST, u, b, KFULL, :], a["ctx_rest"][2 * p + b]).then_inc(ctx_loaded[u], 16)

                sp.dma_start(wv[:], a["wide_wv"]).then_inc(wv_loaded, 16)
                load_t(0)
                load(0, 0)
                sp.wait_ge(scores_ready, 1)
                load_t(1)
                load(1, 1)
                with sp.Fori(1, PAIRS // 2) as i:
                    for u in range(2):
                        p = 2 * i + u
                        sp.wait_ge(scores_ready, p)
                        load_t(p)
                        sp.wait_ge(mix_ready, p - 1)
                        load(p, u)

            @block.gpsimd
            def _(pool):
                for u in range(2):
                    nc.gpsimd.tensor_copy(qk[:, u, :], qk_all[:, P * u:P * u + P]).then_inc(qk_copied, 1)
                with pool.Fori(1, PAIRS // 2) as i:
                    for u in range(2):
                        pool.wait_ge(scores_ready, 2 * i + u - 1)
                        pool.wait_ge(qk_copied, 2)
                        nc.gpsimd.tensor_copy(qk[:, u, :], qk_all[:, bass.ds(P * (2 * i + u), P)]).then_inc(qk_copied, 1)

            @block.tensor
            def _(pe):
                def score(p, u):
                    pe.wait_ge(ctx_t_loaded, 16 * (p + 1))
                    pe.wait_ge(qk_copied, p + 1)
                    for lo, n in SCORE_CHUNKS:
                        for b in range(2):
                            mm = nc.tensor.matmul(scores[T * b:T * b + T, lo:lo + n], qk[:, u, T * b:T * b + T],
                                                  ctx_t[:, b, lo:lo + n], start=True, stop=True)
                    mm.then_inc(scores_ready, 1)

                def turn_mixed(p):
                    pe.wait_ge(mixed_ready, p + 1)
                    at_least(pe, out_added, p)
                    nc.tensor.transpose(small[:, 0:P], mixed[:], g.ident[:]).then_inc(mixed_turned, 1)

                def project(p):
                    pe.wait_ge(mixed_t_ready, p + 1)
                    nc.tensor.matmul(small[:, 0:D], mixed_t[:], wv[:], start=True, stop=True).then_inc(out_ready, 1)

                def body(p, u, before, after):
                    pe.wait_ge(probs_ready, p + 1)
                    if after:
                        score(p + 1, 1 - u)
                    if before:
                        turn_mixed(p - 1)

                    def turn(k):
                        if k >= 2:
                            pe.wait_ge(copied_act, 2 * p + k - 1)
                        for t in KGROUPS[k]:
                            lo, n = KT[t]
                            mm = nc.tensor.transpose(turned[0:n, k % 2, P * (t % 4):P * (t % 4) + P],
                                                     probs[:, u, lo:lo + n], g.ident[:])
                        mm.then_inc(turned_ready, 1)

                    def weigh(k):
                        if k < 2:
                            pe.wait_ge(copied_act, 2 * p + k + 1)
                        else:
                            pe.wait_ge(copied_dve, 2 * p + k - 1)
                        if k == 0:
                            pe.wait_ge(ctx_loaded[u], 32 * (p - u) + 64)
                        for t in KGROUPS[k]:
                            n = KT[t][1]
                            for b in range(2):
                                mm = nc.tensor.matmul(mix[T * b:T * b + T, 0:C], probs_t[0:n, P * t + T * b:P * t + T * b + T],
                                                      ctx[0:n, u, b, t, :], start=(t == 0), stop=(t == len(KT) - 1))
                        if k == 3:
                            mm.then_inc(mix_ready, 1)

                    turn(0)
                    turn(1)
                    weigh(0)
                    turn(2)
                    if before:
                        project(p - 1)
                    weigh(1)
                    turn(3)
                    weigh(2)
                    weigh(3)

                pe.wait_ge(wv_loaded, 16)
                score(0, 0)
                pairs(pe, body)
                turn_mixed(PAIRS - 1)
                project(PAIRS - 1)

            @block.scalar
            def _(act):
                def exp(p, u):
                    act.wait_ge(bias_ready, p + 1)
                    nc.scalar.activation(probs[:, u, :], scores[:, 0:LK], ACT.Exp, bias=bias[:, u:u + 1], scale=1.0,
                                         accum_out=row_sum[:, u:u + 1]).then_inc(probs_ready, 1)

                def take_mixed(p):
                    act.wait_ge(mixed_turned, p + 1)
                    nc.scalar.copy(mixed_t[:], small[:, 0:P]).then_inc(mixed_t_ready, 1)

                def body(p, u, before, after):
                    if before:
                        take_mixed(p - 1)
                    for k in range(2):
                        act.wait_ge(turned_ready, 4 * p + k + 1)
                        nc.scalar.copy(probs_t[:, 512 * k:512 * k + 512], turned[:, k, :]).then_inc(copied_act, 1)
                    if after:
                        exp(p + 1, 1 - u)

                act.preload_act_table(ACT.Exp)
                exp(0, 0)
                pairs(act, body)
                take_mixed(PAIRS - 1)

            @block.vector
            def _(dve):
                def row_max(p, u):
                    dve.wait_ge(scores_ready, p + 1)
                    nc.vector.tensor_reduce(neg_max[:, u:u + 1], scores[:, 0:LK], AX_X, ALU.max, negate=True)\
                        .then_inc(max_ready, 1)
                    dve.wait_ge(max_ready, p + 1)
                    nc.vector.tensor_tensor(lowered[:, u:u + 1], neg_max[:, u:u + 1], shift[:, bass.ds(p, 1)],
                                            ALU.subtract).then_inc(lowered_ready, 1)
                    dve.wait_ge(lowered_ready, p + 1)
                    nc.vector.tensor_tensor(bias[:, u:u + 1], lowered[:, u:u + 1], shift[:, bass.ds(p, 1)],
                                            ALU.add).then_inc(bias_ready, 1)

                def add_out(p):
                    dve.wait_ge(out_ready, p + 1)
                    nc.vector.tensor_tensor(g.X[:, p, :], g.X[:, p, :], small[:, 0:D], ALU.add).then_inc(out_added, 1)

                def body(p, u, before, after):
                    if after:
                        row_max(p + 1, 1 - u)
                    dve.wait_ge(probs_ready, p + 1)
                    nc.vector.reciprocal(inv_sum[:, u:u + 1], row_sum[:, u:u + 1]).then_inc(inv_ready, 1)
                    for k in (2, 3):
                        dve.wait_ge(turned_ready, 4 * p + k + 1)
                        n, w = KT[KGROUPS[k][-1]][1], P * len(KGROUPS[k])
                        nc.vector.tensor_copy(probs_t[0:n, 512 * k:512 * k + w], turned[0:n, k % 2, 0:w])\
                            .then_inc(copied_dve, 1)
                    if before:
                        add_out(p - 1)
                    dve.wait_ge(mix_ready, p + 1)
                    dve.wait_ge(inv_ready, p + 1)
                    nc.vector.tensor_scalar(mixed[:], mix[:, 0:C], inv_sum[:, u:u + 1], None, ALU.mult)\
                        .then_inc(mixed_ready, 1)

                row_max(0, 0)
                pairs(dve, body)
                add_out(PAIRS - 1)


NH, HE = 4, 64
QK = (NH + 1) * HE
QKV = QK + HE
HALF = HE // 2
RMS_EPS = 1e-6


def rotary_qkv(nc, g, a, qkv):
    with ExitStack() as stack:
        m = Memory(nc, stack)
        w = m.sb("self_wqkv", [P, DC, QKV])
        angles = m.sb("self_angles", [P, 2, HALF])
        gain_q, gain_k = m.sb("self_gain_q", [P, HE]), m.sb("self_gain_k", [P, HE])
        table = {n: m.sb(f"self_table_{n}", [P, NH + 1, HALF]) for n in "abcd"}
        square = m.sb("self_square", [P, PAIRS, QK])
        power, root = m.sb("self_power", [P, PAIRS * (NH + 1)]), m.sb("self_root", [P, PAIRS * (NH + 1)])
        part = {n: m.sb(f"self_part_{n}", [P, PAIRS, NH + 1, HALF]) for n in "abcd"}
        ps = m.psum("self_ps_qkv", [P, 4, 512])
        loaded, made, taken, power_done, root_done, step = (m.sem(f"self_{n}") for n in
                                                            ("loaded", "made", "taken", "power_done", "root_done", "step"))
        halves = qkv[:, :, 0:QK].rearrange("p t (h j two) -> p t h j two", h=NH + 1, two=2)
        even, odd = halves[:, :, :, :, 0], halves[:, :, :, :, 1]
        heads = qkv[:, :, 0:QK].rearrange("p t (h j) -> p t h j", h=NH + 1)

        with nc.Block() as block:

            @block.sync
            def _(sp):
                sp.dma_start(w[:], a["self_wqkv_t"].rearrange("(c p) n -> p c n", p=P)).then_inc(loaded, 16)
                sp.dma_start(angles[:], a["self_angles"]).then_inc(loaded, 16)
                sp.dma_start(gain_q[:], a["self_gain_q"].partition_broadcast(P)).then_inc(loaded, 16)
                sp.dma_start(gain_k[:], a["self_gain_k"].partition_broadcast(P)).then_inc(loaded, 16)

            @block.tensor
            def _(pe):
                pe.wait_ge(loaded, 64)
                for t in range(PAIRS):
                    at_least(pe, taken, t - 3)
                    for c in range(DC):
                        mm = nc.tensor.matmul(ps[:, t % 4, 0:QKV], g.YT[:, c, P * t:P * t + P], w[:, c, :],
                                              start=(c == 0), stop=(c == DC - 1))
                    mm.then_inc(made, 1)

            @block.scalar
            def _(act):
                for t in range(PAIRS):
                    act.wait_ge(made, t + 1)
                    nc.scalar.copy(qkv[:, t, :], ps[:, t % 4, 0:QKV]).then_inc(taken, 1)
                act.wait_ge(power_done, 1)
                nc.scalar.activation(root[:], power[:], ACT.Sqrt).then_inc(root_done, 1)

            @block.vector
            def _(dve):
                chain = Chain(dve, step)
                tt, link = nc.vector.tensor_tensor, chain.step
                dve.wait_ge(loaded, 64)
                for name, wave, side in (("a", 0, 0), ("b", 1, 1), ("c", 1, 0), ("d", 0, 1)):
                    for lo, hi, gain in ((0, NH, gain_q), (NH, NH + 1, gain_k)):
                        n = hi - lo
                        link(tt(table[name][:, lo:hi, :], angles[:, wave, :].unsqueeze(1).to_broadcast([P, n, HALF]),
                                gain[:].rearrange("p (j two) -> p two j", two=2)[:, side, :].unsqueeze(1).to_broadcast([P, n, HALF]),
                                ALU.mult))
                    link(nc.vector.tensor_scalar(table[name][:, 0:NH, :], table[name][:, 0:NH, :], HE ** -0.5, None, ALU.mult))
                for n in range(4):
                    dve.wait_ge(taken, 4 * n + 4)
                    t = slice(4 * n, 4 * n + 4)
                    link(tt(square[:, t, :], qkv[:, t, 0:QK], qkv[:, t, 0:QK], ALU.mult))
                    link(nc.vector.tensor_reduce(power[:, 4 * n * (NH + 1):4 * (n + 1) * (NH + 1)],
                                                 square[:, t, :].rearrange("p t (h j) -> p (t h) j", j=HE), AX_X, ALU.add))
                nc.vector.tensor_scalar(power[:], power[:], 1.0 / HE, RMS_EPS, ALU.mult, ALU.add).then_inc(power_done, 1)
                dve.wait_ge(root_done, 1)
                link(nc.vector.reciprocal(power[:], root[:]))
                flat = qkv[:, :, 0:QK].rearrange("p t (h j) -> p t h j", h=NH + 1)
                link(tt(flat, flat, power[:].rearrange("p (t h) -> p t h", t=PAIRS).unsqueeze(3)
                        .to_broadcast([P, PAIRS, NH + 1, HE]), ALU.mult))
                for name, side in (("a", even), ("b", odd), ("c", even), ("d", odd)):
                    link(tt(part[name][:], side, table[name][:].unsqueeze(1).to_broadcast([P, PAIRS, NH + 1, HALF]), ALU.mult))
                link(tt(even, part["a"][:], part["b"][:], ALU.subtract))
                link(tt(odd, part["c"][:], part["d"][:], ALU.add))


def self_attention(nc, g, a):
    with ExitStack() as stack:
        m = Memory(nc, stack)
        qkv = m.sb("self_qkv", [P, PAIRS, QKV])
        rotary_qkv(nc, g, a, qkv)
        wo = m.sb("self_wo", [P, DC, D])
        mask = m.sb("self_mask", [P, P])
        now = m.sb("self_now", [P, QK + HE])
        q_t = m.sb("self_q_t", [P, DC, P])
        k_blocks = m.sb("self_k_blocks", [P, 2, P])
        masked, probs, shares = (m.sb(f"self_{n}", [P, NH, P]) for n in ("masked", "probs", "shares"))
        neg_max, row_sum, inv_sum = (m.sb(f"self_{n}", [P, NH]) for n in ("neg_max", "row_sum", "inv_sum"))
        shares_t = m.sb("self_shares_t", [P, NH, P])
        heads_out, heads_out_t = m.sb("self_heads_out", [P, D]), m.sb("self_heads_out_t", [P, DC, P])
        bank = {n: m.psum(f"self_ps_{n}", [P, 512]) for n in ("turn_qk", "scores", "turn_p", "mix", "turn_o", "out")}
        sem = m.sem
        loaded, zeroed, now_ready = sem("self_att_loaded"), sem("self_zeroed"), sem("self_now_ready")
        qk_turned, qk_taken, scores_ready = sem("self_qk_turned"), sem("self_qk_taken"), sem("self_scores_ready")
        masked_ready, max_ready, probs_ready = sem("self_masked_ready"), sem("self_max_ready"), sem("self_probs_ready")
        inv_ready, shares_ready = sem("self_inv_ready"), sem("self_shares_ready")
        shares_turned, shares_taken = sem("self_shares_turned"), sem("self_shares_taken")
        mix_ready, mix_taken = sem("self_mix_ready"), sem("self_mix_taken")
        out_turned, out_taken, out_ready, out_added = (sem("self_out_turned"), sem("self_out_taken"),
                                                       sem("self_out_ready"), sem("self_out_added"))
        LAST = 5

        def turns(eng, body):
            for i in range(LAST + 1):
                body(i, lambda k: 0 <= i - k)
            with eng.Fori(LAST + 1, PAIRS) as i:
                body(i, lambda k: True)
            for i in range(PAIRS, PAIRS + LAST):
                body(i, lambda k: i - k < PAIRS)

        with nc.Block() as block:

            @block.sync
            def _(sp):
                sp.dma_start(wo[:], a["self_wo_t"].rearrange("(c p) n -> p c n", p=P)).then_inc(loaded, 16)
                sp.dma_start(mask[:], a["self_mask"]).then_inc(loaded, 16)

            @block.gpsimd
            def _(pool):
                nc.gpsimd.memset(k_blocks[:], 0.0).then_inc(zeroed, 1)

                def copy(i):
                    if not isinstance(i, int) or i > 0:
                        pool.wait_ge(qk_turned, i)
                        pool.wait_ge(zeroed, 1)
                    nc.gpsimd.tensor_copy(now[:, 0:QK], qkv[:, i, 0:QK]).then_inc(now_ready, 1)
                    nc.gpsimd.tensor_copy(now[:, QK:QK + HE], qkv[:, i, QK - HE:QK]).then_inc(now_ready, 1)

                copy(0)
                with pool.Fori(1, PAIRS) as i:
                    copy(i)

            @block.tensor
            def _(pe):
                def body(i, stage):
                    if stage(5):
                        pe.wait_ge(out_taken, i - 4)
                        at_least(pe, out_added, i - 5)
                        for c in range(DC):
                            mm = nc.tensor.matmul(bank["out"][:, 0:D], heads_out_t[:, c, :], wo[:, c, :],
                                                  start=(c == 0), stop=(c == DC - 1))
                        mm.then_inc(out_ready, 1)
                    if stage(4):
                        pe.wait_ge(mix_taken, i - 3)
                        for c in range(DC):
                            mm = nc.tensor.transpose(bank["turn_o"][:, P * c:P * c + P], heads_out[:, P * c:P * c + P], g.ident[:])
                        mm.then_inc(out_turned, 1)
                    if stage(3):
                        pe.wait_ge(shares_taken, i - 2)
                        for h in range(NH):
                            mm = nc.tensor.matmul(bank["mix"][:, HE * h:HE * h + HE], shares_t[:, h, :],
                                                  qkv[:, i - 3, QK:QKV], start=True, stop=True)
                        mm.then_inc(mix_ready, 1)
                    if stage(2):
                        pe.wait_ge(shares_ready, i - 1)
                        for h in range(NH):
                            mm = nc.tensor.transpose(bank["turn_p"][:, P * h:P * h + P], shares[:, h, :], g.ident[:])
                        mm.then_inc(shares_turned, 1)
                    if stage(1):
                        pe.wait_ge(qk_taken, 3 * i)
                        for c in range(DC):
                            mm = nc.tensor.matmul(bank["scores"][:, 2 * P * c:2 * P * c + 2 * P], q_t[:, c, :], k_blocks[:],
                                                  start=True, stop=True)
                        mm.then_inc(scores_ready, 1)
                    if stage(0):
                        pe.wait_ge(now_ready, 2 * i + 2)
                        for c in range(3):
                            mm = nc.tensor.transpose(bank["turn_qk"][:, P * c:P * c + P], now[:, P * c:P * c + P], g.ident[:])
                        mm.then_inc(qk_turned, 1)

                pe.wait_ge(loaded, 32)
                turns(pe, body)

            @block.scalar
            def _(act):
                def body(i, stage):
                    if stage(4):
                        act.wait_ge(out_turned, i - 3)
                        nc.scalar.copy(heads_out_t[:].rearrange("p c n -> p (c n)"), bank["turn_o"][:, 0:D]).then_inc(out_taken, 1)
                    if stage(3):
                        act.wait_ge(mix_ready, i - 2)
                        nc.scalar.copy(heads_out[:], bank["mix"][:, 0:D]).then_inc(mix_taken, 1)
                    if stage(1):
                        act.wait_ge(max_ready, i)
                        for h in range(NH):
                            nc.scalar.activation(probs[:, h, :], masked[:, h, :], ACT.Exp, bias=neg_max[:, h:h + 1], scale=1.0,
                                                 accum_out=row_sum[:, h:h + 1]).then_inc(probs_ready, 1)
                    if stage(0):
                        act.wait_ge(qk_turned, i + 1)
                        nc.scalar.copy(q_t[:].rearrange("p c n -> p (c n)"), bank["turn_qk"][:, 0:2 * P]).then_inc(qk_taken, 1)
                        for b in range(2):
                            nc.scalar.copy(k_blocks[HE * b:HE * b + HE, b, :], bank["turn_qk"][HE * b:HE * b + HE, 2 * P:3 * P])\
                                .then_inc(qk_taken, 1)

                act.preload_act_table(ACT.Exp)
                act.wait_ge(zeroed, 1)
                turns(act, body)

            @block.vector
            def _(dve):
                def body(i, stage):
                    if stage(5):
                        dve.wait_ge(out_ready, i - 4)
                        nc.vector.tensor_tensor(g.X[:, i - 5, :], g.X[:, i - 5, :], bank["out"][:, 0:D], ALU.add)\
                            .then_inc(out_added, 1)
                    if stage(2):
                        dve.wait_ge(shares_turned, i - 1)
                        nc.vector.tensor_copy(shares_t[:].rearrange("p h n -> p (h n)"), bank["turn_p"][:]).then_inc(shares_taken, 1)
                    if stage(1):
                        dve.wait_ge(scores_ready, i)
                        nc.vector.tensor_tensor(masked[:], bank["scores"][:].rearrange("p (h n) -> p h n", h=NH),
                                                mask[:].unsqueeze(1).to_broadcast([P, NH, P]), ALU.add).then_inc(masked_ready, 1)
                        dve.wait_ge(masked_ready, i)
                        nc.vector.tensor_reduce(neg_max[:], masked[:], AX_X, ALU.max, negate=True).then_inc(max_ready, 1)
                        dve.wait_ge(probs_ready, NH * i)
                        nc.vector.reciprocal(inv_sum[:], row_sum[:]).then_inc(inv_ready, 1)
                        dve.wait_ge(inv_ready, i)
                        nc.vector.tensor_tensor(shares[:], probs[:], inv_sum[:].unsqueeze(2).to_broadcast([P, NH, P]),
                                                ALU.mult).then_inc(shares_ready, 1)

                dve.wait_ge(loaded, 32)
                turns(dve, body)


I = 704
IT = [(i, min(P, I - i)) for i in range(0, I, P)]
IREST = I - P * (I // P)
QMAX = 127.0


class Quantised:

    def __init__(self, m):
        self.gate_t = m.sb("ffn_gate_t", [P, DC, I], BF16)
        self.up_t = m.sb("ffn_up_t", [P, DC, I], BF16)
        self.down_t = m.sb("ffn_down_t", [P, len(IT), D], BF16)
        self.down_scale = m.sb("ffn_down_scale", [P, D])
        self.scale = {n: m.sb(f"ffn_scale_{n}", [P, t]) for n, t in (("gate", len(IT)), ("up", len(IT)), ("down", DC))}


def quantise_weights(nc, g, a, q):
    with ExitStack() as stack:
        m = Memory(nc, stack)
        shapes = {"gate": (len(IT), D), "up": (len(IT), D), "down": (DC, I)}
        w = {n: m.sb(f"quant_{n}", [P, *s]) for n, s in shapes.items()}
        low = {n: m.sb(f"quant_{n}_int", [P, *s], BF16) for n, s in shapes.items()}
        inverse = {n: m.sb(f"quant_{n}_inverse", [P, s[0]]) for n, s in shapes.items()}
        small_ident, ones, diagonal = m.sb("quant_ident", [P, P], BF16), m.sb("quant_ones", [P, P]), m.sb("quant_diagonal", [P, DC, P])
        turned = m.psum("quant_turned", [P, 6, 1024], BF16)
        spread = m.psum("quant_spread", [P, DC, P])
        loaded, filled, step, low_ready, turned_ready, stored, spread_ready, diagonal_ready = (
            m.sem(f"quant_{n}") for n in ("loaded", "filled", "step", "low_ready", "turned_ready", "stored",
                                          "spread_ready", "diagonal_ready"))
        with nc.Block() as block:

            @block.sync
            def _(sp):
                whole = P * (I // P)
                sp.wait_ge(filled, 2)
                for n, src in (("gate", a["quant_gate"]), ("up", a["quant_up"])):
                    sp.dma_start(w[n][:, 0:I // P, :], src[0:whole].rearrange("(t p) h -> p t h", p=P)).then_inc(loaded, 16)
                    sp.dma_start(w[n][0:IREST, I // P, :], src[whole:I]).then_inc(loaded, 16)
                sp.dma_start(w["down"][:], a["quant_down"].rearrange("(t p) i -> p t i", p=P)).then_inc(loaded, 16)

            @block.gpsimd
            def _(pool):
                nc.gpsimd.memset(w["gate"][:, I // P, :], 1.0).then_inc(filled, 1)
                nc.gpsimd.memset(w["up"][:, I // P, :], 1.0).then_inc(filled, 1)
                nc.gpsimd.memset(ones[:], 1.0).then_inc(filled, 1)
                nc.gpsimd.tensor_copy(small_ident[:], g.ident[:]).then_inc(filled, 1)

            @block.vector
            def _(dve):
                chain = Chain(dve, step)
                link = chain.step
                dve.wait_ge(loaded, 80)
                for n, (tiles, width) in shapes.items():
                    link(nc.vector.tensor_reduce(q.scale[n][:], w[n][:], AX_X, ALU.max, apply_absolute_value=True))
                    link(nc.vector.tensor_scalar(q.scale[n][:], q.scale[n][:], 1.0 / QMAX, None, ALU.mult))
                    link(nc.vector.reciprocal(inverse[n][:], q.scale[n][:]))
                    link(nc.vector.tensor_tensor(w[n][:], w[n][:], inverse[n][:].unsqueeze(2).to_broadcast([P, tiles, width]), ALU.mult))
                    link(nc.vector.tensor_scalar(w[n][:], w[n][:], ROUND, ROUND, ALU.add, ALU.subtract))
                    nc.vector.tensor_scalar(low[n][:], w[n][:], QMAX, -QMAX - 1.0, ALU.min, ALU.max).then_inc(low_ready, 1)
                for c in range(DC):
                    nc.vector.tensor_scalar(diagonal[:, c, :], g.ident[:], q.scale["down"][:, c:c + 1], None, ALU.mult)\
                        .then_inc(diagonal_ready, 1)
                dve.wait_ge(spread_ready, 1)
                nc.vector.tensor_copy(q.down_scale[:], spread[:].rearrange("p c n -> p (c n)")).then_inc(stored, 1)

            @block.tensor
            def _(pe):
                pe.wait_ge(filled, 4)
                for k, n in enumerate(("gate", "up")):
                    pe.wait_ge(low_ready, k + 1)
                    for c in range(DC):
                        for t, (lo, size) in enumerate(IT):
                            mm = nc.tensor.transpose(turned[:, 2 * k + c, lo:lo + size], low[n][0:size, t, P * c:P * c + P],
                                                     small_ident[0:size, 0:size])
                        mm.then_inc(turned_ready, 1)
                pe.wait_ge(low_ready, 3)
                for t, (lo, size) in enumerate(IT):
                    for c in range(DC):
                        mm = nc.tensor.transpose(turned[0:size, 4 + t // 4, 256 * (t % 4) + P * c:256 * (t % 4) + P * c + P],
                                                 low["down"][:, c, lo:lo + size], small_ident[:])
                    if t in (3, 5):
                        mm.then_inc(turned_ready, 1)
                pe.wait_ge(diagonal_ready, DC)
                for c in range(DC):
                    mm = nc.tensor.matmul(spread[:, c, :], ones[:], diagonal[:, c, :], start=True, stop=True)
                mm.then_inc(spread_ready, 1)

            @block.scalar
            def _(act):
                for k, out in enumerate((q.gate_t, q.up_t)):
                    for c in range(DC):
                        act.wait_ge(turned_ready, 2 * k + c + 1)
                        nc.scalar.copy(out[:, c, :], turned[:, 2 * k + c, 0:I]).then_inc(stored, 1)
                act.wait_ge(turned_ready, 5)
                nc.scalar.copy(q.down_t[:, 0:4, :].rearrange("p t n -> p (t n)"), turned[:, 4, :]).then_inc(stored, 1)
                act.wait_ge(turned_ready, 6)
                nc.scalar.copy(q.down_t[:, 4, :], turned[:, 5, 0:D]).then_inc(stored, 1)
                nc.scalar.copy(q.down_t[0:IREST, 5, :], turned[0:IREST, 5, D:2 * D]).then_inc(stored, 1)


def largest(nc, m, name, clip, rows_of, scale, inverse):
    top, top_all = m.sb(f"{name}_top", [P, len(rows_of)]), m.sb(f"{name}_top_all", [P, 1])
    best, clip_col, decay = m.sb(f"{name}_best", [P, 1]), m.sb(f"{name}_clip", [P, 1]), m.sb(f"{name}_decay", [P, 1])
    loaded, zeroed, step, best_ready, all_ready, decay_ready = (m.sem(f"{name}_{n}") for n in
                                                        ("loaded", "zeroed", "step", "best_ready", "all_ready", "decay_ready"))
    with nc.Block() as block:

        @block.sync
        def _(sp):
            sp.dma_start(clip_col[:], clip.partition_broadcast(P)).then_inc(loaded, 16)

        @block.gpsimd
        def _(pool):
            pool.wait_ge(best_ready, 1)
            nc.gpsimd.partition_all_reduce(top_all[:], best[:], P, bass.bass_isa.ReduceOp.max).then_inc(all_ready, 1)

        @block.scalar
        def _(act):
            act.wait_ge(loaded, 16)
            nc.scalar.activation(decay[:], clip_col[:], ACT.Exp, scale=-1.0).then_inc(decay_ready, 1)

        @block.vector
        def _(dve):
            chain = Chain(dve, step)
            link = chain.step
            link(nc.vector.memset(top[:], 0.0))
            for k, (rows, part) in enumerate(rows_of):
                link(nc.vector.tensor_reduce(top[0:rows, k:k + 1], part, AX_X, ALU.max, apply_absolute_value=True))
            nc.vector.tensor_reduce(best[:], top[:], AX_X, ALU.max).then_inc(best_ready, 1)
            dve.wait_ge(decay_ready, 1)
            link(nc.vector.tensor_scalar(decay[:], decay[:], 1.0, None, ALU.add))
            link(nc.vector.reciprocal(decay[:], decay[:]))
            dve.wait_ge(all_ready, 1)
            link(nc.vector.tensor_scalar(scale[:], top_all[:], decay[:], 1.0 / QMAX, ALU.mult, ALU.mult))
            link(nc.vector.reciprocal(inverse[:], scale[:]))


def quantised_ffn(nc, g, a):
    with ExitStack() as stack:
        m = Memory(nc, stack)
        q = Quantised(m)
        quantise_weights(nc, g, a, q)
        x_scale, x_inverse, h_scale, h_inverse = (m.sb(f"ffn_{n}", [P, 1]) for n in
                                                  ("x_scale", "x_inverse", "h_scale", "h_inverse"))
        hidden = m.sb("ffn_hidden", [P, len(IT), ROWS])
        largest(nc, m, "ffn_x", a["quant_clip_x"], [(P, g.YT[:, c, :]) for c in range(DC)], x_scale, x_inverse)
        gate_and_up(nc, g, q, x_scale, x_inverse, hidden)
        parts = [(size, hidden[0:size, t, :]) for t, (lo, size) in enumerate(IT)]
        largest(nc, m, "ffn_h", a["quant_clip_down"], parts, h_scale, h_inverse)
        down(nc, g, q, h_scale, h_inverse, hidden)


def gate_and_up(nc, g, q, x_scale, x_inverse, hidden):
    with ExitStack() as stack:
        m = Memory(nc, stack)
        low = m.sb("gate_low", [P, DC, ROWS], BF16)
        gate_scale, up_scale = m.sb("gate_scale", [P, len(IT)]), m.sb("up_scale", [P, len(IT)])
        active = m.sb("gate_active", [P, 2, 512])
        round_col = m.sb("gate_round", [P, 1])
        ps_gate, ps_up = m.psum("gate_ps_gate", [P, 2, 512]), m.psum("gate_ps_up", [P, 2, 512])
        filled, scales_ready, rounded, clipped, low_ready = (m.sem(f"gate_{n}") for n in
                                                             ("filled", "scales_ready", "rounded", "clipped", "low_ready"))
        made, active_ready, hidden_ready = m.sem("gate_made"), m.sem("gate_active_ready"), m.sem("gate_hidden_ready")
        tiles = [(n, t, lo, size) for n in range(GROUPS) for t, (lo, size) in enumerate(IT)]
        with nc.Block() as block:

            @block.vector
            def _(dve):
                nc.vector.memset(round_col[:], ROUND).then_inc(filled, 1)
                nc.vector.tensor_scalar(gate_scale[:], q.scale["gate"][:], x_scale[:], None, ALU.mult).then_inc(scales_ready, 1)
                nc.vector.tensor_scalar(up_scale[:], q.scale["up"][:], x_scale[:], None, ALU.mult).then_inc(scales_ready, 1)
                for n in range(GROUPS):
                    r = slice(GROUP * n, GROUP * n + GROUP)
                    dve.wait_ge(rounded, n + 1)
                    nc.vector.tensor_scalar(g.YT[:, :, r], g.YT[:, :, r], ROUND + QMAX, ROUND - QMAX - 1.0, ALU.min,
                                            ALU.max).then_inc(clipped, 1)
                    dve.wait_ge(clipped, n + 1)
                    nc.vector.tensor_scalar(low[:, :, r], g.YT[:, :, r], ROUND, None, ALU.subtract).then_inc(low_ready, 1)
                dve.wait_ge(scales_ready, 2)
                for k, (n, t, lo, size) in enumerate(tiles):
                    dve.wait_ge(active_ready, k + 1)
                    nc.vector.scalar_tensor_tensor(hidden[0:size, t, GROUP * n:GROUP * n + GROUP], ps_up[0:size, k % 2, :],
                                                   up_scale[0:size, t:t + 1], active[0:size, k % 2, :], ALU.mult, ALU.mult)\
                        .then_inc(hidden_ready, 1)

            @block.scalar
            def _(act):
                act.wait_ge(filled, 1)
                for n in range(GROUPS):
                    r = slice(GROUP * n, GROUP * n + GROUP)
                    nc.scalar.activation(g.YT[:, :, r], g.YT[:, :, r], ACT.Identity, bias=round_col[:],
                                         scale=x_inverse[:]).then_inc(rounded, 1)
                act.wait_ge(scales_ready, 2)
                for k, (n, t, lo, size) in enumerate(tiles):
                    act.wait_ge(made, k + 1)
                    at_least(act, hidden_ready, k - 1)
                    nc.scalar.activation(active[0:size, k % 2, :], ps_gate[0:size, k % 2, :], ACT.Silu,
                                         scale=gate_scale[0:size, t:t + 1]).then_inc(active_ready, 1)

            @block.tensor
            def _(pe):
                for k, (n, t, lo, size) in enumerate(tiles):
                    pe.wait_ge(low_ready, n + 1)
                    at_least(pe, hidden_ready, k - 1)
                    for ps, w in ((ps_gate, q.gate_t), (ps_up, q.up_t)):
                        for c in range(DC):
                            mm = nc.tensor.matmul(ps[0:size, k % 2, :], w[:, c, lo:lo + size], low[:, c, GROUP * n:GROUP * n + GROUP],
                                                  start=(c == 0), stop=(c == DC - 1))
                    mm.then_inc(made, 1)


def down(nc, g, q, h_scale, h_inverse, hidden):
    with ExitStack() as stack:
        m = Memory(nc, stack)
        low = m.sb("down_low", [P, len(IT), ROWS], BF16)
        round_col, scale = m.sb("down_round", [P, 1]), m.sb("down_scale", [P, D])
        scaled = m.sb("down_scaled", [P, 2, D])
        ps = m.psum("down_ps", [P, 4, 512])
        filled, rounded, clipped, low_ready, scale_ready, made, scaled_ready, added = (
            m.sem(f"down_{n}") for n in ("filled", "rounded", "clipped", "low_ready", "scale_ready", "made",
                                         "scaled_ready", "added"))
        parts = [(n, t, size) for n in range(GROUPS) for t, (lo, size) in ((slice(0, 5), (0, P)), (slice(5, 6), (0, IREST)))]
        with nc.Block() as block:

            @block.scalar
            def _(act):
                act.wait_ge(filled, 1)
                for n, t, size in parts:
                    v = hidden[0:size, t, GROUP * n:GROUP * n + GROUP]
                    nc.scalar.activation(v, v, ACT.Identity, bias=round_col[0:size], scale=h_inverse[0:size]).then_inc(rounded, 1)

            @block.vector
            def _(dve):
                nc.vector.memset(round_col[:], ROUND).then_inc(filled, 1)
                nc.vector.tensor_scalar(scale[:], q.down_scale[:], h_scale[:], None, ALU.mult).then_inc(scale_ready, 1)
                dve.wait_ge(scale_ready, 1)

                def quantise(k):
                    n, t, size = parts[k]
                    v = hidden[0:size, t, GROUP * n:GROUP * n + GROUP]
                    dve.wait_ge(rounded, k + 1)
                    nc.vector.tensor_scalar(v, v, ROUND + QMAX, ROUND - QMAX - 1.0, ALU.min, ALU.max).then_inc(clipped, 1)
                    dve.wait_ge(clipped, k + 1)
                    nc.vector.tensor_scalar(low[0:size, t, GROUP * n:GROUP * n + GROUP], v, ROUND, None, ALU.subtract)\
                        .then_inc(low_ready, 1)

                for n in range(GROUPS + 1):
                    if n < GROUPS:
                        quantise(2 * n)
                        quantise(2 * n + 1)
                    if n == 0:
                        continue
                    for r in range(4 * (n - 1), 4 * n):
                        dve.wait_ge(made, r + 1)
                        at_least(dve, added, r - 1)
                        nc.vector.tensor_tensor(scaled[:, r % 2, :], ps[:, r % 4, 0:D], scale[:], ALU.mult).then_inc(scaled_ready, 1)
                        dve.wait_ge(scaled_ready, r + 1)
                        nc.vector.tensor_tensor(g.X[:, r, :], g.X[:, r, :], scaled[:, r % 2, :], ALU.add).then_inc(added, 1)

            @block.tensor
            def _(pe):
                for r in range(PAIRS):
                    pe.wait_ge(low_ready, 2 * (r // 4) + 2)
                    at_least(pe, scaled_ready, r - 3)
                    for t, (lo, size) in enumerate(IT):
                        mm = nc.tensor.matmul(ps[:, r % 4, 0:D], low[0:size, t, P * r:P * r + P], q.down_t[0:size, t, :],
                                              start=(t == 0), stop=(t == len(IT) - 1))
                    mm.then_inc(made, 1)


def store(nc, g, out):
    with ExitStack() as stack:
        out_stored = Memory(nc, stack).sem("out_stored")
        with nc.Block() as block:

            @block.sync
            def _(sp):
                sp.dma_start(out.rearrange("(p b) q d -> (b q) p d", b=2), g.X[:]).then_inc(out_stored, 16)
                sp.wait_ge(out_stored, 16)


def lay_out(inputs):
    import numpy as np
    f = {k: np.asarray(v) for k, v in inputs.items()}
    ctx = f["ctx_512"]
    wkv = f["L0_xattn_Wkv"]
    main = ctx[:, :KFULL * P].reshape(B, KFULL, P, C).transpose(0, 2, 1, 3)
    arrays = dict(
        x=f["x"], ctx_main=main, ctx_rest=ctx[:, KFULL * P:], ctx_t=ctx.transpose(0, 2, 1),
        wq_t=f["L0_xattn_Wq"].T, wkv=wkv, wv_t=wkv[D:].T, wo_t=f["L0_xattn_Wo"].T,
    )
    part, column = np.arange(P)[:, None], np.arange(P)[None, :]
    arrays["own_head"] = ((part // HD) % 2 == column // T).astype(np.float32)
    columns = [f[f"L0_attn_{n}"] for n in ("bk", "bv", "bq", "bkp", "bqp", "phase_scale", "ln_g", "ln_b")]
    arrays.update(
        mix_columns=np.stack(columns).reshape(8, DC, P).transpose(2, 0, 1),
        mix_wk=f["L0_attn_Wk"], mix_wv=f["L0_attn_Wv"], mix_wq=f["L0_attn_Wq"], mix_wkp=f["L0_attn_Wkp"],
        mix_wqp=f["L0_attn_Wqp"], mix_wo=f["L0_attn_Wo"], mix_bo=f["L0_attn_bo"],
        router_w=f["L0_ffn_Wr"], router_b=f["L0_ffn_br"], expert_w1=f["L0_ffn_W1"], expert_w2=f["L0_ffn_W2"],
        expert_b1=f["L0_ffn_b1"].reshape(E, HC, P).transpose(2, 0, 1), expert_b2=f["L0_ffn_b2"],
    )
    arrays.update(
        wide_wq=f["L1_xattn_Wq"], wide_wk_t=f["L1_xattn_Wk"].T, wide_wv=f["L1_xattn_Wv"],
        wide_bq=f["L1_xattn_bq"].reshape(DC, P).T, wide_bk=f["L1_xattn_bk"].reshape(DC, P).T, wide_bv=f["L1_xattn_bv"],
    )
    inverse = (1.0 / np.float32(1000000.0) ** (np.arange(0, HE, 2, dtype=np.float32) / np.float32(HE))).astype(np.float32)
    turns = np.outer(np.arange(T, dtype=np.float32), inverse)
    angles = np.tile(np.stack([np.cos(turns), np.sin(turns)], axis=1), (2, 1, 1)).astype(np.float32)
    row, key = np.arange(P)[:, None], np.arange(P)[None, :]
    allowed = (row // T == key // T) & (key <= row) & (key >= row - 128)
    arrays.update(
        self_wqkv_t=np.concatenate([f["L1_attn_Wq"], f["L1_attn_Wk"], f["L1_attn_Wv"]]).T, self_wo_t=f["L1_attn_Wo"].T,
        self_gain_q=f["L1_attn_q_gamma"], self_gain_k=f["L1_attn_k_gamma"], self_angles=angles,
        self_mask=np.where(allowed, 0.0, -1e30).astype(np.float32),
    )
    arrays.update(
        quant_gate=f["L1_ffn_w_gate"], quant_up=f["L1_ffn_w_up"], quant_down=f["L1_ffn_w_down"],
        quant_clip_x=f["L1_ffn_clip_x"], quant_clip_down=f["L1_ffn_clip_down"],
    )
    return {k: np.ascontiguousarray(v) for k, v in arrays.items()}


def program(nc, a, out):
    Memory.semaphores.clear()
    with ExitStack() as stack:
        m = Memory(nc, stack)
        g = Kept(m)
        setup(nc, g, a["x"])
        normalise(nc, g, "ln_a")
        heads_cross_attention(nc, g, a)
        normalise(nc, g, "ln_b", into_x=True)
        with ExitStack() as held:
            reserve_experts(g, Memory(nc, held))
            token_mixer(nc, g, a)
            normalise(nc, g, "ln_c")
            experts(nc, g, a)
        recycle(nc)
        normalise(nc, g, "ln_d")
        wide_cross_attention(nc, g, a)
        normalise(nc, g, "ln_e")
        self_attention(nc, g, a)
        normalise(nc, g, "ln_f")
        quantised_ffn(nc, g, a)
        store(nc, g, out)


def kernel(**inputs):
    import numpy as np
    import concourse.bacc as bacc
    from concourse import mybir as m
    from concourse.bass_utils import run_bass_kernel_spmd

    nc = bacc.Bacc("TRN2", target_bir_lowering=False, num_devices=1)
    arrays = lay_out(inputs)
    a = {n: nc.dram_tensor(f"in_{n}", v.shape, m.dt.from_np(v.dtype), kind="ExternalInput").ap()
                 for n, v in arrays.items()}
    out = nc.dram_tensor("out_x", (B, T, D), m.dt.float32, kind="ExternalOutput").ap()
    program(nc, a, out)
    r = run_bass_kernel_spmd(nc, [{f"in_{n}": v for n, v in arrays.items()}], core_ids=[0])
    return np.asarray(r.results[0]["out_x"])
```

```python
from contextlib import ExitStack

import concourse.bass as bass
from concourse import mybir

ALU = mybir.AluOpType
ACT = mybir.ActivationFunctionType
F32 = mybir.dt.float32
F32R = mybir.dt.float32r
BF16 = mybir.dt.bfloat16
AX_X = mybir.AxisListType.X

P = 128
B, T, D = 32, 64, 256
LK, C = 1601, 128
PAIRS = B // 2
DC = D // P
ROWS = B * T
KT = [(t * P, min(P, LK - t * P)) for t in range((LK + P - 1) // P)]
KFULL = LK // P
KREST = LK - KFULL * P
KGROUPS = [list(range(g, min(g + 4, len(KT)))) for g in range(0, len(KT), 4)]
SCORE_CHUNKS = [(c, min(512, LK - c)) for c in range(0, LK, 512)]
EPS = 1e-5


def at_least(eng, sem, value):
    if isinstance(value, int) and value <= 0:
        return
    eng.wait_ge(sem, value)


class Chain:

    def __init__(self, eng, sem, base=0):
        self.eng, self.sem, self.count = eng, sem, base

    def wait(self):
        at_least(self.eng, self.sem, self.count)

    def step(self, instruction):
        instruction.then_inc(self.sem, 1)
        self.count = self.count + 1
        self.wait()


class Memory:
    semaphores = []

    def __init__(self, nc, stack):
        self.nc, self.stack = nc, stack

    def sb(self, name, shape, dt=F32):
        return self.stack.enter_context(self.nc.sbuf_tensor(name, shape, dt))

    def psum(self, name, shape, dt=F32):
        return self.stack.enter_context(self.nc.psum_tensor(name, shape, dt))

    def sem(self, name):
        sem = self.nc.alloc_semaphore(name)
        Memory.semaphores.append(sem)
        return sem


def recycle(nc):
    nc.clear_and_free_semaphores(Memory.semaphores)
    nc.all_engine_barrier()
    Memory.semaphores.clear()


class Kept:

    def __init__(self, m):
        self.X = m.sb("X", [P, PAIRS, D])
        self.Y = m.sb("Y", [P, PAIRS, D])
        self.YT = m.sb("YT", [P, DC, ROWS])
        self.ident = m.sb("ident", [P, P])
        self.experts_loaded = m.sem("experts_loaded")


def setup(nc, g, x):
    with ExitStack() as stack:
        m = Memory(nc, stack)
        x_loaded, zeroed, built = m.sem("x_loaded"), m.sem("ident_zeroed"), m.sem("ident_built")
        with nc.Block() as block:

            @block.sync
            def _(sp):
                sp.dma_start(g.X[:], x.rearrange("(p b) q d -> (b q) p d", b=2)).then_inc(x_loaded, 16)
                sp.wait_ge(x_loaded, 16)

            @block.gpsimd
            def _(pool):
                nc.gpsimd.memset(g.ident[:], 0.0).then_inc(zeroed, 1)
                pool.wait_ge(zeroed, 1)
                nc.gpsimd.affine_select(out=g.ident[:], in_=g.ident[:], compare_op=ALU.not_equal, fill=1.0,
                                        base=0, pattern=[[-1, P]], channel_multiplier=1).then_inc(built, 1)
                pool.wait_ge(built, 1)


def normalise(nc, g, name, src=None, into_x=False, gain=None, shift=None, meanwhile=(None, None)):
    src = g.X if src is None else src
    with ExitStack() as stack:
        m = Memory(nc, stack)
        stats = m.sb(f"{name}_stats", [P, PAIRS, 6])
        total, dif, square, mean, inner, var, std, rstd = (m.sb(f"{name}_{n}", [P, PAIRS]) for n in
                                                   ("total", "dif", "square", "mean", "inner", "var", "std", "rstd"))
        turned = m.psum(f"{name}_turned", [P, 4, DC, 512])
        stats_done, sums_done, squares_done, var_done, std_done, rstd_done, y_done, x_added, turned_done, stored = (
            m.sem(f"{name}_{n}") for n in ("stats_done", "sums_done", "squares_done", "var_done", "std_done",
                                           "rstd_done", "y_done", "x_added", "turned_done", "stored"))
        with nc.Block() as block:

            @block.sync
            def _(sp):
                if meanwhile[0] is not None:
                    meanwhile[0](sp)

            @block.gpsimd
            def _(pool):
                if meanwhile[1] is not None:
                    meanwhile[1](pool)

            @block.vector
            def _(dve):
                with dve.Fori(0, PAIRS) as t:
                    nc.vector.bn_stats(stats[:, t, :], src[:, t, :]).then_inc(stats_done, 1)
                dve.wait_ge(stats_done, PAIRS)
                mean_e, mean_o, var_e, var_o = stats[:, :, 1], stats[:, :, 4], stats[:, :, 2], stats[:, :, 5]
                nc.vector.tensor_tensor(total[:], mean_e, mean_o, ALU.add).then_inc(sums_done, 1)
                nc.vector.tensor_tensor(dif[:], mean_e, mean_o, ALU.subtract).then_inc(sums_done, 1)
                nc.vector.tensor_tensor(inner[:], var_e, var_o, ALU.add).then_inc(sums_done, 1)
                dve.wait_ge(sums_done, 3)
                nc.vector.tensor_scalar(mean[:], total[:], 0.5, None, ALU.mult).then_inc(squares_done, 1)
                nc.vector.tensor_tensor(square[:], dif[:], dif[:], ALU.mult).then_inc(squares_done, 1)
                nc.vector.tensor_scalar(inner[:], inner[:], 1.0 / D, EPS, ALU.mult, ALU.add).then_inc(squares_done, 1)
                dve.wait_ge(squares_done, 3)
                nc.vector.scalar_tensor_tensor(var[:], square[:], 0.25, inner[:], ALU.mult, ALU.add).then_inc(var_done, 1)
                dve.wait_ge(std_done, 1)
                nc.vector.reciprocal(rstd[:], std[:]).then_inc(rstd_done, 1)
                dve.wait_ge(rstd_done, 1)
                with dve.Fori(0, PAIRS) as t:
                    nc.vector.tensor_scalar(g.Y[:, t, :], src[:, t, :], mean[:, bass.ds(t, 1)], rstd[:, bass.ds(t, 1)],
                                            ALU.subtract, ALU.mult).then_inc(y_done, 1)
                if into_x:
                    dve.wait_ge(y_done, PAIRS)
                    nc.vector.tensor_tensor(g.X[:], g.X[:], g.Y[:], ALU.add).then_inc(x_added, 1)

            @block.scalar
            def _(act):
                act.preload_act_table(ACT.Sqrt)
                act.wait_ge(var_done, 1)
                nc.scalar.activation(std[:], var[:], ACT.Sqrt).then_inc(std_done, 1)
                for n in range(4):
                    for c in range(DC):
                        act.wait_ge(turned_done, DC * n + c + 1)
                        out = g.YT[:, c, 512 * n:512 * n + 512]
                        if gain is None:
                            nc.scalar.copy(out, turned[:, n, c, :]).then_inc(stored, 1)
                        else:
                            nc.scalar.activation(out, turned[:, n, c, :], ACT.Identity, bias=shift[:, c:c + 1],
                                                 scale=gain[:, c:c + 1]).then_inc(stored, 1)

            @block.tensor
            def _(pe):
                for n in range(4):
                    pe.wait_ge(y_done, 4 * n + 4)
                    for c in range(DC):
                        for j in range(4):
                            mm = nc.tensor.transpose(turned[:, n, c, P * j:P * j + P],
                                                     g.Y[:, 4 * n + j, P * c:P * c + P], g.ident[:])
                        mm.then_inc(turned_done, 1)


HEADS, HD = 16, D // 16
HEAD_TILES = HEADS // 2
TILES = 2 * HEAD_TILES
QUAD = 4
SCALE0 = HD ** -0.5
LKE = LK + LK % 2
PARTS = [(0, 512), (512, 1024), (1024, LK)]
PART_CHUNKS = [[(c, min(512, (hi + hi % 2) - c)) for c in range(lo, hi, 512)] for lo, hi in PARTS]
NP = len(PARTS)
VALUE_JOBS = (len(KT) + 1) // 2
QK_JOBS = HEADS // 4


def slot_jobs(before, after):
    out = [(r, 2, "inverse") for r in range(QUAD - 1, TILES, QUAD)]
    out += [(r, 2, "gather") for r in range(0 if before else QUAD, TILES, QUAD)]
    if before:
        out.append((2, 2, "wo"))
    if after:
        out.append((1, 3, "q"))
        out += [(r, place, f"qk{k}") for k, (r, place) in enumerate(((5, 3), (6, 3), (8, 3), (10, 2)))]
    places = [((1, 2), (2, 3), (3, 3), (4, 3), (5, 2), (6, 2), (7, 3))]
    if after:
        places.append(((9, 2), (10, 3), (11, 3), (12, 3), (13, 2), (14, 2), (15, 3)))
    for batch in places:
        out += [(r, place, f"v{k}") for k, (r, place) in enumerate(batch)]
    return sorted(out)


def heads_cross_attention(nc, g, a):
    with ExitStack() as stack:
        m = Memory(nc, stack)
        wq_t = m.sb("wq_t", [P, DC, D])
        wk_by_head = m.sb("wk_by_head", [P, HEADS, C])
        wv_t = m.sb("wv_t", [C, D])
        wv_parts = m.sb("wv_parts", [C, 2, D], F32R)
        wo_t = m.sb("wo_t", [P, DC, D])
        ctx_t = m.sb("ctx_t", [C, 2, LKE])
        ctx_parts = m.sb("ctx_parts", [C, 2, 2, LKE], F32R)
        values = m.sb("values", [P, 2, len(KT), D])
        q_t = m.sb("q_t", [P, DC, P])
        qk_next = m.sb("qk_next", [C, 2, HEADS, T])
        qk_parts = m.sb("qk_parts", [C, 2, 2, HEADS, T], F32R)
        part_max = m.sb("part_max", [P, 2, NP])
        neg_max = m.sb("neg_max", [P, 2])
        part_sum = m.sb("part_sum", [P, 2, NP, QUAD])
        row_sum = m.sb("row_sum", [P, QUAD])
        inv_sum = m.sb("inv_sum", [P, QUAD])
        inv_spread = m.sb("inv_spread", [P, QUAD, 2 * HD])
        weight = m.sb("weight", [P, P])
        weighed = m.sb("weighed", [P, P])
        own_head = m.sb("own_head", [P, P])
        zero = m.sb("zero", [P, 1])
        stacked = m.sb("stacked", [P, 2 * HD])
        probs = m.sb("probs", [P, 2, LK])
        probs_t = m.sb("probs_t", [P, len(KT) * P])
        quarters = m.sb("quarters", [P, QUAD, P])
        heads_out_t = m.sb("heads_out_t", [P, DC, P])

        sem = m.sem
        zeroed, weights_loaded, wk_loaded = sem("wk_zeroed"), sem("weights_loaded"), sem("wk_loaded")
        built, wv_split = sem("built"), sem("wv_split")
        ctx_loaded, ctx_split = [sem("ctx_loaded_0"), sem("ctx_loaded_1")], sem("ctx_split")
        scores_ready, part_max_ready, max_ready = sem("scores_ready"), sem("part_max_ready"), sem("max_ready")
        probs_ready, sum_ready = sem("probs_ready"), sem("sum_ready")
        turned_ready, copied_act, copied_dve = sem("turned_ready"), sem("copied_act"), sem("copied_dve")
        mix_ready, quarters_ready = sem("mix_ready"), sem("quarters_ready")
        inv_ready, spread_ready, weighed_ready, heads_ready = sem("inv_ready"), sem("spread_ready"), sem("weighed_ready"), sem("heads_ready")
        small_ready, small_taken = sem("small_ready"), sem("small_taken")
        qk_moved = sem("qk_moved")

        def load(sp, p, b):
            sp.dma_start(ctx_t[:, b, 0:LK], a["ctx_t"][2 * p + b]).then_inc(ctx_loaded[b], 16)

        def split(pool, p, b, before):
            pool.wait_ge(ctx_loaded[b], 16 * (p + 1))
            if before:
                pool.wait_ge(scores_ready, NP * TILES * (p - 1) + NP * HEAD_TILES * (b + 1))
            nc.gpsimd.tensor_tensor(ctx_parts[:, b, 0, :], ctx_t[:, b, :], zero[:].to_broadcast([P, LKE]), ALU.add)\
                .then_inc(ctx_split, 1)
            pool.wait_ge(ctx_split, 4 * p + 2 * b + 1)
            nc.gpsimd.tensor_tensor(ctx_parts[:, b, 1, :], ctx_t[:, b, :], ctx_parts[:, b, 0, :].bitcast(F32),
                                    ALU.subtract).then_inc(ctx_split, 1)

        def first_fills(pool):
            nc.gpsimd.memset(wk_by_head[:], 0.0).then_inc(zeroed, 1)
            nc.gpsimd.memset(ctx_t[:, :, LK:LKE], 0.0).then_inc(zeroed, 1)
            nc.gpsimd.memset(zero[:], 0.0).then_inc(zeroed, 1)
            nc.gpsimd.tensor_tensor(stacked[:], g.ident[:, 0:32], g.ident[:, 32:64], ALU.add).then_inc(built, 1)
            for c in (2, 3):
                pool.wait_ge(built, c - 1)
                nc.gpsimd.tensor_tensor(stacked[:], stacked[:], g.ident[:, 32 * c:32 * c + 32], ALU.add).then_inc(built, 1)
            pool.wait_ge(zeroed, 3)
            split(pool, 0, 0, False)
            split(pool, 0, 1, False)

        def first_loads(sp):
            sp.dma_start(wq_t[:], a["wq_t"].rearrange("(c p) n -> p c n", p=P)).then_inc(weights_loaded, 16)
            sp.dma_start(wv_t[:], a["wv_t"]).then_inc(weights_loaded, 16)
            sp.dma_start(wo_t[:], a["wo_t"].rearrange("(c p) n -> p c n", p=P)).then_inc(weights_loaded, 16)
            sp.dma_start(own_head[:], a["own_head"]).then_inc(weights_loaded, 16)
            for b in range(2):
                load(sp, 0, b)
            sp.wait_ge(zeroed, 1)
            key_weights = a["wkv"][0:D].rearrange("(c h r) f -> h r c f", c=DC, r=HD)
            by_chunk = wk_by_head[:].rearrange("p (c h) f -> p c h f", c=DC)
            for h in range(HEADS // DC):
                sp.dma_start(by_chunk[HD * h:HD * h + HD, :, h, :], key_weights[h]).then_inc(wk_loaded, 16)

        normalise(nc, g, "ln_a", meanwhile=(first_loads, first_fills))
        scores = m.psum("scores", [P, 2048])
        turned = m.psum("turned", [P, 2, 512])
        mix = m.psum("mix", [P, 512])
        small = m.psum("small", [P, 512])

        FIRST = ["q"] + [f"qk{k}" for k in range(QK_JOBS)] + [f"v{k}" for k in range(VALUE_JOBS)]
        FULL, EARLY = len(slot_jobs(True, True)), len(slot_jobs(False, True))

        def job_no(p, before, after, job):
            base = len(FIRST) if isinstance(p, int) and p == 0 else (p - 1) * FULL + len(FIRST) + EARLY
            return base + slot_jobs(before, after).index(job)

        LAST_JOB = len(FIRST) + EARLY + (PAIRS - 2) * FULL + len(slot_jobs(True, False))

        def pairs(eng, body):
            body(0, False, True)
            with eng.Fori(1, PAIRS - 1) as p:
                body(p, True, True)
            body(PAIRS - 1, True, False)

        def first_bank(k):
            return scores[:, 512 * (k % 4):512 * (k % 4) + 512]

        def places(name, b, bank=small):
            if name == "q":
                return q_t[:], bank[:, 0:D].rearrange("p (c n) -> p c n", c=DC)
            if name[0] == "q":
                h = 4 * int(name[2:])
                return qk_next[:, :, h:h + 4, :], bank[:, 0:4 * P].rearrange("p (h b q) -> p b h q", h=4, b=2)
            t = 2 * int(name[1:])
            tiles = min(2, len(KT) - t)
            n = KT[t][1]
            return values[0:n, b, t:t + tiles, :], bank[0:n, 0:D * tiles].rearrange("p (t d) -> p t d", t=tiles)

        def jobs_at(r, place, before, after):
            return [j for j in slot_jobs(before, after) if j[:2] == (r, place)]

        with nc.Block() as block:

            @block.sync
            def _(sp):
                with sp.Fori(1, PAIRS) as p:
                    for b in range(2):
                        sp.wait_ge(ctx_split, 4 * (p - 1) + 2 * b + 2)
                        load(sp, p, b)

            @block.gpsimd
            def _(pool):
                def move(p, b):
                    nc.gpsimd.tensor_tensor(qk_parts[:, b, 0], qk_next[:, b],
                                            zero[:].unsqueeze(2).to_broadcast([P, HEADS, T]), ALU.add).then_inc(qk_moved, 1)
                    pool.wait_ge(qk_moved, 4 * p + 2 * b + 1)
                    nc.gpsimd.tensor_tensor(qk_parts[:, b, 1], qk_next[:, b], qk_parts[:, b, 0].bitcast(F32), ALU.subtract)\
                        .then_inc(qk_moved, 1)

                pool.wait_ge(small_taken, 1 + QK_JOBS)
                move(0, 0)
                move(0, 1)

                def body(p, before):
                    split(pool, p + 1, 0, True)
                    pool.wait_ge(small_taken, job_no(p, before, True, (10, 2, "qk3")) + 1)
                    move(p + 1, 0)
                    split(pool, p + 1, 1, True)
                    move(p + 1, 1)

                body(0, False)
                with pool.Fori(1, PAIRS - 1) as p:
                    body(p, True)

            @block.tensor
            def _(pe):
                def three_products(out, left, right):
                    for k, (x, y) in enumerate(((0, 0), (0, 1), (1, 0))):
                        mm = nc.tensor.matmul(out, left(x), right(y), start=(k == 0), stop=(k == 2))
                    return mm

                def q_product(p, bank=small):
                    for oc in range(DC):
                        for c in range(DC):
                            mm = nc.tensor.matmul(bank[:, P * oc:P * oc + P], wq_t[:, c, P * oc:P * oc + P],
                                                  g.YT[:, c, bass.ds(P * p, P)], start=(c == 0), stop=(c == DC - 1))
                    return mm

                def qk_product(n, bank=small):
                    for h in range(4 * n, 4 * n + 4):
                        mm = nc.tensor.matmul(bank[:, P * (h % 4):P * (h % 4) + P], wk_by_head[:, h, :],
                                              q_t[:, h // 8, :], start=True, stop=True)
                    return mm

                def v_product(b, k, bank=small):
                    for t in range(2 * k, min(2 * k + 2, len(KT))):
                        lo, n = KT[t]
                        out = D * (t % 2)
                        mm = three_products(bank[0:n, out:out + D], lambda x: ctx_parts[:, b, x, lo:lo + n],
                                            lambda y: wv_parts[:, y, :])
                    return mm

                def gather():
                    for j in range(QUAD):
                        q = 2 * HD * j
                        mm = nc.tensor.matmul(small[q:q + 2 * HD, 0:P], stacked[:], quarters[:, j, :], start=True, stop=True)
                    return mm

                def wo_product():
                    for c in range(DC):
                        mm = nc.tensor.matmul(small[:, 0:D], heads_out_t[:, c, :], wo_t[:, c, :],
                                              start=(c == 0), stop=(c == DC - 1))
                    return mm

                def score_part(b, j, part):
                    for lo, n in PART_CHUNKS[part]:
                        mm = three_products(scores[:, lo:lo + n], lambda x: qk_parts[:, b, x, 2 * j:2 * j + 2, :],
                                            lambda y: ctx_parts[:, b, y, lo:lo + n])
                    mm.then_inc(scores_ready, 1)

                def weigh(row, tile, k):
                    if k < 2:
                        pe.wait_ge(copied_act, 2 * row + k + 1)
                    else:
                        pe.wait_ge(copied_dve, 2 * row + k - 1)
                    b, heads = tile // HEAD_TILES, 2 * HD * (tile % HEAD_TILES)
                    for t in KGROUPS[k]:
                        n, q = KT[t][1], 2 * HD * (t % 4)
                        mm = nc.tensor.matmul(mix[q:q + 2 * HD, 0:P], values[0:n, b, t, heads:heads + 2 * HD],
                                              probs_t[0:n, P * t:P * t + P], start=(t < 4), stop=(t + 4 >= len(KT)))
                    if k == len(KGROUPS) - 1:
                        mm.then_inc(mix_ready, 1)

                def body(p, before, after):
                    def run(r, place):
                        for job in jobs_at(r, place, before, after):
                            name = job[2]
                            pe.wait_ge(small_taken, job_no(p, before, after, job))
                            if name == "gather":
                                pe.wait_ge(quarters_ready, TILES * p + r)
                                mm = gather()
                            elif name == "inverse":
                                pe.wait_ge(spread_ready, (TILES // QUAD) * p + r // QUAD + 1)
                                mm = nc.tensor.transpose(small[:, 0:P], inv_spread[:].rearrange("p j d -> p (j d)"), g.ident[:])
                            elif name == "wo":
                                pe.wait_ge(heads_ready, (TILES // QUAD) * p)
                                mm = wo_product()
                            elif name == "q":
                                mm = q_product(p + 1)
                            elif name[0] == "q":
                                mm = qk_product(int(name[2:]))
                            else:
                                k = int(name[1:])
                                if k == 0:
                                    pe.wait_ge(ctx_split, 4 * p + (4 if r < HEAD_TILES else 6))
                                mm = v_product(1 if r < HEAD_TILES else 0, k)
                            mm.then_inc(small_ready, 1)

                    for r in range(TILES):
                        row = TILES * p + r
                        b = r // HEAD_TILES

                        def next_scores(part):
                            pe.wait_ge(probs_ready, NP * row + part + 1)
                            if r + 1 < TILES or after:
                                nxt = (r + 1) % TILES
                                if part == 0 and nxt == HEAD_TILES:
                                    pe.wait_ge(qk_moved, 4 * p + 4)
                                if part == 0 and nxt == 0:
                                    pe.wait_ge(qk_moved, 4 * p + 6)
                                score_part(nxt // HEAD_TILES, nxt % HEAD_TILES, part)

                        def turn(k):
                            if k >= 2:
                                pe.wait_ge(copied_act, 2 * row + k - 1)
                            elif r > 0 or before:
                                pe.wait_ge(copied_dve, 2 * row + k - 1)
                            for t in KGROUPS[k]:
                                lo, n = KT[t]
                                mm = nc.tensor.transpose(turned[0:n, k % 2, P * (t % 4):P * (t % 4) + P],
                                                         probs[:, r % 2, lo:lo + n], g.ident[:])
                            mm.then_inc(turned_ready, 1)

                        for part in range(NP):
                            next_scores(part)
                        turn(0)
                        if r > 0 or before:
                            weigh(row - 1, (r - 1) % TILES, 2)
                            weigh(row - 1, (r - 1) % TILES, 3)
                        turn(1)
                        run(r, 2)
                        turn(2)
                        if r > 0 or before:
                            pe.wait_ge(quarters_ready, row)
                        weigh(row, r, 0)
                        weigh(row, r, 1)
                        turn(3)
                        run(r, 3)

                pe.wait_ge(weights_loaded, 64)
                pe.wait_ge(wk_loaded, 16 * (HEADS // DC))
                pe.wait_ge(built, 3)
                pe.wait_ge(wv_split, 2)
                for k, n in enumerate(FIRST):
                    at_least(pe, small_taken, max(k - 3, 1 if n == "qk0" else 0))
                    if n == "qk0":
                        pe.wait_ge(wk_loaded, 16 * (HEADS // DC))
                    if n == "v0":
                        pe.wait_ge(built, 3)
                        pe.wait_ge(wv_split, 2)
                        pe.wait_ge(ctx_split, 2)
                    if n == "q":
                        mm = q_product(0, first_bank(k))
                    elif n[0] == "q":
                        mm = qk_product(int(n[2:]), first_bank(k))
                    else:
                        mm = v_product(0, int(n[1:]), first_bank(k))
                    mm.then_inc(small_ready, 1)
                pe.wait_ge(small_taken, len(FIRST))
                pe.wait_ge(qk_moved, 2)
                for part in range(NP):
                    score_part(0, 0, part)
                pairs(pe, body)
                weigh(TILES * PAIRS - 1, TILES - 1, 2)
                weigh(TILES * PAIRS - 1, TILES - 1, 3)
                pe.wait_ge(quarters_ready, TILES * PAIRS)
                pe.wait_ge(small_taken, LAST_JOB)
                gather().then_inc(small_ready, 1)
                pe.wait_ge(small_taken, LAST_JOB + 1)
                pe.wait_ge(heads_ready, (TILES // QUAD) * PAIRS)
                wo_product().then_inc(small_ready, 1)

            @block.scalar
            def _(act):
                def take(job, name, b, bank=small):
                    act.wait_ge(small_ready, job + 1)
                    out, src = places(name, b, bank)
                    nc.scalar.activation(out, src, ACT.Copy, scale=SCALE0 if name == "q" else 1.0).then_inc(small_taken, 1)

                def exp(tile, row, part):
                    act.wait_ge(max_ready, row + 1)
                    k, (lo, hi) = tile % (2 * QUAD), PARTS[part]
                    nc.scalar.activation(probs[:, tile % 2, lo:hi], scores[:, lo:hi], ACT.Exp,
                                         bias=neg_max[:, tile % 2:tile % 2 + 1], scale=1.0,
                                         accum_out=part_sum[:, k // QUAD, part, k % QUAD:k % QUAD + 1]).then_inc(probs_ready, 1)

                def body(p, before, after):
                    def take_jobs(r):
                        for job in jobs_at(r, 3, before, after):
                            if job[2] == "qk0":
                                act.wait_ge(qk_moved, 4 * p + 4)
                            take(job_no(p, before, after, job), job[2], 1 if r < HEAD_TILES else 0)

                    for r in range(TILES):
                        row = TILES * p + r
                        for k in range(2):
                            act.wait_ge(turned_ready, 4 * row + k + 1)
                            nc.scalar.copy(probs_t[:, 512 * k:512 * k + 512], turned[:, k, :]).then_inc(copied_act, 1)
                        if r + 1 < TILES or after:
                            for part in range(NP):
                                exp((r + 1) % TILES, row + 1, part)
                        take_jobs(r)

                act.preload_act_table(ACT.Exp)
                for k, n in enumerate(FIRST):
                    take(k, n, 0, first_bank(k))
                for part in range(NP):
                    exp(0, 0, part)
                pairs(act, body)

            @block.vector
            def _(dve):
                def part_row_max(tile, row, part):
                    lo, hi = PARTS[part]
                    dve.wait_ge(scores_ready, NP * row + part + 1)
                    nc.vector.tensor_reduce(part_max[:, tile % 2, part:part + 1], scores[:, lo:hi], AX_X, ALU.max)\
                        .then_inc(part_max_ready, 1)

                def row_max(tile, row):
                    dve.wait_ge(part_max_ready, NP * (row + 1))
                    nc.vector.tensor_reduce(neg_max[:, tile % 2:tile % 2 + 1], part_max[:, tile % 2, :], AX_X, ALU.max,
                                            negate=True).then_inc(max_ready, 1)

                def finish_quad(job, tile):
                    dve.wait_ge(small_ready, job + 1)
                    nc.vector.tensor_tensor(weighed[:], small[:, 0:P], weight[:], ALU.mult).then_inc(small_taken, 1)
                    dve.wait_ge(small_taken, job + 1)
                    b, c = tile // HEAD_TILES, (tile // QUAD) % 2
                    nc.vector.tensor_tensor(heads_out_t[:, c, T * b:T * b + T], weighed[:, 0:T], weighed[:, T:2 * T], ALU.add)\
                        .then_inc(heads_ready, 1)

                def take_quarters(rows, tile):
                    dve.wait_ge(mix_ready, rows)
                    nc.vector.tensor_copy(quarters[:, tile % QUAD, :], mix[:, 0:P]).then_inc(quarters_ready, 1)

                def take_turned(row, k):
                    dve.wait_ge(turned_ready, 4 * row + k + 1)
                    n, w = KT[KGROUPS[k][-1]][1], P * len(KGROUPS[k])
                    nc.vector.tensor_copy(probs_t[0:n, 512 * k:512 * k + w], turned[0:n, k % 2, 0:w]).then_inc(copied_dve, 1)

                def add_to_x(job, p):
                    dve.wait_ge(small_ready, job + 1)
                    nc.vector.tensor_tensor(g.X[:, p, :], g.X[:, p, :], small[:, 0:D], ALU.add).then_inc(small_taken, 1)

                def body(p, before, after):
                    for r in range(TILES):
                        row = TILES * p + r
                        quad = (TILES // QUAD) * p + r // QUAD
                        if r % QUAD == QUAD - 1:
                            dve.wait_ge(probs_ready, NP * (row + 1))
                            k = (r // QUAD) % 2
                            nc.vector.tensor_reduce(row_sum[:], part_sum[:, k].rearrange("p n q -> p q n"), AX_X, ALU.add)\
                                .then_inc(sum_ready, 1)
                            dve.wait_ge(sum_ready, quad + 1)
                            nc.vector.reciprocal(inv_sum[:], row_sum[:]).then_inc(inv_ready, 1)
                            dve.wait_ge(inv_ready, quad + 1)
                            nc.vector.tensor_copy(inv_spread[:], inv_sum[:].unsqueeze(2).to_broadcast([P, QUAD, 2 * HD]))\
                                .then_inc(spread_ready, 1)
                        if r + 1 < TILES or after:
                            for part in range(NP):
                                part_row_max((r + 1) % TILES, row + 1, part)
                        if r > 0 or before:
                            take_quarters(row, (r - 1) % TILES)
                        if r + 1 < TILES or after:
                            row_max((r + 1) % TILES, row + 1)
                        for job in jobs_at(r, 2, before, after):
                            if job[2] not in ("gather", "wo", "inverse"):
                                number = job_no(p, before, after, job)
                                dve.wait_ge(small_ready, number + 1)
                                out, src = places(job[2], 1 if r < HEAD_TILES else 0)
                                nc.vector.tensor_copy(out, src).then_inc(small_taken, 1)
                        if r % QUAD == 0 and (r > 0 or before):
                            finish_quad(job_no(p, before, after, (r, 2, "gather")), (r - 1) % TILES)
                        if before and r == 2:
                            add_to_x(job_no(p, before, after, (2, 2, "wo")), p - 1)
                        take_turned(row, 2)
                        if r % QUAD == QUAD - 1:
                            inverse = job_no(p, before, after, (r, 2, "inverse"))
                            dve.wait_ge(small_ready, inverse + 1)
                            nc.vector.tensor_tensor(weight[:], small[:, 0:P], own_head[:], ALU.mult).then_inc(small_taken, 1)
                            dve.wait_ge(small_taken, inverse + 1)
                        take_turned(row, 3)

                dve.wait_ge(weights_loaded, 64)
                nc.vector.tensor_copy(wv_parts[:, 0, :], wv_t[:]).then_inc(wv_split, 1)
                dve.wait_ge(wv_split, 1)
                nc.vector.tensor_tensor(wv_parts[:, 1, :], wv_t[:], wv_parts[:, 0, :].bitcast(F32), ALU.subtract).then_inc(wv_split, 1)
                for part in range(NP):
                    part_row_max(0, 0, part)
                row_max(0, 0)
                pairs(dve, body)
                take_quarters(TILES * PAIRS, TILES - 1)
                finish_quad(LAST_JOB, TILES - 1)
                add_to_x(LAST_JOB + 1, PAIRS - 1)


GROUP = 512
GROUPS = ROWS // GROUP
ROUND = 12582912.0
TWO_PI = 6.2831845
TURN = 0.15915494309189535
BK, BV, BQ, BKP, BQP, PHASE, GAIN, SHIFT = range(8)


def token_mixer(nc, g, a):
    with ExitStack() as stack:
        m = Memory(nc, stack)
        columns = m.sb("mix_columns", [P, 8, DC])
        wo = m.sb("mix_wo", [P, DC, D])
        bo = m.sb("mix_bo", [P, D])
        retrieve(nc, g, a, columns, wo, bo)
        normalise(nc, g, "ln_r", src=g.Y, gain=columns[:, GAIN], shift=columns[:, SHIFT])
        with ExitStack() as inner:
            n = Memory(nc, inner)
            product = n.psum("mix_product", [P, 2, 512])
            product_done, product_added = n.sem("mix_product_done"), n.sem("mix_product_added")
            with nc.Block() as block:

                @block.tensor
                def _(pe):
                    for t in range(PAIRS):
                        at_least(pe, product_added, t - 1)
                        for c in range(DC):
                            mm = nc.tensor.matmul(product[:, t % 2, 0:D], g.YT[:, c, P * t:P * t + P], wo[:, c, :],
                                                  start=(c == 0), stop=(c == DC - 1))
                        mm.then_inc(product_done, 1)

                @block.vector
                def _(dve):
                    for t in range(PAIRS):
                        dve.wait_ge(product_done, t + 1)
                        nc.vector.tensor_tensor(g.X[:, t, :], g.X[:, t, :], product[:, t % 2, 0:D],
                                                ALU.add).then_inc(product_added, 1)


def retrieve(nc, g, a, columns, wo, bo):
    with ExitStack() as stack:
        m = Memory(nc, stack)
        w = {n: m.sb(f"mix_{n}", [P, DC, D]) for n in ("wk", "wv", "wq", "wkp", "wqp")}
        key, value, query, turn_k, turn_q = (m.sb(f"mix_{n}", [P, DC, GROUP]) for n in
                                             ("key", "value", "query", "turn_k", "turn_q"))
        wave = {n: m.sb(f"mix_{n}", [P, DC, GROUP]) for n in ("cos_k", "sin_k", "cos_q", "sin_q")}
        whole = m.sb("mix_whole", [P, DC, GROUP])
        bound = m.sb("mix_bound", [P, DC, GROUP])
        memory = [m.sb("mix_memory_re", [P, DC, GROUP]), m.sb("mix_memory_im", [P, DC, GROUP])]
        retrieved = m.sb("mix_retrieved", [P, DC, GROUP])
        keep = m.sb("mix_keep", [P, GROUP])
        per_turn = m.sb("mix_per_turn", [P, DC])
        sem = m.sem
        weights, bo_loaded, bo_added = sem("mix_weights"), sem("mix_bo_loaded"), sem("mix_bo_added")
        made_k, made_q, made_v = sem("mix_made_k"), sem("mix_made_q"), sem("mix_made_v")
        made_kp, made_qp = sem("mix_made_kp"), sem("mix_made_qp")
        took_k, took_q, took_v, tanh_done = sem("mix_took_k"), sem("mix_took_q"), sem("mix_took_v"), sem("mix_tanh_done")
        angle_done, wave_done, step, retrieved_done = sem("mix_angle_done"), sem("mix_wave_done"), sem("mix_step"), sem("mix_retrieved_done")
        rows_turned, rows_stored = sem("mix_rows_turned"), sem("mix_rows_stored")
        SETUP, STEPS = 3, 4 * (DC + 1) + 2 * (1 + DC) + 2

        def first_loads(sp):
            sp.dma_start(columns[:], a["mix_columns"]).then_inc(weights, 16)
            for n, src in (("wk", a["mix_wk"]), ("wv", a["mix_wv"]), ("wq", a["mix_wq"]), ("wkp", a["mix_wkp"]), ("wqp", a["mix_wqp"])):
                sp.dma_start(w[n][:], src.rearrange("(c p) n -> p c n", p=P)).then_inc(weights, 16)
            sp.dma_start(wo[:], a["mix_wo"].rearrange("(c p) n -> p c n", p=P)).then_inc(weights, 16)
            sp.dma_start(bo[:], a["mix_bo"].partition_broadcast(P)).then_inc(bo_loaded, 16)
            load_experts(sp, g, a)

        normalise(nc, g, "ln_b", into_x=True, meanwhile=(first_loads, None))
        ps_k, ps_v, ps_q = (m.psum(f"mix_ps_{n}", [P, DC, 512]) for n in "kvq")
        ps_r = m.psum("mix_ps_r", [P, 2, 512])

        def groups(eng, body):
            body(0, True)
            with eng.Fori(1, GROUPS) as n:
                body(n, False)

        with nc.Block() as block:

            @block.gpsimd
            def _(pool):
                pool.wait_ge(bo_loaded, 16)
                nc.gpsimd.tensor_tensor(g.X[:], g.X[:], bo[:].unsqueeze(1).to_broadcast([P, PAIRS, D]),
                                        ALU.add).then_inc(bo_added, 1)

            @block.tensor
            def _(pe):
                def project(out, weight, moving, done):
                    for oc in range(DC):
                        for c in range(DC):
                            mm = nc.tensor.matmul(out[:, oc, :], weight[:, c, P * oc:P * oc + P], moving(c),
                                                  start=(c == 0), stop=(c == DC - 1))
                    mm.then_inc(done, 1)

                def turn_rows(n):
                    pe.wait_ge(retrieved_done, n + 1)
                    for j in range(4):
                        for c in range(DC):
                            mm = nc.tensor.transpose(ps_r[:, j // 2, D * (j % 2) + P * c:D * (j % 2) + P * c + P],
                                                     retrieved[:, c, P * j:P * j + P], g.ident[:])
                        if j % 2:
                            mm.then_inc(rows_turned, 1)

                def body(n, first):
                    y = lambda c: g.YT[:, c, bass.ds(GROUP * n, GROUP)]
                    if not first:
                        pe.wait_ge(tanh_done, 2 * n)
                        pe.wait_ge(took_v, n)
                    project(ps_k, w["wk"], y, made_k)
                    project(ps_q, w["wq"], y, made_q)
                    project(ps_v, w["wv"], y, made_v)
                    pe.wait_ge(took_k, n + 1)
                    project(ps_k, w["wkp"], lambda c: key[:, c, :], made_kp)
                    pe.wait_ge(took_q, n + 1)
                    project(ps_q, w["wqp"], lambda c: query[:, c, :], made_qp)
                    if not first:
                        turn_rows(n - 1)

                pe.wait_ge(weights, 16 * 7)
                groups(pe, body)
                turn_rows(GROUPS - 1)

            @block.scalar
            def _(act):
                def take(made, n, src, dst, row, func, done):
                    act.wait_ge(made, n + 1)
                    for c in range(DC):
                        ins = nc.scalar.activation(dst[:, c, :], src[:, c, :], func, bias=columns[:, row, c:c + 1], scale=1.0)
                    ins.then_inc(done, 1)

                def body(n, first):
                    take(made_k, n, ps_k, key, BK, ACT.Identity, took_k)
                    take(made_q, n, ps_q, query, BQ, ACT.Identity, took_q)
                    if not first:
                        act.wait_ge(retrieved_done, n)
                    take(made_v, n, ps_v, value, BV, ACT.Identity, took_v)
                    take(made_kp, n, ps_k, turn_k, BKP, ACT.Tanh, tanh_done)
                    take(made_qp, n, ps_q, turn_q, BQP, ACT.Tanh, tanh_done)
                    for k, name in enumerate(wave):
                        act.wait_ge(angle_done, 4 * n + k + 1)
                        nc.scalar.activation(wave[name][:], wave[name][:], ACT.Sin, scale=TWO_PI).then_inc(wave_done, 1)

                act.preload_act_table(ACT.Silu)
                act.wait_ge(weights, 16 * 7)
                groups(act, body)

            @block.vector
            def _(dve):
                chain = Chain(dve, step)
                chain.step(nc.vector.memset(keep[:], 1.0))
                chain.step(nc.vector.memset(keep[:].rearrange("p (b q) -> p b q", q=T)[:, :, 0:1], 0.0))
                dve.wait_ge(weights, 16 * 7)
                chain.step(nc.vector.tensor_scalar(per_turn[:], columns[:, PHASE, :], TURN, None, ALU.mult))

                def store_rows(n):
                    for j in range(2):
                        dve.wait_ge(rows_turned, 2 * n + j + 1)
                        nc.vector.tensor_scalar(g.Y[:, bass.ds(4 * n + 2 * j, 2), :],
                                                ps_r[:, j, :].rearrange("p (t d) -> p t d", t=2), D ** -0.5, None,
                                                ALU.mult).then_inc(rows_stored, 1)

                def body(n, first):
                    chain = Chain(dve, step, SETUP + STEPS * n)
                    for k, (name, turn) in enumerate(zip(wave, (turn_k, turn_k, turn_q, turn_q))):
                        if k % 2 == 0:
                            dve.wait_ge(tanh_done, 2 * n + k // 2 + 1)
                        for c in range(DC):
                            chain.step(nc.vector.tensor_scalar(wave[name][:, c, :], turn[:, c, :], per_turn[:, c:c + 1],
                                                               0.25 if name.startswith("cos") else 0.0, ALU.mult, ALU.add))
                        chain.step(nc.vector.tensor_scalar(whole[:], wave[name][:], ROUND, ROUND, ALU.add, ALU.subtract))
                        nc.vector.tensor_tensor(wave[name][:], wave[name][:], whole[:], ALU.subtract).then_inc(angle_done, 1)
                        dve.wait_ge(angle_done, 4 * n + k + 1)
                    if not first:
                        store_rows(n - 1)
                    dve.wait_ge(took_v, n + 1)
                    for k, name in enumerate(("cos_k", "sin_k")):
                        dve.wait_ge(wave_done, 4 * n + k + 1)
                        chain.step(nc.vector.tensor_tensor(bound[:], value[:], wave[name][:], ALU.mult))
                        for c in range(DC):
                            chain.step(nc.vector.tensor_tensor_scan(memory[k][:, c, :], keep[:], bound[:, c, :], 0.0,
                                                                    ALU.mult, ALU.add))
                    for k, name in enumerate(("cos_q", "sin_q")):
                        dve.wait_ge(wave_done, 4 * n + k + 3)
                        chain.step(nc.vector.tensor_tensor(memory[k][:], memory[k][:], wave[name][:], ALU.mult))
                    nc.vector.tensor_tensor(retrieved[:], memory[0][:], memory[1][:], ALU.add).then_inc(retrieved_done, 1)
                    dve.wait_ge(retrieved_done, n + 1)

                groups(dve, body)
                store_rows(GROUPS - 1)


E, H = 8, 2 * D
HC = H // P


def reserve_experts(g, m):
    g.w1, g.w2 = m.sb("expert_w1", [P, 2, DC, H]), m.sb("expert_w2", [P, 2, HC, D])
    g.b1, g.b2 = m.sb("expert_b1", [P, 2, HC]), m.sb("expert_b2", [E, D])
    g.wr, g.br = m.sb("router_w", [P, DC, E]), m.sb("router_b", [P, E])
    g.share, g.share_t = m.sb("share", [P, PAIRS, E]), m.sb("share_t", [E, ROWS])


def load_experts(sp, g, a):
    sp.dma_start(g.w1[:], a["expert_w1"][0:2].rearrange("e (c p) d -> p e c d", p=P)).then_inc(g.experts_loaded, 16)
    sp.dma_start(g.w2[:], a["expert_w2"][0:2].rearrange("e (c p) d -> p e c d", p=P)).then_inc(g.experts_loaded, 16)
    sp.dma_start(g.b1[:], a["expert_b1"][:, 0:2, :]).then_inc(g.experts_loaded, 16)
    sp.dma_start(g.b2[:], a["expert_b2"]).then_inc(g.experts_loaded, 16)
    sp.dma_start(g.wr[:], a["router_w"].rearrange("(c p) e -> p c e", p=P)).then_inc(g.experts_loaded, 16)
    sp.dma_start(g.br[:], a["router_b"].partition_broadcast(P)).then_inc(g.experts_loaded, 16)


class Parts:

    def __init__(self, m):
        self.w1 = m.sb("expert_w1_parts", [P, 2, 2, DC, H], F32R)
        self.w2 = m.sb("expert_w2_parts", [P, 2, 2, HC, D], F32R)
        self.yt = m.sb("yt_parts", [P, 2, DC, ROWS], F32R)
        self.zero = m.sb("expert_zero", [P, 1])
        self.zeroed, self.weights_split = m.sem("expert_zeroed"), m.sem("expert_weights_split")

    def split_expert(self, pool, nc, g, e, place):
        for n, (whole, parts) in enumerate(((g.w1, self.w1), (g.w2, self.w2))):
            zeros = self.zero[:].unsqueeze(2).to_broadcast([P, whole.shape[2], whole.shape[3]])
            nc.gpsimd.tensor_tensor(parts[:, place, 0], whole[:, place], zeros, ALU.add).then_inc(self.weights_split, 1)
            pool.wait_ge(self.weights_split, 4 * e + 2 * n + 1)
            nc.gpsimd.tensor_tensor(parts[:, place, 1], whole[:, place], parts[:, place, 0].bitcast(F32), ALU.subtract)\
                .then_inc(self.weights_split, 1)


def route(nc, g, parts):
    with ExitStack() as stack:
        m = Memory(nc, stack)
        logits, probs, top, order, rank, chosen, rest = (m.sb(f"route_{n}", [P, PAIRS, E]) for n in
                                                         ("logits", "probs", "top", "order", "rank", "chosen", "rest"))
        best, total = m.sb("route_best", [P, PAIRS]), m.sb("route_total", [P, PAIRS])
        ps = m.psum("route_ps", [P, PAIRS, E])
        ps_t = m.psum("route_ps_t", [P, 4, 512])
        made, step, shifted, exp_done, share_done, turned, stored, order_done, yt_split = (
            m.sem(f"route_{n}") for n in ("made", "step", "shifted", "exp_done", "share_done", "turned", "stored", "order_done", "yt_split"))

        def by_row(column):
            return column[:].unsqueeze(2).to_broadcast([P, PAIRS, E])

        with nc.Block() as block:

            @block.gpsimd
            def _(pool):
                nc.gpsimd.iota(order[:], pattern=[[0, PAIRS], [-1, E]], base=E, channel_multiplier=0,
                               allow_small_or_imprecise_dtypes=True).then_inc(order_done, 1)
                nc.gpsimd.memset(parts.zero[:], 0.0).then_inc(parts.zeroed, 1)
                pool.wait_ge(yt_split, 1)
                nc.gpsimd.tensor_tensor(parts.yt[:, 1], g.YT[:], parts.yt[:, 0].bitcast(F32), ALU.subtract).then_inc(yt_split, 1)
                pool.wait_ge(g.experts_loaded, 96)
                pool.wait_ge(parts.zeroed, 1)
                parts.split_expert(pool, nc, g, 0, 0)
                pool.wait_ge(yt_split, 2)

            @block.tensor
            def _(pe):
                pe.wait_ge(g.experts_loaded, 96)
                for t in range(PAIRS):
                    for c in range(DC):
                        mm = nc.tensor.matmul(ps[:, t, :], g.YT[:, c, P * t:P * t + P], g.wr[:, c, :],
                                              start=(c == 0), stop=(c == DC - 1))
                mm.then_inc(made, 1)
                pe.wait_ge(share_done, 1)
                for t in range(PAIRS):
                    mm = nc.tensor.transpose(ps_t[0:E, t // 4, P * (t % 4):P * (t % 4) + P], g.share[:, t, :], g.ident[:])
                mm.then_inc(turned, 1)

            @block.scalar
            def _(act):
                nc.scalar.copy(parts.yt[:, 0], g.YT[:]).then_inc(yt_split, 1)
                act.wait_ge(shifted, 1)
                nc.scalar.activation(probs[:], logits[:], ACT.Exp).then_inc(exp_done, 1)
                act.wait_ge(turned, 1)
                nc.scalar.copy(g.share_t[:].rearrange("p (n r) -> p n r", n=4), ps_t[0:E, :, :]).then_inc(stored, 1)

            @block.vector
            def _(dve):
                chain = Chain(dve, step)
                tt, link = nc.vector.tensor_tensor, chain.step
                dve.wait_ge(made, 1)
                link(tt(logits[:], ps[:], g.br[:].unsqueeze(1).to_broadcast([P, PAIRS, E]), ALU.add))
                link(nc.vector.tensor_reduce(best[:], logits[:], AX_X, ALU.max))
                tt(logits[:], logits[:], by_row(best), ALU.subtract).then_inc(shifted, 1)
                dve.wait_ge(exp_done, 1)
                link(nc.vector.tensor_reduce(total[:], probs[:], AX_X, ALU.add))
                link(nc.vector.reciprocal(total[:], total[:]))
                link(tt(probs[:], probs[:], by_row(total), ALU.mult))
                dve.wait_ge(order_done, 1)
                for n, left in enumerate((probs, rest)):
                    pick = chosen if n == 0 else top
                    link(nc.vector.tensor_reduce(best[:], left[:], AX_X, ALU.max))
                    link(tt(rank[:], left[:], by_row(best), ALU.is_equal))
                    link(tt(rank[:], rank[:], order[:], ALU.mult))
                    link(nc.vector.tensor_reduce(best[:], rank[:], AX_X, ALU.max))
                    link(tt(pick[:], rank[:], by_row(best), ALU.is_equal))
                    if n == 0:
                        link(nc.vector.scalar_tensor_tensor(rest[:], pick[:], -2.0, probs[:], ALU.mult, ALU.add))
                link(tt(chosen[:], chosen[:], top[:], ALU.add))
                tt(g.share[:], probs[:], chosen[:], ALU.mult).then_inc(share_done, 1)


def experts(nc, g, a):
    with ExitStack() as stack:
        m = Memory(nc, stack)
        parts = Parts(m)
        route(nc, g, parts)
        hidden = m.sb("hidden", [P, HC, GROUP])
        hidden_parts = m.sb("hidden_parts", [P, 2, HC, GROUP], F32R)
        PRODUCTS = ((0, 0), (0, 1), (1, 0))
        ps_h = m.psum("expert_ps_h", [P, HC, 512])
        ps_y = m.psum("expert_ps_y", [P, 4, 512])
        made_h, took_h, split_h, made_y, added_y, biased = (m.sem(f"expert_{n}") for n in
                                                            ("made_h", "took_h", "split_h", "made_y", "added_y", "biased"))

        weights_loaded = [m.sem("expert_weights_loaded_0"), m.sem("expert_weights_loaded_1")]
        b1_loaded = [m.sem("expert_b1_loaded_0"), m.sem("expert_b1_loaded_1")]
        CHUNKS = HC * GROUPS

        def by_two(eng, body):
            body(0, True)
            with eng.Fori(1, E // 2) as q:
                body(q, False)

        with nc.Block() as block:

            @block.sync
            def _(sp):
                with sp.Fori(1, E // 2) as q:
                    for k in range(2):
                        e = 2 * q + k
                        sp.wait_ge(parts.weights_split, 4 * (e - 1))
                        sp.dma_start(g.w1[:, k], a["expert_w1"].rearrange("e (c p) d -> e p c d", p=P)[e]).then_inc(weights_loaded[k], 16)
                        sp.dma_start(g.w2[:, k], a["expert_w2"].rearrange("e (c p) d -> e p c d", p=P)[e]).then_inc(weights_loaded[k], 16)
                        sp.wait_ge(took_h, 2 * CHUNKS * (e - 1))
                        sp.dma_start(g.b1[:, k], a["expert_b1"].rearrange("p e h -> e p h")[e]).then_inc(b1_loaded[k], 16)

            @block.gpsimd
            def _(pool):
                parts.split_expert(pool, nc, g, 1, 1)
                with pool.Fori(1, E // 2) as q:
                    for k in range(2):
                        e = 2 * q + k
                        pool.wait_ge(weights_loaded[k], 32 * q)
                        pool.wait_ge(made_y, PAIRS + 4 * GROUPS * (e - 1))
                        parts.split_expert(pool, nc, g, e, k)

            @block.tensor
            def _(pe):
                def first_product(s, n, k, h):
                    at_least(pe, took_h, 2 * (HC * s + h - HC) + 2)
                    for c in range(DC):
                        for i, (x, y) in enumerate(PRODUCTS):
                            mm = nc.tensor.matmul(ps_h[:, h, :], parts.w1[:, k, x, c, P * h:P * h + P],
                                                  parts.yt[:, y, c, GROUP * n:GROUP * n + GROUP],
                                                  start=(c == i == 0), stop=(c == DC - 1 and i == 2))
                    mm.then_inc(made_h, 1)

                def second_product(s, k, h):
                    pe.wait_ge(split_h, HC * s + h + 1)
                    for j in range(4):
                        if h == 0:
                            at_least(pe, added_y, 4 * (s - 1) + j + 1)
                        for i, (x, y) in enumerate(PRODUCTS):
                            mm = nc.tensor.matmul(ps_y[:, j, 0:D], hidden_parts[:, x, h, P * j:P * j + P],
                                                  parts.w2[:, k, y, h, :], start=(h == i == 0), stop=(h == HC - 1 and i == 2))
                        if h == HC - 1:
                            mm.then_inc(made_y, 1)

                def body(q, first):
                    for k in range(2):
                        e = 2 * q + k
                        pe.wait_ge(parts.weights_split, 4 * (e + 1))
                        for n in range(GROUPS):
                            s = GROUPS * e + n
                            for h in range(HC):
                                first_product(s, n, k, h)
                                if h >= 2:
                                    second_product(s, k, h - 2)
                                elif n > 0:
                                    second_product(s - 1, k, h + 2)
                                elif k > 0 or not first:
                                    second_product(s - 1, 1 - k, h + 2)

                for t in range(PAIRS):
                    at_least(pe, biased, t - 3)
                    nc.tensor.matmul(ps_y[:, t % 4, 0:D], g.share_t[:, P * t:P * t + P], g.b2[:],
                                     start=True, stop=True).then_inc(made_y, 1)
                pe.wait_ge(biased, PAIRS)
                by_two(pe, body)
                for h in (HC - 2, HC - 1):
                    second_product(E * GROUPS - 1, 1, h)

            @block.scalar
            def _(act):
                def body(q, first):
                    for k in range(2):
                        e = 2 * q + k
                        if not first:
                            act.wait_ge(b1_loaded[k], 16 * q)
                        for n in range(GROUPS):
                            for h in range(HC):
                                act.wait_ge(made_h, HC * (GROUPS * e + n) + h + 1)
                                for out in (hidden_parts[:, 0, h, :], hidden[:, h, :]):
                                    nc.scalar.activation(out, ps_h[:, h, :], ACT.Relu,
                                                         bias=g.b1[:, k, h:h + 1], scale=1.0).then_inc(took_h, 1)

                act.preload_act_table(ACT.Relu)
                by_two(act, body)

            @block.vector
            def _(dve):
                def split_hidden(s, h):
                    dve.wait_ge(took_h, 2 * (HC * s + h) + 2)
                    nc.vector.tensor_tensor(hidden_parts[:, 1, h, :], hidden[:, h, :],
                                            hidden_parts[:, 0, h, :].bitcast(F32), ALU.subtract).then_inc(split_h, 1)

                def add(s, n, e):
                    for j in range(4):
                        t = 4 * n + j
                        dve.wait_ge(made_y, PAIRS + 4 * s + j + 1)
                        nc.vector.scalar_tensor_tensor(g.X[:, t, :], ps_y[:, j, 0:D], g.share[:, t, bass.ds(e, 1)],
                                                       g.X[:, t, :], ALU.mult, ALU.add).then_inc(added_y, 1)

                def body(q, first):
                    for k in range(2):
                        e = 2 * q + k
                        for n in range(GROUPS):
                            s = GROUPS * e + n
                            for h in range(HC):
                                split_hidden(s, h)
                                if h == 1 and n > 0:
                                    add(s - 1, n - 1, e)
                                elif h == 1 and (k > 0 or not first):
                                    add(s - 1, GROUPS - 1, e - 1)

                for t in range(PAIRS):
                    dve.wait_ge(made_y, t + 1)
                    nc.vector.tensor_tensor(g.X[:, t, :], g.X[:, t, :], ps_y[:, t % 4, 0:D], ALU.add).then_inc(biased, 1)
                by_two(dve, body)
                add(E * GROUPS - 1, GROUPS - 1, E - 1)


def wide_queries(nc, g, wq, bq, wk_t, bk, bv, weights, qk_all, shift):
    with ExitStack() as stack:
        m = Memory(nc, stack)
        q_t = m.sb("wide_q_t", [P, DC, ROWS])
        ps_q = m.psum("wide_ps_q", [P, 2, DC, 512])
        ps_qk = m.psum("wide_ps_qk", [P, 2, 512])
        ps_shift = m.psum("wide_ps_shift", [P, PAIRS])
        bv_added, made_q, took_q, made_qk, took_qk, made_shift, took_shift = (
            m.sem(f"wide_{n}") for n in ("bv_added", "made_q", "took_q", "made_qk", "took_qk",
                                         "made_shift", "took_shift"))
        with nc.Block() as block:

            @block.gpsimd
            def _(pool):
                pool.wait_ge(weights, 80)
                nc.gpsimd.tensor_tensor(g.X[:], g.X[:], bv[:].unsqueeze(1).to_broadcast([P, PAIRS, D]),
                                        ALU.add).then_inc(bv_added, 1)

            @block.tensor
            def _(pe):
                def queries(n):
                    at_least(pe, took_q, n - 1)
                    for oc in range(DC):
                        for c in range(DC):
                            mm = nc.tensor.matmul(ps_q[:, n % 2, oc, :], wq[:, c, P * oc:P * oc + P],
                                                  g.YT[:, c, GROUP * n:GROUP * n + GROUP], start=(c == 0), stop=(c == DC - 1))
                    mm.then_inc(made_q, 1)

                pe.wait_ge(weights, 80)
                queries(0)
                for n in range(GROUPS):
                    if n + 1 < GROUPS:
                        queries(n + 1)
                    pe.wait_ge(took_q, n + 1)
                    at_least(pe, took_qk, n - 1)
                    for c in range(DC):
                        mm = nc.tensor.matmul(ps_qk[:, n % 2, :], wk_t[:, c, :], q_t[:, c, GROUP * n:GROUP * n + GROUP],
                                              start=(c == 0), stop=(c == DC - 1))
                    mm.then_inc(made_qk, 1)
                for t in range(PAIRS):
                    for c in range(DC):
                        mm = nc.tensor.matmul(ps_shift[:, t:t + 1], q_t[:, c, P * t:P * t + P], bk[:, c:c + 1],
                                              start=(c == 0), stop=(c == DC - 1))
                mm.then_inc(made_shift, 1)

            @block.scalar
            def _(act):
                for n in range(GROUPS):
                    act.wait_ge(made_q, n + 1)
                    for c in range(DC):
                        ins = nc.scalar.activation(q_t[:, c, GROUP * n:GROUP * n + GROUP], ps_q[:, n % 2, c, :],
                                                   ACT.Identity, bias=bq[:, c:c + 1], scale=1.0)
                    ins.then_inc(took_q, 1)

            @block.vector
            def _(dve):
                for n in range(GROUPS):
                    dve.wait_ge(made_qk, n + 1)
                    nc.vector.tensor_copy(qk_all[:, GROUP * n:GROUP * n + GROUP], ps_qk[:, n % 2, :]).then_inc(took_qk, 1)
                dve.wait_ge(made_shift, 1)
                nc.vector.tensor_copy(shift[:], ps_shift[:]).then_inc(took_shift, 1)


def wide_cross_attention(nc, g, a):
    with ExitStack() as stack:
        m = Memory(nc, stack)
        wq, wk_t, wv = m.sb("wide_wq", [P, DC, D]), m.sb("wide_wk_t", [P, DC, C]), m.sb("wide_wv", [C, D])
        bq, bk = m.sb("wide_bq", [P, DC]), m.sb("wide_bk", [P, DC])
        qk_all, shift = m.sb("wide_qk_all", [C, ROWS]), m.sb("wide_shift", [P, PAIRS])
        bv, weights = m.sb("wide_bv", [P, D]), m.sem("wide_weights")
        ctx = m.sb("wide_ctx", [P, 2, 2, len(KT), C])
        ctx_t = m.sb("wide_ctx_t", [C, 2, 2, LK])
        qk = m.sb("wide_qk", [C, 2, P])
        neg_max, lowered, bias, row_sum, inv_sum = (m.sb(f"wide_{n}", [P, 2]) for n in
                                                    ("neg_max", "lowered", "bias", "row_sum", "inv_sum"))
        part_max, part_sum = m.sb("wide_part_max", [P, 2, NP]), m.sb("wide_part_sum", [P, 2, NP])
        probs = m.sb("wide_probs", [P, 2, LK])
        probs_t = m.sb("wide_probs_t", [P, len(KT) * P])
        mixed, mixed_t = m.sb("wide_mixed", [P, C]), m.sb("wide_mixed_t", [C, P])
        sem = m.sem
        wv_loaded, qk_copied = sem("wide_wv_loaded"), sem("wide_qk_copied")
        ctx_t_loaded = [sem("wide_ctx_t_loaded_0"), sem("wide_ctx_t_loaded_1")]
        ctx_loaded = [sem("wide_ctx_loaded_0"), sem("wide_ctx_loaded_1")]
        scores_ready, max_ready, probs_ready = sem("wide_scores_ready"), sem("wide_max_ready"), sem("wide_probs_ready")
        part_max_ready, sum_ready = sem("wide_part_max_ready"), sem("wide_sum_ready")
        lowered_ready, bias_ready = sem("wide_lowered_ready"), sem("wide_bias_ready")
        turned_ready, copied_act, copied_dve = sem("wide_turned_ready"), sem("wide_copied_act"), sem("wide_copied_dve")
        mix_ready, inv_ready, mixed_ready = sem("wide_mix_ready"), sem("wide_inv_ready"), sem("wide_mixed_ready")
        mixed_turned, mixed_t_ready, out_ready, out_added = (sem("wide_mixed_turned"), sem("wide_mixed_t_ready"),
                                                             sem("wide_out_ready"), sem("wide_out_added"))

        def load_t(sp, p, u):
            sp.dma_start(ctx_t[:, u], a["ctx_t"][bass.ds(2 * p, 2)].rearrange("b f k -> f b k")).then_inc(ctx_t_loaded[u], 16)

        def load(sp, p, u):
            for b in range(2):
                sp.dma_start(ctx[:, u, b, 0:KFULL, :], a["ctx_main"][2 * p + b]).then_inc(ctx_loaded[u], 16)
                sp.dma_start(ctx[0:KREST, u, b, KFULL, :], a["ctx_rest"][2 * p + b]).then_inc(ctx_loaded[u], 16)

        def first_loads(sp):
            sp.dma_start(wq[:], a["wide_wq"].rearrange("(c p) n -> p c n", p=P)).then_inc(weights, 16)
            sp.dma_start(wk_t[:], a["wide_wk_t"].rearrange("(c p) n -> p c n", p=P)).then_inc(weights, 16)
            sp.dma_start(bq[:], a["wide_bq"]).then_inc(weights, 16)
            sp.dma_start(bk[:], a["wide_bk"]).then_inc(weights, 16)
            sp.dma_start(bv[:], a["wide_bv"].partition_broadcast(P)).then_inc(weights, 16)
            sp.dma_start(wv[:], a["wide_wv"]).then_inc(wv_loaded, 16)
            for u in range(2):
                load_t(sp, u, u)
                load(sp, u, u)

        normalise(nc, g, "ln_d", meanwhile=(first_loads, None))
        wide_queries(nc, g, wq, bq, wk_t, bk, bv, weights, qk_all, shift)
        scores = m.psum("wide_scores", [P, 2048])
        turned = m.psum("wide_turned", [P, 2, 512])
        mix, small = m.psum("wide_mix", [P, 512]), m.psum("wide_small", [P, 512])

        def pairs(eng, body):
            for u in range(2):
                body(u, u, u > 0, True)
            with eng.Fori(1, PAIRS // 2 - 1) as i:
                for u in range(2):
                    body(2 * i + u, u, True, True)
            for u in range(2):
                body(PAIRS - 2 + u, u, True, u == 0)

        with nc.Block() as block:

            @block.sync
            def _(sp):
                with sp.Fori(1, PAIRS // 2) as i:
                    for u in range(2):
                        p = 2 * i + u
                        sp.wait_ge(scores_ready, NP * (p - 1))
                        load_t(sp, p, u)
                        sp.wait_ge(mix_ready, p - 1)
                        load(sp, p, u)

            @block.gpsimd
            def _(pool):
                for u in range(2):
                    nc.gpsimd.tensor_copy(qk[:, u, :], qk_all[:, P * u:P * u + P]).then_inc(qk_copied, 1)
                with pool.Fori(1, PAIRS // 2) as i:
                    for u in range(2):
                        pool.wait_ge(scores_ready, NP * (2 * i + u - 1))
                        pool.wait_ge(qk_copied, 2)
                        nc.gpsimd.tensor_copy(qk[:, u, :], qk_all[:, bass.ds(P * (2 * i + u), P)]).then_inc(qk_copied, 1)

            @block.tensor
            def _(pe):
                def score(p, u, part):
                    if part == 0:
                        pe.wait_ge(ctx_t_loaded[u], 8 * (p - u) + 16)
                        pe.wait_ge(qk_copied, p + 1)
                    for lo, n in [chunk for chunk in SCORE_CHUNKS if PARTS[part][0] <= chunk[0] < PARTS[part][1]]:
                        for b in range(2):
                            mm = nc.tensor.matmul(scores[T * b:T * b + T, lo:lo + n], qk[:, u, T * b:T * b + T],
                                                  ctx_t[:, u, b, lo:lo + n], start=True, stop=True)
                    mm.then_inc(scores_ready, 1)

                def turn_mixed(p):
                    pe.wait_ge(mixed_ready, p + 1)
                    at_least(pe, out_added, p)
                    nc.tensor.transpose(small[:, 0:P], mixed[:], g.ident[:]).then_inc(mixed_turned, 1)

                def project(p):
                    pe.wait_ge(mixed_t_ready, p + 1)
                    nc.tensor.matmul(small[:, 0:D], mixed_t[:], wv[:], start=True, stop=True).then_inc(out_ready, 1)

                def body(p, u, before, after):
                    def next_scores(part):
                        pe.wait_ge(probs_ready, NP * p + part + 1)
                        if after:
                            score(p + 1, 1 - u, part)

                    def turn(k):
                        if k >= 2:
                            pe.wait_ge(copied_act, 2 * p + k - 1)
                        elif before:
                            pe.wait_ge(copied_dve, 2 * p + k - 1)
                        for t in KGROUPS[k]:
                            lo, n = KT[t]
                            mm = nc.tensor.transpose(turned[0:n, k % 2, P * (t % 4):P * (t % 4) + P],
                                                     probs[:, u, lo:lo + n], g.ident[:])
                        mm.then_inc(turned_ready, 1)

                    def weigh(k):
                        if k < 2:
                            pe.wait_ge(copied_act, 2 * p + k + 1)
                        else:
                            pe.wait_ge(copied_dve, 2 * p + k - 1)
                        if k == 0:
                            pe.wait_ge(ctx_loaded[u], 32 * (p - u) + 64)
                        for t in KGROUPS[k]:
                            n = KT[t][1]
                            for b in range(2):
                                mm = nc.tensor.matmul(mix[T * b:T * b + T, 0:C], probs_t[0:n, P * t + T * b:P * t + T * b + T],
                                                      ctx[0:n, u, b, t, :], start=(t == 0), stop=(t == len(KT) - 1))
                        if k == 3:
                            mm.then_inc(mix_ready, 1)

                    next_scores(0)
                    turn(0)
                    next_scores(1)
                    turn(1)
                    if before:
                        turn_mixed(p - 1)
                    next_scores(2)
                    weigh(0)
                    turn(2)
                    if before:
                        project(p - 1)
                    weigh(1)
                    turn(3)
                    weigh(2)
                    weigh(3)

                pe.wait_ge(wv_loaded, 16)
                for part in range(NP):
                    score(0, 0, part)
                pairs(pe, body)
                turn_mixed(PAIRS - 1)
                project(PAIRS - 1)

            @block.scalar
            def _(act):
                def exp(p, u):
                    act.wait_ge(bias_ready, p + 1)
                    for part, (lo, hi) in enumerate(PARTS):
                        nc.scalar.activation(probs[:, u, lo:hi], scores[:, lo:hi], ACT.Exp, bias=bias[:, u:u + 1], scale=1.0,
                                             accum_out=part_sum[:, u, part:part + 1]).then_inc(probs_ready, 1)

                def take_mixed(p):
                    act.wait_ge(mixed_turned, p + 1)
                    nc.scalar.copy(mixed_t[:], small[:, 0:P]).then_inc(mixed_t_ready, 1)

                def body(p, u, before, after):
                    for k in range(2):
                        act.wait_ge(turned_ready, 4 * p + k + 1)
                        nc.scalar.copy(probs_t[:, 512 * k:512 * k + 512], turned[:, k, :]).then_inc(copied_act, 1)
                    if before:
                        take_mixed(p - 1)
                    if after:
                        exp(p + 1, 1 - u)

                act.preload_act_table(ACT.Exp)
                exp(0, 0)
                pairs(act, body)
                take_mixed(PAIRS - 1)

            @block.vector
            def _(dve):
                def row_max(p, u):
                    for part, (lo, hi) in enumerate(PARTS):
                        dve.wait_ge(scores_ready, NP * p + part + 1)
                        nc.vector.tensor_reduce(part_max[:, u, part:part + 1], scores[:, lo:hi], AX_X, ALU.max)\
                            .then_inc(part_max_ready, 1)
                    dve.wait_ge(part_max_ready, NP * (p + 1))
                    nc.vector.tensor_reduce(neg_max[:, u:u + 1], part_max[:, u, :], AX_X, ALU.max, negate=True)\
                        .then_inc(max_ready, 1)
                    dve.wait_ge(max_ready, p + 1)
                    nc.vector.tensor_tensor(lowered[:, u:u + 1], neg_max[:, u:u + 1], shift[:, bass.ds(p, 1)],
                                            ALU.subtract).then_inc(lowered_ready, 1)
                    dve.wait_ge(lowered_ready, p + 1)
                    nc.vector.tensor_tensor(bias[:, u:u + 1], lowered[:, u:u + 1], shift[:, bass.ds(p, 1)],
                                            ALU.add).then_inc(bias_ready, 1)

                def add_out(p):
                    dve.wait_ge(out_ready, p + 1)
                    nc.vector.tensor_tensor(g.X[:, p, :], g.X[:, p, :], small[:, 0:D], ALU.add).then_inc(out_added, 1)

                def body(p, u, before, after):
                    if after:
                        row_max(p + 1, 1 - u)
                    dve.wait_ge(probs_ready, NP * (p + 1))
                    nc.vector.tensor_reduce(row_sum[:, u:u + 1], part_sum[:, u, :], AX_X, ALU.add).then_inc(sum_ready, 1)
                    dve.wait_ge(sum_ready, p + 1)
                    nc.vector.reciprocal(inv_sum[:, u:u + 1], row_sum[:, u:u + 1]).then_inc(inv_ready, 1)
                    for k in (2, 3):
                        dve.wait_ge(turned_ready, 4 * p + k + 1)
                        n, w = KT[KGROUPS[k][-1]][1], P * len(KGROUPS[k])
                        nc.vector.tensor_copy(probs_t[0:n, 512 * k:512 * k + w], turned[0:n, k % 2, 0:w])\
                            .then_inc(copied_dve, 1)
                    if before:
                        add_out(p - 1)
                    dve.wait_ge(mix_ready, p + 1)
                    dve.wait_ge(inv_ready, p + 1)
                    nc.vector.tensor_scalar(mixed[:], mix[:, 0:C], inv_sum[:, u:u + 1], None, ALU.mult)\
                        .then_inc(mixed_ready, 1)

                row_max(0, 0)
                pairs(dve, body)
                add_out(PAIRS - 1)


NH, HE = 4, 64
QK = (NH + 1) * HE
QKV = QK + HE
HALF = HE // 2
RMS_EPS = 1e-6


def rotary_qkv(nc, g, a, qkv):
    with ExitStack() as stack:
        m = Memory(nc, stack)
        w = m.sb("self_wqkv", [P, DC, QKV])
        angles = m.sb("self_angles", [P, 2, HALF])
        gain_q, gain_k = m.sb("self_gain_q", [P, HE]), m.sb("self_gain_k", [P, HE])
        table = {n: m.sb(f"self_table_{n}", [P, NH + 1, HALF]) for n in "abcd"}
        square = m.sb("self_square", [P, PAIRS, QK])
        power, root = m.sb("self_power", [P, PAIRS * (NH + 1)]), m.sb("self_root", [P, PAIRS * (NH + 1)])
        part = {n: m.sb(f"self_part_{n}", [P, PAIRS, NH + 1, HALF]) for n in "abcd"}
        loaded, made, taken, power_done, root_done, step = (m.sem(f"self_{n}") for n in
                                                            ("loaded", "made", "taken", "power_done", "root_done", "step"))
        halves = qkv[:, :, 0:QK].rearrange("p t (h j two) -> p t h j two", h=NH + 1, two=2)
        even, odd = halves[:, :, :, :, 0], halves[:, :, :, :, 1]
        heads = qkv[:, :, 0:QK].rearrange("p t (h j) -> p t h j", h=NH + 1)

        def first_loads(sp):
            sp.dma_start(w[:], a["self_wqkv_t"].rearrange("(c p) n -> p c n", p=P)).then_inc(loaded, 16)
            sp.dma_start(angles[:], a["self_angles"]).then_inc(loaded, 16)
            sp.dma_start(gain_q[:], a["self_gain_q"].partition_broadcast(P)).then_inc(loaded, 16)
            sp.dma_start(gain_k[:], a["self_gain_k"].partition_broadcast(P)).then_inc(loaded, 16)

        normalise(nc, g, "ln_e", meanwhile=(first_loads, None))
        ps = m.psum("self_ps_qkv", [P, 4, 512])

        with nc.Block() as block:

            @block.tensor
            def _(pe):
                pe.wait_ge(loaded, 64)
                for t in range(PAIRS):
                    at_least(pe, taken, t - 3)
                    for c in range(DC):
                        mm = nc.tensor.matmul(ps[:, t % 4, 0:QKV], g.YT[:, c, P * t:P * t + P], w[:, c, :],
                                              start=(c == 0), stop=(c == DC - 1))
                    mm.then_inc(made, 1)

            @block.scalar
            def _(act):
                for t in range(PAIRS):
                    act.wait_ge(made, t + 1)
                    nc.scalar.copy(qkv[:, t, :], ps[:, t % 4, 0:QKV]).then_inc(taken, 1)
                act.wait_ge(power_done, 1)
                nc.scalar.activation(root[:], power[:], ACT.Sqrt).then_inc(root_done, 1)

            @block.vector
            def _(dve):
                chain = Chain(dve, step)
                tt, link = nc.vector.tensor_tensor, chain.step
                dve.wait_ge(loaded, 64)
                for name, wave, side in (("a", 0, 0), ("b", 1, 1), ("c", 1, 0), ("d", 0, 1)):
                    for lo, hi, gain in ((0, NH, gain_q), (NH, NH + 1, gain_k)):
                        n = hi - lo
                        link(tt(table[name][:, lo:hi, :], angles[:, wave, :].unsqueeze(1).to_broadcast([P, n, HALF]),
                                gain[:].rearrange("p (j two) -> p two j", two=2)[:, side, :].unsqueeze(1).to_broadcast([P, n, HALF]),
                                ALU.mult))
                    link(nc.vector.tensor_scalar(table[name][:, 0:NH, :], table[name][:, 0:NH, :], HE ** -0.5, None, ALU.mult))
                for n in range(4):
                    dve.wait_ge(taken, 4 * n + 4)
                    t = slice(4 * n, 4 * n + 4)
                    link(tt(square[:, t, :], qkv[:, t, 0:QK], qkv[:, t, 0:QK], ALU.mult))
                    link(nc.vector.tensor_reduce(power[:, 4 * n * (NH + 1):4 * (n + 1) * (NH + 1)],
                                                 square[:, t, :].rearrange("p t (h j) -> p (t h) j", j=HE), AX_X, ALU.add))
                nc.vector.tensor_scalar(power[:], power[:], 1.0 / HE, RMS_EPS, ALU.mult, ALU.add).then_inc(power_done, 1)
                dve.wait_ge(root_done, 1)
                link(nc.vector.reciprocal(power[:], root[:]))
                flat = qkv[:, :, 0:QK].rearrange("p t (h j) -> p t h j", h=NH + 1)
                link(tt(flat, flat, power[:].rearrange("p (t h) -> p t h", t=PAIRS).unsqueeze(3)
                        .to_broadcast([P, PAIRS, NH + 1, HE]), ALU.mult))
                for name, side in (("a", even), ("b", odd), ("c", even), ("d", odd)):
                    link(tt(part[name][:], side, table[name][:].unsqueeze(1).to_broadcast([P, PAIRS, NH + 1, HALF]), ALU.mult))
                link(tt(even, part["a"][:], part["b"][:], ALU.subtract))
                link(tt(odd, part["c"][:], part["d"][:], ALU.add))


def self_attention(nc, g, a):
    with ExitStack() as stack:
        m = Memory(nc, stack)
        qkv = m.sb("self_qkv", [P, PAIRS, QKV])
        rotary_qkv(nc, g, a, qkv)
        wo = m.sb("self_wo", [P, DC, D])
        mask = m.sb("self_mask", [P, P])
        now = m.sb("self_now", [P, QK + HE])
        q_t = m.sb("self_q_t", [P, DC, P])
        k_blocks = m.sb("self_k_blocks", [P, 2, P])
        masked, probs, shares = (m.sb(f"self_{n}", [P, NH, P]) for n in ("masked", "probs", "shares"))
        neg_max, row_sum, inv_sum = (m.sb(f"self_{n}", [P, NH]) for n in ("neg_max", "row_sum", "inv_sum"))
        shares_t = m.sb("self_shares_t", [P, NH, P])
        heads_out, heads_out_t = m.sb("self_heads_out", [P, D]), m.sb("self_heads_out_t", [P, DC, P])
        bank = {n: m.psum(f"self_ps_{n}", [P, 512]) for n in ("turn_qk", "scores", "turn_p", "mix", "turn_o", "out")}
        sem = m.sem
        loaded, zeroed, now_ready = sem("self_att_loaded"), sem("self_zeroed"), sem("self_now_ready")
        qk_turned, qk_taken, scores_ready = sem("self_qk_turned"), sem("self_qk_taken"), sem("self_scores_ready")
        masked_ready, max_ready, probs_ready = sem("self_masked_ready"), sem("self_max_ready"), sem("self_probs_ready")
        inv_ready, shares_ready = sem("self_inv_ready"), sem("self_shares_ready")
        shares_turned, shares_taken = sem("self_shares_turned"), sem("self_shares_taken")
        mix_ready, mix_taken = sem("self_mix_ready"), sem("self_mix_taken")
        out_turned, out_taken, out_ready, out_added = (sem("self_out_turned"), sem("self_out_taken"),
                                                       sem("self_out_ready"), sem("self_out_added"))
        LAST = 5

        def turns(eng, body):
            for i in range(LAST + 1):
                body(i, lambda k: 0 <= i - k)
            with eng.Fori(LAST + 1, PAIRS) as i:
                body(i, lambda k: True)
            for i in range(PAIRS, PAIRS + LAST):
                body(i, lambda k: i - k < PAIRS)

        with nc.Block() as block:

            @block.sync
            def _(sp):
                sp.dma_start(wo[:], a["self_wo_t"].rearrange("(c p) n -> p c n", p=P)).then_inc(loaded, 16)
                sp.dma_start(mask[:], a["self_mask"]).then_inc(loaded, 16)

            @block.gpsimd
            def _(pool):
                nc.gpsimd.memset(k_blocks[:], 0.0).then_inc(zeroed, 1)

                def copy(i):
                    if not isinstance(i, int) or i > 0:
                        pool.wait_ge(qk_turned, i)
                        pool.wait_ge(zeroed, 1)
                    nc.gpsimd.tensor_copy(now[:, 0:QK], qkv[:, i, 0:QK]).then_inc(now_ready, 1)
                    nc.gpsimd.tensor_copy(now[:, QK:QK + HE], qkv[:, i, QK - HE:QK]).then_inc(now_ready, 1)

                copy(0)
                with pool.Fori(1, PAIRS) as i:
                    copy(i)

            @block.tensor
            def _(pe):
                def body(i, stage):
                    if stage(5):
                        pe.wait_ge(out_taken, i - 4)
                        at_least(pe, out_added, i - 5)
                        for c in range(DC):
                            mm = nc.tensor.matmul(bank["out"][:, 0:D], heads_out_t[:, c, :], wo[:, c, :],
                                                  start=(c == 0), stop=(c == DC - 1))
                        mm.then_inc(out_ready, 1)
                    if stage(4):
                        pe.wait_ge(mix_taken, i - 3)
                        for c in range(DC):
                            mm = nc.tensor.transpose(bank["turn_o"][:, P * c:P * c + P], heads_out[:, P * c:P * c + P], g.ident[:])
                        mm.then_inc(out_turned, 1)
                    if stage(3):
                        pe.wait_ge(shares_taken, i - 2)
                        for h in range(NH):
                            mm = nc.tensor.matmul(bank["mix"][:, HE * h:HE * h + HE], shares_t[:, h, :],
                                                  qkv[:, i - 3, QK:QKV], start=True, stop=True)
                        mm.then_inc(mix_ready, 1)
                    if stage(2):
                        pe.wait_ge(shares_ready, i - 1)
                        for h in range(NH):
                            mm = nc.tensor.transpose(bank["turn_p"][:, P * h:P * h + P], shares[:, h, :], g.ident[:])
                        mm.then_inc(shares_turned, 1)
                    if stage(1):
                        pe.wait_ge(qk_taken, 3 * i)
                        for c in range(DC):
                            mm = nc.tensor.matmul(bank["scores"][:, 2 * P * c:2 * P * c + 2 * P], q_t[:, c, :], k_blocks[:],
                                                  start=True, stop=True)
                        mm.then_inc(scores_ready, 1)
                    if stage(0):
                        pe.wait_ge(now_ready, 2 * i + 2)
                        for c in range(3):
                            mm = nc.tensor.transpose(bank["turn_qk"][:, P * c:P * c + P], now[:, P * c:P * c + P], g.ident[:])
                        mm.then_inc(qk_turned, 1)

                pe.wait_ge(loaded, 32)
                turns(pe, body)

            @block.scalar
            def _(act):
                def body(i, stage):
                    if stage(4):
                        act.wait_ge(out_turned, i - 3)
                        nc.scalar.copy(heads_out_t[:].rearrange("p c n -> p (c n)"), bank["turn_o"][:, 0:D]).then_inc(out_taken, 1)
                    if stage(3):
                        act.wait_ge(mix_ready, i - 2)
                        nc.scalar.copy(heads_out[:], bank["mix"][:, 0:D]).then_inc(mix_taken, 1)
                    if stage(1):
                        act.wait_ge(max_ready, i)
                        for h in range(NH):
                            nc.scalar.activation(probs[:, h, :], masked[:, h, :], ACT.Exp, bias=neg_max[:, h:h + 1], scale=1.0,
                                                 accum_out=row_sum[:, h:h + 1]).then_inc(probs_ready, 1)
                    if stage(0):
                        act.wait_ge(qk_turned, i + 1)
                        nc.scalar.copy(q_t[:].rearrange("p c n -> p (c n)"), bank["turn_qk"][:, 0:2 * P]).then_inc(qk_taken, 1)
                        for b in range(2):
                            nc.scalar.copy(k_blocks[HE * b:HE * b + HE, b, :], bank["turn_qk"][HE * b:HE * b + HE, 2 * P:3 * P])\
                                .then_inc(qk_taken, 1)

                act.preload_act_table(ACT.Exp)
                act.wait_ge(zeroed, 1)
                turns(act, body)

            @block.vector
            def _(dve):
                def body(i, stage):
                    if stage(5):
                        dve.wait_ge(out_ready, i - 4)
                        nc.vector.tensor_tensor(g.X[:, i - 5, :], g.X[:, i - 5, :], bank["out"][:, 0:D], ALU.add)\
                            .then_inc(out_added, 1)
                    if stage(2):
                        dve.wait_ge(shares_turned, i - 1)
                        nc.vector.tensor_copy(shares_t[:].rearrange("p h n -> p (h n)"), bank["turn_p"][:]).then_inc(shares_taken, 1)
                    if stage(1):
                        dve.wait_ge(scores_ready, i)
                        nc.vector.tensor_tensor(masked[:], bank["scores"][:].rearrange("p (h n) -> p h n", h=NH),
                                                mask[:].unsqueeze(1).to_broadcast([P, NH, P]), ALU.add).then_inc(masked_ready, 1)
                        dve.wait_ge(masked_ready, i)
                        nc.vector.tensor_reduce(neg_max[:], masked[:], AX_X, ALU.max, negate=True).then_inc(max_ready, 1)
                        dve.wait_ge(probs_ready, NH * i)
                        nc.vector.reciprocal(inv_sum[:], row_sum[:]).then_inc(inv_ready, 1)
                        dve.wait_ge(inv_ready, i)
                        nc.vector.tensor_tensor(shares[:], probs[:], inv_sum[:].unsqueeze(2).to_broadcast([P, NH, P]),
                                                ALU.mult).then_inc(shares_ready, 1)

                dve.wait_ge(loaded, 32)
                turns(dve, body)


I = 704
IT = [(i, min(P, I - i)) for i in range(0, I, P)]
IREST = I - P * (I // P)
QMAX = 127.0


class Quantised:

    def __init__(self, m):
        self.gate_t = m.sb("ffn_gate_t", [P, DC, I], BF16)
        self.up_t = m.sb("ffn_up_t", [P, DC, I], BF16)
        self.down_t = m.sb("ffn_down_t", [P, len(IT), D], BF16)
        self.down_scale = m.sb("ffn_down_scale", [P, D])
        self.scale = {n: m.sb(f"ffn_scale_{n}", [P, t]) for n, t in (("gate", len(IT)), ("up", len(IT)), ("down", DC))}


def quantise_weights(nc, g, a, q):
    with ExitStack() as stack:
        m = Memory(nc, stack)
        shapes = {"gate": (len(IT), D), "up": (len(IT), D), "down": (DC, I)}
        w = {n: m.sb(f"quant_{n}", [P, *s]) for n, s in shapes.items()}
        low = {n: m.sb(f"quant_{n}_int", [P, *s], BF16) for n, s in shapes.items()}
        inverse = {n: m.sb(f"quant_{n}_inverse", [P, s[0]]) for n, s in shapes.items()}
        small_ident, ones, diagonal = m.sb("quant_ident", [P, P], BF16), m.sb("quant_ones", [P, P]), m.sb("quant_diagonal", [P, DC, P])
        loaded, filled, step, low_ready, turned_ready, stored, spread_ready, diagonal_ready = (
            m.sem(f"quant_{n}") for n in ("loaded", "filled", "step", "low_ready", "turned_ready", "stored",
                                          "spread_ready", "diagonal_ready"))
        def first_loads(sp):
            whole = P * (I // P)
            sp.wait_ge(filled, 2)
            for n, src in (("gate", a["quant_gate"]), ("up", a["quant_up"])):
                sp.dma_start(w[n][:, 0:I // P, :], src[0:whole].rearrange("(t p) h -> p t h", p=P)).then_inc(loaded, 16)
                sp.dma_start(w[n][0:IREST, I // P, :], src[whole:I]).then_inc(loaded, 16)
            sp.dma_start(w["down"][:], a["quant_down"].rearrange("(t p) i -> p t i", p=P)).then_inc(loaded, 16)

        def first_fills(pool):
            nc.gpsimd.memset(w["gate"][:, I // P, :], 1.0).then_inc(filled, 1)
            nc.gpsimd.memset(w["up"][:, I // P, :], 1.0).then_inc(filled, 1)
            nc.gpsimd.memset(ones[:], 1.0).then_inc(filled, 1)
            nc.gpsimd.tensor_copy(small_ident[:], g.ident[:]).then_inc(filled, 1)

        normalise(nc, g, "ln_f", meanwhile=(first_loads, first_fills))
        turned = m.psum("quant_turned", [P, 6, 1024], BF16)
        spread = m.psum("quant_spread", [P, DC, P])
        with nc.Block() as block:

            @block.vector
            def _(dve):
                chain = Chain(dve, step)
                link = chain.step
                dve.wait_ge(loaded, 80)
                for n, (tiles, width) in shapes.items():
                    link(nc.vector.tensor_reduce(q.scale[n][:], w[n][:], AX_X, ALU.max, apply_absolute_value=True))
                    link(nc.vector.tensor_scalar(q.scale[n][:], q.scale[n][:], 1.0 / QMAX, None, ALU.mult))
                    link(nc.vector.reciprocal(inverse[n][:], q.scale[n][:]))
                    link(nc.vector.tensor_tensor(w[n][:], w[n][:], inverse[n][:].unsqueeze(2).to_broadcast([P, tiles, width]), ALU.mult))
                    link(nc.vector.tensor_scalar(w[n][:], w[n][:], ROUND, ROUND, ALU.add, ALU.subtract))
                    nc.vector.tensor_scalar(low[n][:], w[n][:], QMAX, -QMAX - 1.0, ALU.min, ALU.max).then_inc(low_ready, 1)
                for c in range(DC):
                    nc.vector.tensor_scalar(diagonal[:, c, :], g.ident[:], q.scale["down"][:, c:c + 1], None, ALU.mult)\
                        .then_inc(diagonal_ready, 1)
                dve.wait_ge(spread_ready, 1)
                nc.vector.tensor_copy(q.down_scale[:], spread[:].rearrange("p c n -> p (c n)")).then_inc(stored, 1)

            @block.tensor
            def _(pe):
                pe.wait_ge(filled, 4)
                for k, n in enumerate(("gate", "up")):
                    pe.wait_ge(low_ready, k + 1)
                    for c in range(DC):
                        for t, (lo, size) in enumerate(IT):
                            mm = nc.tensor.transpose(turned[:, 2 * k + c, lo:lo + size], low[n][0:size, t, P * c:P * c + P],
                                                     small_ident[0:size, 0:size])
                        mm.then_inc(turned_ready, 1)
                pe.wait_ge(low_ready, 3)
                for t, (lo, size) in enumerate(IT):
                    for c in range(DC):
                        mm = nc.tensor.transpose(turned[0:size, 4 + t // 4, 256 * (t % 4) + P * c:256 * (t % 4) + P * c + P],
                                                 low["down"][:, c, lo:lo + size], small_ident[:])
                    if t in (3, 5):
                        mm.then_inc(turned_ready, 1)
                pe.wait_ge(diagonal_ready, DC)
                for c in range(DC):
                    mm = nc.tensor.matmul(spread[:, c, :], ones[:], diagonal[:, c, :], start=True, stop=True)
                mm.then_inc(spread_ready, 1)

            @block.scalar
            def _(act):
                for k, out in enumerate((q.gate_t, q.up_t)):
                    for c in range(DC):
                        act.wait_ge(turned_ready, 2 * k + c + 1)
                        nc.scalar.copy(out[:, c, :], turned[:, 2 * k + c, 0:I]).then_inc(stored, 1)
                act.wait_ge(turned_ready, 5)
                nc.scalar.copy(q.down_t[:, 0:4, :].rearrange("p t n -> p (t n)"), turned[:, 4, :]).then_inc(stored, 1)
                act.wait_ge(turned_ready, 6)
                nc.scalar.copy(q.down_t[:, 4, :], turned[:, 5, 0:D]).then_inc(stored, 1)
                nc.scalar.copy(q.down_t[0:IREST, 5, :], turned[0:IREST, 5, D:2 * D]).then_inc(stored, 1)


def largest(nc, m, name, clip, rows_of, scale, inverse):
    top, top_all = m.sb(f"{name}_top", [P, len(rows_of)]), m.sb(f"{name}_top_all", [P, 1])
    best, clip_col, decay = m.sb(f"{name}_best", [P, 1]), m.sb(f"{name}_clip", [P, 1]), m.sb(f"{name}_decay", [P, 1])
    loaded, zeroed, step, best_ready, all_ready, decay_ready = (m.sem(f"{name}_{n}") for n in
                                                        ("loaded", "zeroed", "step", "best_ready", "all_ready", "decay_ready"))
    with nc.Block() as block:

        @block.sync
        def _(sp):
            sp.dma_start(clip_col[:], clip.partition_broadcast(P)).then_inc(loaded, 16)

        @block.gpsimd
        def _(pool):
            pool.wait_ge(best_ready, 1)
            nc.gpsimd.partition_all_reduce(top_all[:], best[:], P, bass.bass_isa.ReduceOp.max).then_inc(all_ready, 1)

        @block.scalar
        def _(act):
            act.wait_ge(loaded, 16)
            nc.scalar.activation(decay[:], clip_col[:], ACT.Exp, scale=-1.0).then_inc(decay_ready, 1)

        @block.vector
        def _(dve):
            chain = Chain(dve, step)
            link = chain.step
            link(nc.vector.memset(top[:], 0.0))
            for k, (rows, part) in enumerate(rows_of):
                link(nc.vector.tensor_reduce(top[0:rows, k:k + 1], part, AX_X, ALU.max, apply_absolute_value=True))
            nc.vector.tensor_reduce(best[:], top[:], AX_X, ALU.max).then_inc(best_ready, 1)
            dve.wait_ge(decay_ready, 1)
            link(nc.vector.tensor_scalar(decay[:], decay[:], 1.0, None, ALU.add))
            link(nc.vector.reciprocal(decay[:], decay[:]))
            dve.wait_ge(all_ready, 1)
            link(nc.vector.tensor_scalar(scale[:], top_all[:], decay[:], 1.0 / QMAX, ALU.mult, ALU.mult))
            link(nc.vector.reciprocal(inverse[:], scale[:]))


def quantised_ffn(nc, g, a):
    with ExitStack() as stack:
        m = Memory(nc, stack)
        q = Quantised(m)
        quantise_weights(nc, g, a, q)
        x_scale, x_inverse, h_scale, h_inverse = (m.sb(f"ffn_{n}", [P, 1]) for n in
                                                  ("x_scale", "x_inverse", "h_scale", "h_inverse"))
        hidden = m.sb("ffn_hidden", [P, len(IT), ROWS])
        largest(nc, m, "ffn_x", a["quant_clip_x"], [(P, g.YT[:, c, :]) for c in range(DC)], x_scale, x_inverse)
        gate_and_up(nc, g, q, x_scale, x_inverse, hidden)
        parts = [(size, hidden[0:size, t, :]) for t, (lo, size) in enumerate(IT)]
        largest(nc, m, "ffn_h", a["quant_clip_down"], parts, h_scale, h_inverse)
        down(nc, g, q, h_scale, h_inverse, hidden)


def gate_and_up(nc, g, q, x_scale, x_inverse, hidden):
    with ExitStack() as stack:
        m = Memory(nc, stack)
        low = m.sb("gate_low", [P, DC, ROWS], BF16)
        gate_scale, up_scale = m.sb("gate_scale", [P, len(IT)]), m.sb("up_scale", [P, len(IT)])
        active = m.sb("gate_active", [P, 2, 512])
        round_col = m.sb("gate_round", [P, 1])
        ps_gate, ps_up = m.psum("gate_ps_gate", [P, 2, 512]), m.psum("gate_ps_up", [P, 2, 512])
        filled, scales_ready, rounded, clipped, low_ready = (m.sem(f"gate_{n}") for n in
                                                             ("filled", "scales_ready", "rounded", "clipped", "low_ready"))
        made, active_ready, hidden_ready = m.sem("gate_made"), m.sem("gate_active_ready"), m.sem("gate_hidden_ready")
        tiles = [(n, t, lo, size) for n in range(GROUPS) for t, (lo, size) in enumerate(IT)]
        with nc.Block() as block:

            @block.vector
            def _(dve):
                nc.vector.memset(round_col[:], ROUND).then_inc(filled, 1)
                nc.vector.tensor_scalar(gate_scale[:], q.scale["gate"][:], x_scale[:], None, ALU.mult).then_inc(scales_ready, 1)
                nc.vector.tensor_scalar(up_scale[:], q.scale["up"][:], x_scale[:], None, ALU.mult).then_inc(scales_ready, 1)
                for n in range(GROUPS):
                    r = slice(GROUP * n, GROUP * n + GROUP)
                    dve.wait_ge(rounded, n + 1)
                    nc.vector.tensor_scalar(g.YT[:, :, r], g.YT[:, :, r], ROUND + QMAX, ROUND - QMAX - 1.0, ALU.min,
                                            ALU.max).then_inc(clipped, 1)
                    dve.wait_ge(clipped, n + 1)
                    nc.vector.tensor_scalar(low[:, :, r], g.YT[:, :, r], ROUND, None, ALU.subtract).then_inc(low_ready, 1)
                dve.wait_ge(scales_ready, 2)
                for k, (n, t, lo, size) in enumerate(tiles):
                    dve.wait_ge(active_ready, k + 1)
                    nc.vector.scalar_tensor_tensor(hidden[0:size, t, GROUP * n:GROUP * n + GROUP], ps_up[0:size, k % 2, :],
                                                   up_scale[0:size, t:t + 1], active[0:size, k % 2, :], ALU.mult, ALU.mult)\
                        .then_inc(hidden_ready, 1)

            @block.scalar
            def _(act):
                act.wait_ge(filled, 1)
                for n in range(GROUPS):
                    r = slice(GROUP * n, GROUP * n + GROUP)
                    nc.scalar.activation(g.YT[:, :, r], g.YT[:, :, r], ACT.Identity, bias=round_col[:],
                                         scale=x_inverse[:]).then_inc(rounded, 1)
                act.wait_ge(scales_ready, 2)
                for k, (n, t, lo, size) in enumerate(tiles):
                    act.wait_ge(made, k + 1)
                    at_least(act, hidden_ready, k - 1)
                    nc.scalar.activation(active[0:size, k % 2, :], ps_gate[0:size, k % 2, :], ACT.Silu,
                                         scale=gate_scale[0:size, t:t + 1]).then_inc(active_ready, 1)

            @block.tensor
            def _(pe):
                for k, (n, t, lo, size) in enumerate(tiles):
                    pe.wait_ge(low_ready, n + 1)
                    at_least(pe, hidden_ready, k - 1)
                    for ps, w in ((ps_gate, q.gate_t), (ps_up, q.up_t)):
                        for c in range(DC):
                            mm = nc.tensor.matmul(ps[0:size, k % 2, :], w[:, c, lo:lo + size], low[:, c, GROUP * n:GROUP * n + GROUP],
                                                  start=(c == 0), stop=(c == DC - 1))
                    mm.then_inc(made, 1)


def down(nc, g, q, h_scale, h_inverse, hidden):
    with ExitStack() as stack:
        m = Memory(nc, stack)
        low = m.sb("down_low", [P, len(IT), ROWS], BF16)
        round_col, scale = m.sb("down_round", [P, 1]), m.sb("down_scale", [P, D])
        scaled = m.sb("down_scaled", [P, 2, D])
        ps = m.psum("down_ps", [P, 4, 512])
        filled, rounded, clipped, low_ready, scale_ready, made, scaled_ready, added = (
            m.sem(f"down_{n}") for n in ("filled", "rounded", "clipped", "low_ready", "scale_ready", "made",
                                         "scaled_ready", "added"))
        parts = [(n, t, size) for n in range(GROUPS) for t, (lo, size) in ((slice(0, 5), (0, P)), (slice(5, 6), (0, IREST)))]
        with nc.Block() as block:

            @block.scalar
            def _(act):
                act.wait_ge(filled, 1)
                for n, t, size in parts:
                    v = hidden[0:size, t, GROUP * n:GROUP * n + GROUP]
                    nc.scalar.activation(v, v, ACT.Identity, bias=round_col[0:size], scale=h_inverse[0:size]).then_inc(rounded, 1)

            @block.vector
            def _(dve):
                nc.vector.memset(round_col[:], ROUND).then_inc(filled, 1)
                nc.vector.tensor_scalar(scale[:], q.down_scale[:], h_scale[:], None, ALU.mult).then_inc(scale_ready, 1)
                dve.wait_ge(scale_ready, 1)

                def quantise(k):
                    n, t, size = parts[k]
                    v = hidden[0:size, t, GROUP * n:GROUP * n + GROUP]
                    dve.wait_ge(rounded, k + 1)
                    nc.vector.tensor_scalar(v, v, ROUND + QMAX, ROUND - QMAX - 1.0, ALU.min, ALU.max).then_inc(clipped, 1)
                    dve.wait_ge(clipped, k + 1)
                    nc.vector.tensor_scalar(low[0:size, t, GROUP * n:GROUP * n + GROUP], v, ROUND, None, ALU.subtract)\
                        .then_inc(low_ready, 1)

                for n in range(GROUPS + 1):
                    if n < GROUPS:
                        quantise(2 * n)
                        quantise(2 * n + 1)
                    if n == 0:
                        continue
                    for r in range(4 * (n - 1), 4 * n):
                        dve.wait_ge(made, r + 1)
                        at_least(dve, added, r - 1)
                        nc.vector.tensor_tensor(scaled[:, r % 2, :], ps[:, r % 4, 0:D], scale[:], ALU.mult).then_inc(scaled_ready, 1)
                        dve.wait_ge(scaled_ready, r + 1)
                        nc.vector.tensor_tensor(g.X[:, r, :], g.X[:, r, :], scaled[:, r % 2, :], ALU.add).then_inc(added, 1)

            @block.tensor
            def _(pe):
                for r in range(PAIRS):
                    pe.wait_ge(low_ready, 2 * (r // 4) + 2)
                    at_least(pe, scaled_ready, r - 3)
                    for t, (lo, size) in enumerate(IT):
                        mm = nc.tensor.matmul(ps[:, r % 4, 0:D], low[0:size, t, P * r:P * r + P], q.down_t[0:size, t, :],
                                              start=(t == 0), stop=(t == len(IT) - 1))
                    mm.then_inc(made, 1)


def store(nc, g, out):
    with ExitStack() as stack:
        out_stored = Memory(nc, stack).sem("out_stored")
        with nc.Block() as block:

            @block.sync
            def _(sp):
                sp.dma_start(out.rearrange("(p b) q d -> (b q) p d", b=2), g.X[:]).then_inc(out_stored, 16)
                sp.wait_ge(out_stored, 16)


def lay_out(inputs):
    import numpy as np
    f = {k: np.asarray(v) for k, v in inputs.items()}
    ctx = f["ctx_512"]
    wkv = f["L0_xattn_Wkv"]
    main = ctx[:, :KFULL * P].reshape(B, KFULL, P, C).transpose(0, 2, 1, 3)
    arrays = dict(
        x=f["x"], ctx_main=main, ctx_rest=ctx[:, KFULL * P:], ctx_t=ctx.transpose(0, 2, 1),
        wq_t=f["L0_xattn_Wq"].T, wkv=wkv, wv_t=wkv[D:].T, wo_t=f["L0_xattn_Wo"].T,
    )
    part, column = np.arange(P)[:, None], np.arange(P)[None, :]
    arrays["own_head"] = ((part // HD) % 2 == column // T).astype(np.float32)
    columns = [f[f"L0_attn_{n}"] for n in ("bk", "bv", "bq", "bkp", "bqp", "phase_scale", "ln_g", "ln_b")]
    arrays.update(
        mix_columns=np.stack(columns).reshape(8, DC, P).transpose(2, 0, 1),
        mix_wk=f["L0_attn_Wk"], mix_wv=f["L0_attn_Wv"], mix_wq=f["L0_attn_Wq"], mix_wkp=f["L0_attn_Wkp"],
        mix_wqp=f["L0_attn_Wqp"], mix_wo=f["L0_attn_Wo"], mix_bo=f["L0_attn_bo"],
        router_w=f["L0_ffn_Wr"], router_b=f["L0_ffn_br"], expert_w1=f["L0_ffn_W1"], expert_w2=f["L0_ffn_W2"],
        expert_b1=f["L0_ffn_b1"].reshape(E, HC, P).transpose(2, 0, 1), expert_b2=f["L0_ffn_b2"],
    )
    arrays.update(
        wide_wq=f["L1_xattn_Wq"], wide_wk_t=f["L1_xattn_Wk"].T, wide_wv=f["L1_xattn_Wv"],
        wide_bq=f["L1_xattn_bq"].reshape(DC, P).T, wide_bk=f["L1_xattn_bk"].reshape(DC, P).T, wide_bv=f["L1_xattn_bv"],
    )
    inverse = (1.0 / np.float32(1000000.0) ** (np.arange(0, HE, 2, dtype=np.float32) / np.float32(HE))).astype(np.float32)
    turns = np.outer(np.arange(T, dtype=np.float32), inverse)
    angles = np.tile(np.stack([np.cos(turns), np.sin(turns)], axis=1), (2, 1, 1)).astype(np.float32)
    row, key = np.arange(P)[:, None], np.arange(P)[None, :]
    allowed = (row // T == key // T) & (key <= row) & (key >= row - 128)
    arrays.update(
        self_wqkv_t=np.concatenate([f["L1_attn_Wq"], f["L1_attn_Wk"], f["L1_attn_Wv"]]).T, self_wo_t=f["L1_attn_Wo"].T,
        self_gain_q=f["L1_attn_q_gamma"], self_gain_k=f["L1_attn_k_gamma"], self_angles=angles,
        self_mask=np.where(allowed, 0.0, -1e30).astype(np.float32),
    )
    arrays.update(
        quant_gate=f["L1_ffn_w_gate"], quant_up=f["L1_ffn_w_up"], quant_down=f["L1_ffn_w_down"],
        quant_clip_x=f["L1_ffn_clip_x"], quant_clip_down=f["L1_ffn_clip_down"],
    )
    return {k: np.ascontiguousarray(v) for k, v in arrays.items()}


def program(nc, a, out):
    Memory.semaphores.clear()
    with ExitStack() as stack:
        m = Memory(nc, stack)
        g = Kept(m)
        setup(nc, g, a["x"])
        heads_cross_attention(nc, g, a)
        with ExitStack() as held:
            reserve_experts(g, Memory(nc, held))
            token_mixer(nc, g, a)
            normalise(nc, g, "ln_c")
            experts(nc, g, a)
        recycle(nc)
        wide_cross_attention(nc, g, a)
        self_attention(nc, g, a)
        quantised_ffn(nc, g, a)
        store(nc, g, out)


def kernel(**inputs):
    import numpy as np
    import concourse.bacc as bacc
    from concourse import mybir as m
    from concourse.bass_utils import run_bass_kernel_spmd

    nc = bacc.Bacc("TRN2", target_bir_lowering=False, num_devices=1)
    arrays = lay_out(inputs)
    a = {n: nc.dram_tensor(f"in_{n}", v.shape, m.dt.from_np(v.dtype), kind="ExternalInput").ap()
                 for n, v in arrays.items()}
    out = nc.dram_tensor("out_x", (B, T, D), m.dt.float32, kind="ExternalOutput").ap()
    program(nc, a, out)
    r = run_bass_kernel_spmd(nc, [{f"in_{n}": v for n, v in arrays.items()}], core_ids=[0])
    return np.asarray(r.results[0]["out_x"])
```
